# Optimizing a Trainium2 kernel written in Bass

```python
import numpy as np
import jax
import jax.numpy as jnp

def _softmax(x, axis=-1):
    return jax.nn.softmax(x, axis=axis)

def _gelu(x):
    return jax.nn.gelu(x, approximate=True)

def _silu(x):
    return jax.nn.silu(x)

def _sigmoid(x):
    return jax.nn.sigmoid(x)

def _layernorm(x, axis=-1, eps=1e-05):
    m = jnp.mean(x, axis=axis, keepdims=True)
    v = jnp.var(x, axis=axis, keepdims=True)
    return (x - m) / jnp.sqrt(v + eps)

def _scatter_add(tgt, idx, src, axis=0):
    return tgt.at[idx].add(src)

def _segment_sum(src, seg, n):
    return jax.ops.segment_sum(src, seg, n)
kernel_name = 'mk_hybrid_d1_jaxref_r4_0b1111'

def setup_inputs(seed: int=0):
    np.random.seed(seed)
    _w = jnp.asarray

    def _L0_attn_a_setup():
        import jax, jax.numpy as jnp
        import numpy as np
        DECAY = 0.9
        key = jax.random.key(seed)
        ks = jax.random.split(key, 8)
        B, L, d_model = (4, 512, 256)
        d_state = 16
        d_inner = 2 * d_model
        x = jax.random.normal(ks[0], (B, L, d_model), dtype=jnp.float32)
        Win = jax.random.normal(ks[1], (d_model, d_inner), dtype=jnp.float32) / np.sqrt(d_model)
        bin_ = jnp.zeros((d_inner,), dtype=jnp.float32)
        Bp = jax.random.normal(ks[2], (d_inner, d_state), dtype=jnp.float32) * 0.01
        Cp = jax.random.normal(ks[3], (d_state, d_inner), dtype=jnp.float32) * 0.01
        Dp = jnp.ones((d_inner,), dtype=jnp.float32)
        Wout = jax.random.normal(ks[4], (d_inner, d_model), dtype=jnp.float32) / np.sqrt(d_inner)
        bout = jnp.zeros((d_model,), dtype=jnp.float32)
        return {'x': x, 'Win': Win, 'bin_': bin_, 'Bp': Bp, 'Cp': Cp, 'Dp': Dp, 'Wout': Wout, 'bout': bout}
    _L0_attn_a_in = _L0_attn_a_setup()

    def _L0_attn_b_setup():
        import jax, jax.numpy as jnp
        import numpy as np
        B, N, D, H = (2, 512, 256, 16)
        DH = D // H
        EPS = 1e-05

        def _lrpe(t, theta, n):
            idx = jnp.arange(n, dtype=t.dtype).reshape(1, n, 1)
            th = theta * idx
            return jnp.concatenate([t * jnp.cos(th), t * jnp.sin(th)], axis=-1)
        key = jax.random.key(seed)
        ks = jax.random.split(key, 8)
        x = jax.random.normal(ks[0], (B, N, D), dtype=jnp.float32)
        context = jax.random.normal(ks[1], (B, N, D), dtype=jnp.float32)
        Wqkvu = jax.random.normal(ks[2], (4 * D, D), dtype=jnp.float32) * 0.02
        bqkvu = jax.random.normal(ks[3], (4 * D,), dtype=jnp.float32) * 0.02
        Wout = jax.random.normal(ks[4], (D, D), dtype=jnp.float32) * 0.02
        bout = jax.random.normal(ks[5], (D,), dtype=jnp.float32) * 0.02
        theta = (10000.0 ** (-2.0 / D * jnp.arange(D, dtype=jnp.float32))).reshape(H, 1, DH)
        ln_w = jnp.ones((D,), dtype=jnp.float32)
        ln_b = jnp.zeros((D,), dtype=jnp.float32)
        return {'x': x, 'context': context, 'Wqkvu': Wqkvu, 'bqkvu': bqkvu, 'Wout': Wout, 'bout': bout, 'theta': theta, 'ln_w': ln_w, 'ln_b': ln_b}
    _L0_attn_b_in = _L0_attn_b_setup()

    def _L0_ffn_setup():
        import jax, jax.numpy as jnp
        import numpy as np
        IN_DIM = 256
        OUT_DIM = 256
        NUM_EXPERTS = 8
        TOP_K = 2
        key = jax.random.key(seed)
        ks = jax.random.split(key, 5)
        s = 1.0 / np.sqrt(IN_DIM)
        x = jax.random.normal(ks[0], (4, 512, IN_DIM), dtype=jnp.float32)
        Wg = jax.random.uniform(ks[1], (IN_DIM, NUM_EXPERTS), jnp.float32, -s, s)
        bg = jnp.zeros((NUM_EXPERTS,), jnp.float32)
        We = jax.random.uniform(ks[2], (NUM_EXPERTS, OUT_DIM, IN_DIM), jnp.float32, -s, s)
        be = jax.random.uniform(ks[3], (NUM_EXPERTS, OUT_DIM), jnp.float32, -s, s)
        return {'x': x, 'Wg': Wg, 'bg': bg, 'We': We, 'be': be}
    _L0_ffn_in = _L0_ffn_setup()
    _d = {'L0_attn_a_x': _L0_attn_a_in['x'], 'L0_attn_a_Win': _L0_attn_a_in['Win'], 'L0_attn_a_bin_': _L0_attn_a_in['bin_'], 'L0_attn_a_Bp': _L0_attn_a_in['Bp'], 'L0_attn_a_Cp': _L0_attn_a_in['Cp'], 'L0_attn_a_Dp': _L0_attn_a_in['Dp'], 'L0_attn_a_Wout': _L0_attn_a_in['Wout'], 'L0_attn_a_bout': _L0_attn_a_in['bout'], 'L0_attn_b_context': _L0_attn_b_in['context'], 'L0_attn_b_Wqkvu': _L0_attn_b_in['Wqkvu'], 'L0_attn_b_bqkvu': _L0_attn_b_in['bqkvu'], 'L0_attn_b_Wout': _L0_attn_b_in['Wout'], 'L0_attn_b_bout': _L0_attn_b_in['bout'], 'L0_attn_b_theta': _L0_attn_b_in['theta'], 'L0_attn_b_ln_w': _L0_attn_b_in['ln_w'], 'L0_attn_b_ln_b': _L0_attn_b_in['ln_b'], 'L0_ffn_Wg': _L0_ffn_in['Wg'], 'L0_ffn_bg': _L0_ffn_in['bg'], 'L0_ffn_We': _L0_ffn_in['We'], 'L0_ffn_be': _L0_ffn_in['be']}
    _x0 = _d['L0_attn_a_x']
    _d['L0_attn_a_x'] = jax.random.normal(jax.random.fold_in(jax.random.key(seed), 1), (8, 512, 256), dtype=_x0.dtype)
    del _x0
    return _d

def reference(L0_attn_a_x, L0_attn_a_Win, L0_attn_a_bin_, L0_attn_a_Bp, L0_attn_a_Cp, L0_attn_a_Dp, L0_attn_a_Wout, L0_attn_a_bout, L0_attn_b_context, L0_attn_b_Wqkvu, L0_attn_b_bqkvu, L0_attn_b_Wout, L0_attn_b_bout, L0_attn_b_theta, L0_attn_b_ln_w, L0_attn_b_ln_b, L0_ffn_Wg, L0_ffn_bg, L0_ffn_We, L0_ffn_be):

    def _L0_attn_a_ref(x, Win, bin_, Bp, Cp, Dp, Wout, bout):
        import jax, jax.numpy as jnp
        import numpy as np
        DECAY = 0.9
        B, L, _ = x.shape
        d_inner, d_state = Bp.shape
        xi = jax.nn.silu(x @ Win + bin_)
        xt_seq = jnp.swapaxes(xi, 0, 1)

        def step(h, xt):
            h = h * DECAY + xt[:, :, None] * Bp[None, :, :]
            y = jnp.einsum('bij,ji->bi', h, Cp) + Dp * xt
            return (h, y)
        h0 = jnp.zeros((B, d_inner, d_state), dtype=x.dtype)
        _, ys = jax.lax.scan(step, h0, xt_seq)
        y = jnp.swapaxes(ys, 0, 1)
        return y @ Wout + bout

    def _L0_attn_b_ref(x, context, Wqkvu, bqkvu, Wout, bout, theta, ln_w, ln_b):
        import jax, jax.numpy as jnp
        import numpy as np
        B, N, D, H = (2, 512, 256, 16)
        DH = D // H
        EPS = 1e-05

        def _lrpe(t, theta, n):
            idx = jnp.arange(n, dtype=t.dtype).reshape(1, n, 1)
            th = theta * idx
            return jnp.concatenate([t * jnp.cos(th), t * jnp.sin(th)], axis=-1)
        b, n, d = x.shape
        qkvu = x @ Wqkvu.T + bqkvu
        q, k, v, u = jnp.split(qkvu, 4, axis=-1)
        tohead = lambda t: t.reshape(b, n, H, DH).transpose(0, 2, 1, 3)
        q, k, v = (tohead(q), tohead(k), tohead(v))
        q = jax.nn.silu(q)
        k = jax.nn.silu(k)
        q = _lrpe(q, theta, n)
        k = _lrpe(k, theta, n)
        qk = jnp.einsum('bhmd,bhnd->bhmn', q, k)
        out = jnp.einsum('bhmn,bhne->bhme', qk, v)
        out = out.transpose(0, 2, 1, 3).reshape(b, n, d)
        mu = jnp.mean(out, axis=-1, keepdims=True)
        var = jnp.var(out, axis=-1, keepdims=True)
        out = (out - mu) * jax.lax.rsqrt(var + EPS) * ln_w + ln_b
        out = u * out
        return out @ Wout.T + bout

    def _L0_ffn_ref(x, Wg, bg, We, be):
        import jax, jax.numpy as jnp
        import numpy as np
        IN_DIM = 256
        OUT_DIM = 256
        NUM_EXPERTS = 8
        TOP_K = 2
        gate = jax.nn.softmax(x @ Wg + bg, axis=-1)
        topk_vals, topk_idx = jax.lax.top_k(gate, TOP_K)
        onehot = jax.nn.one_hot(topk_idx, NUM_EXPERTS, dtype=gate.dtype)
        gate_sparse = jnp.einsum('bsk,bske->bse', topk_vals, onehot)
        gate_sparse = gate_sparse / jnp.sum(gate_sparse, axis=-1, keepdims=True)
        y = jnp.einsum('bsi,eoi->bseo', x, We) + be[None, None, :, :].transpose(0, 1, 2, 3)
        out = jnp.einsum('bseo,bse->bso', y, gate_sparse)
        return out
    x = L0_attn_a_x
    x = x + _L0_attn_a_ref(_layernorm(x, axis=-1), L0_attn_a_Win, L0_attn_a_bin_, L0_attn_a_Bp, L0_attn_a_Cp, L0_attn_a_Dp, L0_attn_a_Wout, L0_attn_a_bout)
    x = x + _L0_ffn_ref(_layernorm(x, axis=-1), L0_ffn_Wg, L0_ffn_bg, L0_ffn_We, L0_ffn_be)
    x = x + _L0_attn_b_ref(_layernorm(x, axis=-1), L0_attn_b_context, L0_attn_b_Wqkvu, L0_attn_b_bqkvu, L0_attn_b_Wout, L0_attn_b_bout, L0_attn_b_theta, L0_attn_b_ln_w, L0_attn_b_ln_b)
    x = x + _L0_ffn_ref(_layernorm(x, axis=-1), L0_ffn_Wg, L0_ffn_bg, L0_ffn_We, L0_ffn_be)
    return x

_drawn_inputs = setup_inputs


def setup_inputs(seed=0):
    import zlib

    import numpy as np

    out = dict(_drawn_inputs(seed))
    spreads = {'L0_attn_a_bin_': (0.0, 0.1),
     'L0_attn_a_Dp': (1.0, 0.2),
     'L0_attn_a_bout': (0.0, 0.1),
     'L0_attn_b_ln_w': (1.0, 0.2),
     'L0_attn_b_ln_b': (0.0, 0.327),
     'L0_ffn_bg': (0.0, 0.1)}
    factors = {'L0_attn_a_Bp': 4.255, 'L0_attn_a_Cp': 6.606}
    for name, (base, spread) in spreads.items():
        noise = np.random.default_rng([zlib.crc32(name.encode()), seed]).standard_normal(out[name].shape)
        drawn = base * np.exp(spread * noise) if base else spread * noise
        out[name] = jnp.asarray(drawn.astype(out[name].dtype))
    for name, factor in factors.items():
        out[name] = (out[name] * factor).astype(out[name].dtype)
    return out
```

```python
from contextlib import ExitStack

import numpy as np

import concourse.bass as bass
from concourse import mybir

ALU = mybir.AluOpType
ACT = mybir.ActivationFunctionType
AX = mybir.AxisListType
F32 = mybir.dt.float32
F32R = mybir.dt.float32r

P = 128
B, L, D = 8, 512, 256
T = L // P
KD = D // P
DI = 512
MI = DI // P
DS = 16
DH = 16
NE = 8
NP = NE // 2
LPAD = 16
TS = L // B
DECAY = 0.9
EPS = 1e-5
SENTINEL = -3.0e38

TWO_PI_1, TWO_PI_2 = 6.28125, 0.0019350051879882812
TWO_PI_3 = float(2 * np.pi - TWO_PI_1 - TWO_PI_2)
INV_TWO_PI = float(1 / (2 * np.pi))
ROUND = 12582912.0
PI_BELOW = 3.1415925


def columns(*widths):
    at, out = 0, {}
    for name, w in widths:
        out[name] = (at, at + w)
        at += w
    return out, at


CON, CON_W = columns(("ident", P), ("mask", P), ("pos", L), ("sel2", 2), ("sel24", 2))
PAR, PAR_W = columns(("bin", MI), ("dp", MI), ("bp", MI * DS), ("cp", MI * DS), ("bq", KD), ("bu", KD), ("theta", KD),
                     ("lnw", KD), ("lnb", KD), ("bg", NE), ("wg", KD * NE), ("bout", D), ("bo", D))


def shape_constants():
    c = np.zeros((P, CON_W), np.float32)
    c[:, slice(*CON["ident"])] = np.eye(P)
    c[:, slice(*CON["mask"])] = np.kron(np.eye(P // DH), np.ones((DH, DH)))
    c[:, slice(*CON["pos"])] = np.arange(L)[None, :]
    c[0:2, slice(*CON["sel2"])] = [[0, 1], [1, -1]]
    c[0:3 * NE, slice(*CON["sel24"])] = np.repeat([[0, 1], [1, -1], [0, 1]], NE, axis=0)
    return c


def build(nc, x, consts, params, win, wout, wqkvu, wo, we, be3, bkv2, out):
    with ExitStack() as ctx:
        def sb(name, shape, dt=F32):
            return ctx.enter_context(nc.sbuf_tensor(name, shape, dt))

        def sem(name):
            return ctx.enter_context(nc.semaphore(name))

        X = sb("X", [P, B * T, D])
        con, par = sb("con", [P, CON_W]), sb("par", [P, PAR_W])
        ident, head_mask, pos = (con[:, slice(*CON[n])] for n in ("ident", "mask", "pos"))
        sel2, sel24 = CON["sel2"][0], CON["sel24"][0]
        bin_s, dp_s, bq_s, bu_s, theta_s, lnw_s, lnb_s, bg_s, bout_s, bo_s = (
            par[:, slice(*PAR[n])] for n in ("bin", "dp", "bq", "bu", "theta", "lnw", "lnb", "bg", "bout", "bo"))
        win_h, win_l = sb("win_h", [P, KD, DI], F32R), sb("win_l", [P, KD, DI], F32R)
        wq_h, wq_l = sb("wq_h", [P, KD, 4 * D], F32R), sb("wq_l", [P, KD, 4 * D], F32R)
        we_h, we_l = sb("we_h", [P, KD, NE * D], F32R), sb("we_l", [P, KD, NE * D], F32R)
        wg_h, wg_l = sb("wg_h", [P, KD, NE], F32R), sb("wg_l", [P, KD, NE], F32R)
        be_rows, bkv_rows = sb("be_rows", [3 * NE, D], F32R), sb("bkv_rows", [2, 2 * D], F32R)
        ones_f, ones2 = sb("ones_f", [2, P]), sb("ones2", [2, P], F32R)
        wout_s, wo_s = sb("wout_s", [P, MI, D]), sb("wo_s", [P, KD, D])
        bc_s, g_s = sb("bc_s", [P, MI * DS]), sb("g_s", [P, MI])
        decay, minus_half = sb("decay", [P, L]), sb("minus_half", [P, T])
        cosT, sinT = sb("cosT", [P, KD, L]), sb("sinT", [P, KD, L])
        cosN, sinN = sb("cosN", [P, T, D]), sb("sinN", [P, T, D])

        stats, mv = sb("stats", [P, T, 6]), sb("mv", [P, T, 2])
        veps, rstd = sb("veps", [P, T]), sb("rstd", [P, T])
        XN = sb("XN", [P, T, D])
        XH, XL = sb("XH", [P, KD, L], F32R), sb("XL", [P, KD, L], F32R)

        work = sb("work", [P, 16 * 1024])

        def part(k, n, w):
            return work[:, k * 1024:k * 1024 + n * w].rearrange("p (n w) -> p n w", n=n)

        XI, XG, SG = part(0, MI, L), part(2, MI, L), part(4, MI, L)
        Y = [part(6, MI, L), part(8, MI, L)]
        XB = part(10, T, D)
        SQ, QC, QS = part(0, KD, L), part(1, KD, L), part(2, KD, L)
        KS, KC, KSN, V = part(3, T, D), part(4, T, D), part(5, T, D), part(6, T, D)
        KVM = part(7, 2 * KD, P)
        ON, ONA, UT, ZT = part(8, T, D), part(9, KD, L), part(11, KD, L), part(12, KD, L)
        ostats, omv = sb("ostats", [P, T, 6]), sb("omv", [P, T, 2])
        oveps, orstd = sb("oveps", [P, T]), sb("orstd", [P, T])
        ACC, TMP = part(13, T, D), part(14, 4, D)
        win_raw, we_raw = part(11, KD, DI), part(12, KD, NE * D)
        wq_raw = [cosN[:].rearrange("p t d -> p (t d)"), sinN[:].rearrange("p t d -> p (t d)")]

        bkv_raw, bkv_a = cosT[0:2, 0, :], cosT[0:2, 1, :]
        be_raw, be_a, be_hi = sinT[0:3 * NE, 0, 0:D], sinT[0:3 * NE, 0, D:], sinT[0:3 * NE, 1, 0:D].bitcast(F32R)

        th, turn, whole, prod, arg = (sb(n, [P, 2, KD, TS]) for n in ("th", "turn", "whole", "prod", "arg"))

        LGX, M8, VAL, MR = sb("LGX", [P, T, LPAD]), sb("M8", [P, T, 8]), sb("VAL", [P, T, 8]), sb("MR", [P, T, LPAD])
        CHO, TOP, LEAN, G = (sb(n, [P, T, NE]) for n in ("CHO", "TOP", "LEAN", "G"))
        GAP, TH = sb("GAP", [P, T]), sb("TH", [P, T])
        GH = sb("GH", [P, T, NE], F32R)
        G3 = sb("G3", [P, T, 3 * NE])
        G3T = sb("G3T", [3 * NE, L], F32R)
        bkv_hi = G3T[0:2, :]

        ps = ctx.enter_context(nc.psum_tensor("ps", [P, 8, 512], F32))
        TB = [ps[:, 0, :], ps[:, 1, :]]
        GB = [ps[:, 2 + i, :] for i in range(6)]

        ld_con, ld_par, ld_x0, ld_x, ld_win, ld_wout = (sem("ld_" + n) for n in ("con", "par", "x0", "x", "win", "wout"))
        ld_wq = [sem("ld_wq0"), sem("ld_wq1")]
        ld_wo, ld_we, ld_be, ld_bkv = (sem("ld_" + n) for n in ("wo", "we", "be", "bkv"))
        fills_p, fills_v = sem("fills_p"), sem("fills_v")
        win_hi, win_lo, wq_hi, wq_lo, wg_hi, wg_lo, we_hi, we_lo = (
            sem(n) for n in ("win_hi", "win_lo", "wq_hi", "wq_lo", "wg_hi", "wg_lo", "we_hi", "we_lo"))
        rows_hi, rows_a, rows_done, bc_done, g_done = (sem(n) for n in ("rows_hi", "rows_a", "rows_done", "bc_done", "g_done"))
        arg_step, arg_done, trig_done, trig_t, trig_n = (sem(n) for n in ("arg_step", "arg_done", "trig_done", "trig_t", "trig_n"))
        st_done, mv_done, rs_add, rs_done = sem("st_done"), sem("mv_done"), sem("rs_add"), sem("rs_done")
        xn_done, t_done, hi_done, lo_done = sem("xn_done"), sem("t_done"), sem("hi_done"), sem("lo_done")
        a_win, a_silu, a_xg, a_scan, a_y, a_xb, a_out, a_x1 = (
            sem("a_" + n) for n in ("win", "silu", "xg", "scan", "y", "xb", "out", "x1"))
        f_logit, f_lg, f_m8, f_val, f_gap, f_top, f_mr, f_cho, f_tanh, f_lean, f_gate, f_gh, f_g3 = (
            sem("f_" + n) for n in ("logit", "lg", "m8", "val", "gap", "top", "mr", "cho", "tanh", "lean", "gate", "gh", "g3"))
        f_g3t, f_g3s, f_bias, f_acc0, f_mm, f_acc, f_tmp, f_sum, f_x = (
            sem("f_" + n) for n in ("g3t", "g3s", "bias", "acc0", "mm", "acc", "tmp", "sum", "x"))
        b_kv, b_ks, b_v, b_kc, b_q, b_sq, b_qc, b_u, b_ut, b_outer, b_kvm = (
            sem("b_" + n) for n in ("kv", "ks", "v", "kc", "q", "sq", "qc", "u", "ut", "outer", "kvm"))
        b_o, b_ost, b_omv, b_oadd, b_ors, b_on, b_ot, b_ona, b_z, b_xb, b_out, b_x3 = (
            sem("b_" + n) for n in ("o", "ost", "omv", "oadd", "ors", "on", "ot", "ona", "z", "xb", "out", "x3"))
        stored = sem("stored")

        LN_A, LN_F1, LN_B, LN_F2 = 0, 1, 2, 3
        LN_F = (LN_F1, LN_F2)

        def after_first(b):
            return not isinstance(b, int) or b > 0

        wait_value = [nc.vector.alloc_register("wait_value"), nc.gpsimd.alloc_register("wait_value")]

        def wait_apart(engine, semaphore, value):
            if not isinstance(value, int):
                engine.reg_mov(wait_value[engine is nc.gpsimd], value)
                value = wait_value[engine is nc.gpsimd]
            engine.wait_ge(fills_p if engine is nc.gpsimd else fills_v, 2)
            engine.wait_ge(semaphore, value)

        def mm3(pe, acc, pairs, more=False):
            n = len(pairs)
            for i, (ah, al, bh, bl) in enumerate(pairs):
                pe.matmul(acc, ah, bh, start=(i == 0), stop=False)
                pe.matmul(acc, ah, bl, start=False, stop=False)
                last = pe.matmul(acc, al, bh, start=False, stop=(i == n - 1 and not more))
            return last

        def seq(b):
            return X[:, bass.ds(b * T, T), :]

        def two_tiles(b, h):
            return X[:, bass.ds(b * T + 2 * h, 2), :]

        def bank2(bank):
            return bank.rearrange("p (t d) -> p t d", t=2)

        block = ctx.enter_context(nc.Block())

        @block.sync
        def _(sp):
            xt = x.rearrange("b (t p) d -> p (b t) d", p=P)
            ot = out.rearrange("b (t p) d -> p (b t) d", p=P)
            sp.dma_start(X[:, 0:T, :], xt[:, 0:T, :]).then_inc(ld_x0, 16)
            sp.dma_start(con[:, :], consts).then_inc(ld_con, 16)
            sp.dma_start(par[:, :], params).then_inc(ld_par, 16)
            sp.dma_start(X[:, T:, :], xt[:, T:, :]).then_inc(ld_x, 16)
            sp.dma_start(wout_s[:], wout.rearrange("(m p) n -> p m n", p=P)).then_inc(ld_wout, 16)
            sp.dma_start(we_raw, we.rearrange("(k p) n -> p k n", p=P)).then_inc(ld_we, 16)
            sp.dma_start(wo_s[:], wo.rearrange("(k p) n -> p k n", p=P)).then_inc(ld_wo, 16)
            for b in range(B):
                sp.wait_ge(f_x, B * T + T * (b + 1))
                sp.dma_start(ot[:, b * T:(b + 1) * T, :], X[:, b * T:(b + 1) * T, :]).then_inc(stored, 16)
            sp.wait_ge(stored, 16 * B)

        @block.tensor
        def _(pe):
            def transposes(b, p):
                q = p * B + b
                pe.wait_ge(xn_done, q + 1)
                if p or after_first(b):
                    pe.wait_ge(lo_done, q * KD)
                for c in range(KD):
                    for t in range(T):
                        last = pe.transpose(TB[c][:, t * P:(t + 1) * P], XN[:, t, c * P:(c + 1) * P], ident)
                    last.then_inc(t_done, 1)

            def win_products(b):
                pe.wait_ge(lo_done, b * KD + KD)
                for m in range(MI):
                    if after_first(b):
                        pe.wait_ge(a_silu, (b - 1) * MI + m + 1)
                    mm3(pe, GB[m], [(win_h[:, k, m * P:(m + 1) * P], win_l[:, k, m * P:(m + 1) * P],
                                     XH[:, k, :], XL[:, k, :]) for k in range(KD)]).then_inc(a_win, 1)

            def wout_products(b, y):
                pe.wait_ge(a_y, b * MI + MI)
                for h in range(2):
                    if after_first(b):
                        pe.wait_ge(a_x1, (b - 1) * 2 + h + 1)
                    for t in (2 * h, 2 * h + 1):
                        for m in range(MI):
                            last = pe.matmul(GB[4 + h][:, (t % 2) * D:(t % 2 + 1) * D], y[:, m, t * P:(t + 1) * P],
                                             wout_s[:, m, :], start=(m == 0), stop=(m == MI - 1))
                    last.then_inc(a_out, 1)

            def a_body(b, parity, has1, has2):
                if has1:
                    win_products(b + 1)
                if has2:
                    transposes(b + 2, LN_A)
                wout_products(b, Y[parity])

            pe.wait_ge(ld_con, 16)
            transposes(0, LN_A)
            pe.wait_ge(win_lo, 1)
            win_products(0)
            transposes(1, LN_A)
            pe.wait_ge(ld_wout, 16)
            a_body(0, 0, True, True)
            with pe.Fori(0, (B - 4) // 2) as i:
                a_body(i * 2 + 1, 1, True, True)
                a_body(i * 2 + 2, 0, True, True)
            a_body(B - 3, 1, True, True)
            a_body(B - 2, 0, True, False)
            a_body(B - 1, 1, False, False)

            pe.wait_ge(trig_done, 2 * B)
            pe.wait_ge(lo_done, B * KD)
            for i, tab in enumerate((cosT, sinT)):
                if i:
                    pe.wait_ge(trig_n, 2)
                for t in range(T):
                    for c in range(KD):
                        last = pe.transpose(TB[t // 2][:, (t % 2) * D + c * P:(t % 2) * D + (c + 1) * P],
                                            tab[:, c, t * P:(t + 1) * P], ident)
                    if t % 2:
                        last.then_inc(trig_t, 1)
            pe.wait_ge(trig_n, 4)

            def experts(b, f):
                p, q = LN_F[f], f * B + b
                later = f or after_first(b)
                transposes(b, p)
                pe.wait_ge(lo_done, (p * B + b) * KD + KD)
                for t in range(T):
                    for j, (a, w) in enumerate([(XH, wg_h), (XH, wg_l), (XL, wg_h)]):
                        for k in range(KD):
                            last = pe.matmul(TB[0][:, t * NE:(t + 1) * NE], a[:, k, t * P:(t + 1) * P], w[:, k, :],
                                             start=(j == 0 and k == 0), stop=(j == 2 and k == KD - 1))
                last.then_inc(f_logit, 1)
                for t in range(T):
                    n = q * T + t
                    for pr in range(NP):
                        if later or t:
                            if pr < NP - 1:
                                pe.wait_ge(f_acc, (n - 1) * 6 + 2 * pr + 2)
                            else:
                                pe.wait_ge(f_tmp, n * 2)
                        cols = slice(pr * 2 * D, (pr + 1) * 2 * D)
                        mm3(pe, GB[pr], [(XH[:, k, t * P:(t + 1) * P], XL[:, k, t * P:(t + 1) * P],
                                          we_h[:, k, cols], we_l[:, k, cols]) for k in range(KD)]).then_inc(f_mm, 1)
                    if t == 0:
                        pe.wait_ge(f_g3, q + 1)
                        for u in range(T):
                            last = pe.transpose(TB[1][0:3 * NE, u * P:(u + 1) * P], G3[:, u, :], ident)
                        last.then_inc(f_g3t, 1)
                        pe.wait_ge(f_g3s, q + 1)
                        for h in range(2):
                            if later:
                                pe.wait_ge(f_acc0, (q - 1) * 2 + h + 1)
                            for u in range(2):
                                at = (2 * h + u) * P
                                last = pe.matmul(GB[4 + h][:, u * D:(u + 1) * D], G3T[:, at:at + P], be_rows[:, :],
                                                 start=True, stop=True)
                            last.then_inc(f_bias, 1)

            pe.wait_ge(a_silu, B * MI)
            pe.wait_ge(a_x1, B * 2)
            pe.wait_ge(we_lo, B)
            pe.wait_ge(wg_lo, 1)
            pe.wait_ge(rows_done, 2)
            experts(0, 0)
            with pe.Fori(1, B) as b:
                experts(b, 0)

            def kv_products(b, tiles):
                for t in tiles:
                    n = b * T + t
                    if after_first(b) or t >= 2:
                        pe.wait_ge(b_v, n - 1)
                    mm3(pe, GB[t % 2], [(XH[:, k, t * P:(t + 1) * P], XL[:, k, t * P:(t + 1) * P],
                                         wq_h[:, k, D:3 * D], wq_l[:, k, D:3 * D]) for k in range(KD)], more=True)
                    pe.matmul(GB[t % 2], ones2[:, :], bkv_rows[:, :], start=False, stop=True).then_inc(b_kv, 1)

            def feature_products(b, first_col, wait, done):
                for m in range(KD):
                    if wait is not None:
                        pe.wait_ge(wait[0], (b - wait[1]) * KD + m + 1)
                    col = first_col + m * P
                    mm3(pe, GB[2 + m], [(wq_h[:, k, col:col + P], wq_l[:, k, col:col + P], XH[:, k, :], XL[:, k, :])
                                        for k in range(KD)]).then_inc(done, 1)

            def q_products(b):
                feature_products(b, 0, (b_ut, 1) if after_first(b) else None, b_q)

            def u_products(b):
                feature_products(b, 3 * D, (b_sq, 0), b_u)

            def outer_products(b):
                pe.wait_ge(b_v, b * T + T)
                pe.wait_ge(b_kc, b * 4 + 4)
                if after_first(b):
                    pe.wait_ge(b_x3, b * 2)
                for c in range(KD):
                    for s, kk in enumerate((KC, KSN)):
                        g = 2 * c + s
                        for t in range(T):
                            last = pe.matmul(GB[5][:, g * P:(g + 1) * P], kk[:, t, c * P:(c + 1) * P],
                                             V[:, t, c * P:(c + 1) * P], start=(t == 0), stop=(t == T - 1))
                last.then_inc(b_outer, 1)

            def attend(b):
                pe.wait_ge(b_kvm, b + 1)
                pe.wait_ge(b_qc, b * 4 + 4)
                for h in range(2):
                    for t in (2 * h, 2 * h + 1):
                        for c in range(KD):
                            at = (t % 2) * D + c * P
                            for s, qq in enumerate((QC, QS)):
                                last = pe.matmul(GB[4 + h][:, at:at + P], qq[:, c, t * P:(t + 1) * P],
                                                 KVM[:, 2 * c + s, :], start=(s == 0), stop=(s == 1))
                    last.then_inc(b_o, 1)

            def out_transposes(b, has1):
                pe.wait_ge(b_on, b + 1)
                pe.wait_ge(lo_done, (LN_B * B + b + (2 if has1 else 1)) * KD)
                for c in range(KD):
                    for t in range(T):
                        last = pe.transpose(TB[c][:, t * P:(t + 1) * P], ON[:, t, c * P:(c + 1) * P], ident)
                    last.then_inc(b_ot, 1)

            def out_products(b):
                pe.wait_ge(b_z, b * KD + KD)
                for h in range(2):
                    for t in (2 * h, 2 * h + 1):
                        for c in range(KD):
                            last = pe.matmul(GB[4 + h][:, (t % 2) * D:(t % 2 + 1) * D], ZT[:, c, t * P:(t + 1) * P],
                                             wo_s[:, c, :], start=(c == 0), stop=(c == KD - 1))
                    last.then_inc(b_out, 1)

            def b_body(b, has1, has2):
                outer_products(b)
                if has1:
                    pe.wait_ge(lo_done, (LN_B * B + b + 2) * KD)
                    kv_products(b + 1, (0, 1))
                attend(b)
                if has1:
                    kv_products(b + 1, (2, 3))
                    q_products(b + 1)
                out_transposes(b, has1)
                if has1:
                    u_products(b + 1)
                if has2:
                    pe.wait_ge(b_ona, b * KD + KD)
                    transposes(b + 2, LN_B)
                out_products(b)

            pe.wait_ge(f_tmp, 2 * B * T)
            pe.wait_ge(f_acc, 6 * B * T)
            pe.wait_ge(f_acc0, 2 * B)
            pe.wait_ge(wq_lo, 2)
            pe.wait_ge(ld_wo, 16)
            transposes(0, LN_B)
            pe.wait_ge(lo_done, (LN_B * B + 1) * KD)
            kv_products(0, range(T))
            q_products(0)
            u_products(0)
            transposes(1, LN_B)
            b_body(0, True, True)
            with pe.Fori(1, B - 2) as b:
                b_body(b, True, True)
            b_body(B - 2, True, False)
            b_body(B - 1, False, False)

            pe.wait_ge(b_x3, B * 2)
            pe.wait_ge(b_ona, B * KD)
            with pe.Fori(0, B) as b:
                experts(b, 1)

        @block.scalar
        def _(act):
            def high_part(b, p, free, count):
                q = p * B + b
                if free is not None:
                    act.wait_ge(free, count)
                for c in range(KD):
                    act.wait_ge(t_done, q * KD + c + 1)
                    act.activation(XH[:, c, :], TB[c], ACT.Copy).then_inc(hi_done, 1)

            act.dma_start(win_raw, win.rearrange("(k p) n -> p k n", p=P)).then_inc(ld_win, 16)
            for k in range(KD):
                act.dma_start(wq_raw[k], wqkvu[k * P:(k + 1) * P, :]).then_inc(ld_wq[k], 16)
            act.dma_start(be_raw, be3).then_inc(ld_be, 16)
            act.dma_start(bkv_raw, bkv2).then_inc(ld_bkv, 16)

            def silu(b, m):
                act.wait_ge(a_win, b * MI + m + 1)
                if after_first(b):
                    act.wait_ge(a_y, (b - 1) * MI + m + 1)
                act.activation(XI[:, m, :], GB[m], ACT.Silu, bias=bin_s[:, m:m + 1]).then_inc(a_silu, 1)

            def scaled(b, m):
                act.wait_ge(a_silu, b * MI + m + 1)
                act.mul(XG[:, m, :], XI[:, m, :], g_s[:, m:m + 1]).then_inc(a_xg, 1)

            def inner(b):
                silu(b, 0)
                for m in range(1, MI):
                    silu(b, m)
                    scaled(b, m - 1)
                scaled(b, MI - 1)

            def we_high(b):
                cols = bass.ds(b * D, D)
                act.activation(we_h[:, :, cols], we_raw[:, :, cols], ACT.Copy).then_inc(we_hi, 1)

            def trig(b):
                act.wait_ge(arg_done, b + 1)
                for s, tab in enumerate((sinT, cosT)):
                    act.activation(tab[:, :, bass.ds(b * TS, TS)], arg[:, s, :, :], ACT.Sin).then_inc(trig_done, 1)

            def a_body(b, has1, has2):
                if has1:
                    inner(b + 1)
                if has2:
                    high_part(b + 2, LN_A, a_win, (b + 2) * MI)
                we_high(b)
                trig(b)

            act.wait_ge(ld_win, 16)
            act.activation(win_h[:], win_raw, ACT.Copy).then_inc(win_hi, 1)
            high_part(0, LN_A, None, 0)
            act.wait_ge(ld_par, 16)
            act.wait_ge(g_done, 1)
            inner(0)
            high_part(1, LN_A, a_win, MI)
            for k in range(KD):
                act.wait_ge(ld_wq[k], 16)
                act.activation(wq_h[:, k, :], wq_raw[k], ACT.Copy).then_inc(wq_hi, 1)
            act.activation(wg_h[:], par[:, slice(*PAR["wg"])].rearrange("p (k e) -> p k e", k=KD), ACT.Copy).then_inc(wg_hi, 1)
            act.wait_ge(ld_be, 16)
            act.activation(be_hi, be_raw, ACT.Copy).then_inc(rows_hi, 1)
            act.wait_ge(ld_bkv, 16)
            act.activation(bkv_hi, bkv_raw, ACT.Copy).then_inc(rows_hi, 1)
            act.wait_ge(fills_p, 2)
            act.activation(ones2[:, :], ones_f[:, :], ACT.Copy).then_inc(rows_hi, 1)
            act.wait_ge(rows_done, 2)
            act.wait_ge(ld_we, 16)
            a_body(0, True, True)
            with act.Fori(1, B - 2) as b:
                a_body(b, True, True)
            a_body(B - 2, True, False)
            a_body(B - 1, False, False)

            act.wait_ge(wq_lo, 2)
            for i, tab in enumerate((cosN, sinN)):
                for h in range(2):
                    act.wait_ge(trig_t, 2 * i + h + 1)
                    act.activation(tab[:, 2 * h:2 * h + 2, :], bank2(TB[h]), ACT.Copy).then_inc(trig_n, 1)

            def experts(b, f, free, count):
                p, q = LN_F[f], f * B + b
                high_part(b, p, free, count)
                act.wait_ge(f_gap, q + 1)
                act.activation(TH[:, :], GAP[:, :], ACT.Tanh, scale=0.5).then_inc(f_tanh, 1)
                act.wait_ge(f_g3t, q + 1)
                if f or after_first(b):
                    act.wait_ge(f_bias, q * 2)
                act.activation(G3T[:, :], TB[1][0:3 * NE, :], ACT.Copy).then_inc(f_g3s, 1)
                for t in range(T):
                    n = q * T + t
                    act.wait_ge(f_mm, n * NP + NP)
                    if f or after_first(b) or t >= 2:
                        act.wait_ge(f_x, n - 1)
                    for e in range(2):
                        act.mul(TMP[:, 2 * (t % 2) + e, :], GB[NP - 1][:, e * D:(e + 1) * D],
                                G[:, t, NE - 2 + e:NE - 1 + e]).then_inc(f_tmp, 1)

            experts(0, 0, a_win, B * MI)
            with act.Fori(1, B) as b:
                experts(b, 0, f_mm, b * T * NP)

            def kv_parts(b, tiles):
                for t in tiles:
                    act.wait_ge(b_kv, b * T + t + 1)
                    if after_first(b):
                        act.wait_ge(b_kc, b * 4)
                        act.wait_ge(b_outer, b)
                    act.activation(KS[:, t, :], GB[t % 2][:, 0:D], ACT.Silu).then_inc(b_ks, 1)
                    act.activation(V[:, t, :], GB[t % 2][:, D:2 * D], ACT.Copy).then_inc(b_v, 1)

            def q_part(b):
                for m in range(KD):
                    act.wait_ge(b_q, b * KD + m + 1)
                    if after_first(b):
                        act.wait_ge(b_qc, b * 4)
                    act.activation(SQ[:, m, :], GB[2 + m], ACT.Silu, bias=bq_s[:, m:m + 1]).then_inc(b_sq, 1)

            def u_part(b):
                for m in range(KD):
                    act.wait_ge(b_u, b * KD + m + 1)
                    if after_first(b):
                        act.wait_ge(b_z, b * KD)
                    act.activation(UT[:, m, :], GB[2 + m], ACT.Identity, bias=bu_s[:, m:m + 1]).then_inc(b_ut, 1)

            def affine(b):
                for c in range(KD):
                    act.wait_ge(b_ot, b * KD + c + 1)
                    if after_first(b):
                        act.wait_ge(b_z, b * KD)
                    act.activation(ONA[:, c, :], TB[c], ACT.Identity, scale=lnw_s[:, c:c + 1],
                                   bias=lnb_s[:, c:c + 1]).then_inc(b_ona, 1)

            def b_body(b, has1, has2):
                if has1:
                    kv_parts(b + 1, range(T))
                    q_part(b + 1)
                affine(b)
                if has1:
                    u_part(b + 1)
                if has2:
                    high_part(b + 2, LN_B, b_u, (b + 2) * KD)

            high_part(0, LN_B, f_mm, B * T * NP)
            kv_parts(0, range(T))
            q_part(0)
            u_part(0)
            high_part(1, LN_B, b_u, KD)
            b_body(0, True, True)
            with act.Fori(1, B - 2) as b:
                b_body(b, True, True)
            b_body(B - 2, True, False)
            b_body(B - 1, False, False)

            experts(0, 1, b_u, B * KD)
            with act.Fori(1, B) as b:
                experts(b, 1, f_mm, (B + b) * T * NP)

        @block.gpsimd
        def _(pool):
            def inv_std(b, p):
                q = p * B + b
                wait_apart(pool, mv_done, q + 1)
                pool.tensor_scalar(veps[:, :], mv[:, :, 1], EPS, None, ALU.add).then_inc(rs_add, 1)
                pool.wait_ge(rs_add, q + 1)
                pool.tensor_tensor(rstd[:, :], veps[:, :], minus_half[:, :], ALU.pow).then_inc(rs_done, 1)

            pool.memset(minus_half[:, :], -0.5).then_inc(fills_p, 1)
            pool.memset(ones_f[:, :], 1.0).then_inc(fills_p, 1)
            pool.wait_ge(fills_p, 2)
            inv_std(0, LN_A)
            inv_std(1, LN_A)
            inv_std(2, LN_A)

            ARG_STEPS = 12

            def trig_arguments(b):
                step = [0]

                def stepped(ins):
                    step[0] += 1
                    ins.then_inc(arg_step, 1)

                def settled():
                    wait_apart(pool, arg_step, b * ARG_STEPS + step[0])

                if after_first(b):
                    pool.wait_ge(trig_done, b * 2)
                for c in range(KD):
                    stepped(pool.tensor_tensor(th[:, 0, c, :], pos[:, bass.ds(b * TS, TS)],
                                                 theta_s[:, c:c + 1].to_broadcast([P, TS]), ALU.mult))
                settled()
                stepped(pool.tensor_scalar(turn[:, 0, :, :], th[:, 0, :, :], INV_TWO_PI, None, ALU.mult))
                stepped(pool.tensor_scalar(turn[:, 1, :, :], th[:, 0, :, :], INV_TWO_PI, 0.25, ALU.mult, ALU.add))
                settled()
                stepped(pool.tensor_scalar(whole[:], turn[:], ROUND, -ROUND, ALU.add, ALU.add))
                settled()
                for i, part_of_2pi in enumerate((TWO_PI_1, TWO_PI_2, TWO_PI_3)):
                    stepped(pool.tensor_scalar(prod[:], whole[:], part_of_2pi, None, ALU.mult))
                    settled()
                    less = th[:, 0:1, :, :].to_broadcast([P, 2, KD, TS]) if i == 0 else turn[:]
                    stepped(pool.tensor_tensor(turn[:], less, prod[:], ALU.subtract))
                    settled()
                pool.tensor_scalar(arg[:, 0, :, :], turn[:, 0, :, :], PI_BELOW, -PI_BELOW, ALU.min, ALU.max)
                stepped(pool.tensor_scalar(prod[:, 1, :, :], turn[:, 1, :, :], float(np.pi / 2), None, ALU.add))
                settled()
                pool.tensor_scalar(arg[:, 1, :, :], prod[:, 1, :, :], PI_BELOW, -PI_BELOW, ALU.min, ALU.max).then_inc(arg_done, 1)
                assert step[0] == ARG_STEPS

            def we_low(b):
                pool.wait_ge(we_hi, b + 1)
                cols = bass.ds(b * D, D)
                pool.tensor_tensor(we_l[:, :, cols], we_raw[:, :, cols], we_h[:, :, cols].bitcast(F32),
                                   ALU.subtract).then_inc(we_lo, 1)

            def biased(b, bias, read, done):
                if after_first(b):
                    pool.wait_ge(read, b * 2)
                pool.tensor_tensor(XB, seq(b), bias.unsqueeze(1).to_broadcast([P, T, D]), ALU.add).then_inc(done, 1)

            def a_body(b, has3):
                biased(b, bout_s, a_x1, a_xb)
                trig_arguments(b)
                we_low(b)
                if has3:
                    inv_std(b + 3, LN_A)

            pool.wait_ge(ld_par, 16)
            pool.wait_ge(ld_con, 16)
            pool.wait_ge(ld_x, 16)
            a_body(0, True)
            with pool.Fori(1, B - 3) as b:
                a_body(b, True)
            with pool.Fori(B - 3, B) as b:
                a_body(b, False)

            def experts(b, f, has1):
                q = f * B + b
                if has1:
                    inv_std(b + 1, LN_F[f])
                for t in range(T):
                    n = q * T + t
                    two = TMP[:, 2 * (t % 2):2 * (t % 2) + 2, :]
                    pool.wait_ge(f_tmp, n * 2 + 2)
                    pool.tensor_tensor(two[:, 0, :], two[:, 0, :], two[:, 1, :], ALU.add).then_inc(f_sum, 1)
                    pool.wait_ge(f_sum, n + 1)
                    pool.wait_ge(f_acc, n * 6 + 6)
                    pool.tensor_tensor(X[:, bass.ds(b * T + t, 1), :], two[:, 0:1, :], ACC[:, t:t + 1, :],
                                       ALU.add).then_inc(f_x, 1)

            inv_std(0, LN_F1)
            with pool.Fori(0, B - 1) as b:
                experts(b, 0, True)
            experts(B - 1, 0, False)

            def q_parts(b):
                for c in range(KD):
                    pool.wait_ge(b_sq, b * KD + c + 1)
                    if after_first(b):
                        pool.wait_ge(b_o, b * 2)
                    pool.tensor_tensor(QC[:, c, :], SQ[:, c, :], cosT[:, c, :], ALU.mult).then_inc(b_qc, 1)
                    pool.tensor_tensor(QS[:, c, :], SQ[:, c, :], sinT[:, c, :], ALU.mult).then_inc(b_qc, 1)

            def out_inv_std(b):
                wait_apart(pool, b_omv, b + 1)
                pool.tensor_scalar(oveps[:, :], omv[:, :, 1], EPS, None, ALU.add).then_inc(b_oadd, 1)
                pool.wait_ge(b_oadd, b + 1)
                pool.tensor_tensor(orstd[:, :], oveps[:, :], minus_half[:, :], ALU.pow).then_inc(b_ors, 1)

            def b_body(b, has1, has3):
                out_inv_std(b)
                biased(b, bo_s, b_x3, b_xb)
                if has1:
                    q_parts(b + 1)
                if has3:
                    inv_std(b + 3, LN_B)

            inv_std(0, LN_B)
            inv_std(1, LN_B)
            q_parts(0)
            inv_std(2, LN_B)
            b_body(0, True, True)
            with pool.Fori(1, B - 3) as b:
                b_body(b, True, True)
            with pool.Fori(B - 3, B - 1) as b:
                b_body(b, True, False)
            b_body(B - 1, False, False)

            inv_std(0, LN_F2)
            with pool.Fori(0, B - 1) as b:
                experts(b, 1, True)
            experts(B - 1, 1, False)

        @block.vector
        def _(dve):
            def moments(b, p, ready=None, count=0):
                q = p * B + b
                if ready is not None:
                    dve.wait_ge(ready, count)
                for t in range(T):
                    last = dve.bn_stats(stats[:, t, :], X[:, bass.ds(b * T + t, 1), :].squeeze(1))
                last.then_inc(st_done, 1)
                wait_apart(dve, st_done, q + 1)
                for t in range(T):
                    last = dve.bn_aggr(mv[:, t, :], stats[:, t, :])
                last.then_inc(mv_done, 1)

            def normalise(b, p):
                q = p * B + b
                dve.wait_ge(rs_done, q + 1)
                if p or after_first(b):
                    dve.wait_ge(t_done, q * KD)
                for t in range(T):
                    last = dve.tensor_scalar(XN[:, t, :], X[:, bass.ds(b * T + t, 1), :].squeeze(1), mv[:, t, 0:1],
                                             rstd[:, t:t + 1], ALU.subtract, ALU.mult)
                last.then_inc(xn_done, 1)

            def low_part(b, p):
                q = p * B + b
                for c in range(KD):
                    dve.wait_ge(hi_done, q * KD + c + 1)
                    dve.tensor_tensor(XL[:, c, :], TB[c], XH[:, c, :].bitcast(F32), ALU.subtract).then_inc(lo_done, 1)

            def scan(b, m):
                dve.wait_ge(a_xg, b * MI + m + 1)
                dve.tensor_tensor_scan(SG[:, m, :], decay[:, :], XG[:, m, :], 0.0, ALU.mult, ALU.add).then_inc(a_scan, 1)

            def channel_out(b, y, m):
                if m == 0 and (not isinstance(b, int) or b >= 2):
                    dve.wait_ge(a_out, (b - 1) * 2)
                dve.wait_ge(a_scan, b * MI + m + 1)
                dve.scalar_tensor_tensor(out=y[:, m, :], in0=XI[:, m, :], scalar=dp_s[:, m:m + 1], in1=SG[:, m, :],
                                         op0=ALU.mult, op1=ALU.add).then_inc(a_y, 1)

            def channels(b, y):
                scan(b, 0)
                for m in range(1, MI):
                    scan(b, m)
                    channel_out(b, y, m - 1)
                channel_out(b, y, MI - 1)

            def a_residual(b):
                dve.wait_ge(a_xb, b + 1)
                for h in range(2):
                    dve.wait_ge(a_out, b * 2 + h + 1)
                    dve.tensor_tensor(two_tiles(b, h), bank2(GB[4 + h]), XB[:, 2 * h:2 * h + 2, :],
                                      ALU.add).then_inc(a_x1, 1)

            def a_body(b, parity, has1, has2, has3):
                if has2:
                    normalise(b + 2, LN_A)
                if has1:
                    channels(b + 1, Y[1 - parity])
                if has2:
                    low_part(b + 2, LN_A)
                if has3:
                    moments(b + 3, LN_A)
                a_residual(b)

            dve.memset(decay[:, :], DECAY).then_inc(fills_v, 1)
            dve.memset(VAL[:], SENTINEL).then_inc(fills_v, 1)
            dve.memset(LGX[:], SENTINEL).then_inc(fills_v, 1)
            dve.wait_ge(fills_v, 3)
            dve.wait_ge(ld_x0, 16)
            moments(0, LN_A)
            dve.wait_ge(ld_par, 16)
            dve.tensor_tensor(bc_s[:, :], par[:, slice(*PAR["bp"])], par[:, slice(*PAR["cp"])], ALU.mult).then_inc(bc_done, 1)
            normalise(0, LN_A)
            dve.wait_ge(win_hi, 1)
            dve.tensor_tensor(win_l[:], win_raw, win_h[:].bitcast(F32), ALU.subtract).then_inc(win_lo, 1)
            low_part(0, LN_A)
            dve.wait_ge(bc_done, 1)
            dve.tensor_reduce(g_s[:, :], bc_s[:, :].rearrange("p (m s) -> p m s", m=MI), AX.X, ALU.add).then_inc(g_done, 1)
            dve.wait_ge(ld_x, 16)
            moments(1, LN_A)
            normalise(1, LN_A)
            channels(0, Y[0])
            low_part(1, LN_A)
            for k in range(KD):
                dve.wait_ge(wq_hi, k + 1)
                dve.tensor_tensor(wq_l[:, k, :], wq_raw[k], wq_h[:, k, :].bitcast(F32), ALU.subtract).then_inc(wq_lo, 1)
            dve.wait_ge(wg_hi, 1)
            dve.tensor_tensor(wg_l[:], par[:, slice(*PAR["wg"])].rearrange("p (k e) -> p k e", k=KD),
                              wg_h[:].bitcast(F32), ALU.subtract).then_inc(wg_lo, 1)
            dve.wait_ge(ld_con, 16)
            for i, (rows, raw, hi, a, sel, n) in enumerate([(be_rows, be_raw, be_hi, be_a, sel24, 3 * NE),
                                                           (bkv_rows, bkv_raw, bkv_hi, bkv_a, sel2, 2)]):
                dve.wait_ge(rows_hi, i + 1)
                dve.tensor_scalar(a, raw, con[0:n, sel:sel + 1], None, ALU.mult).then_inc(rows_a, 1)
                dve.wait_ge(rows_a, i + 1)
                dve.scalar_tensor_tensor(out=rows[:, :], in0=hi.bitcast(F32), scalar=con[0:n, sel + 1:sel + 2],
                                         in1=a, op0=ALU.mult, op1=ALU.add).then_inc(rows_done, 1)
            moments(2, LN_A)
            a_body(0, 0, True, True, True)
            with dve.Fori(0, (B - 4) // 2) as i:
                a_body(i * 2 + 1, 1, True, True, True)
                a_body(i * 2 + 2, 0, True, True, True)
            a_body(B - 3, 1, True, True, False)
            a_body(B - 2, 0, True, False, False)
            a_body(B - 1, 1, False, False, False)

            def gates(b, f):
                q = f * B + b
                lg = LGX[:, :, 0:NE]
                dve.wait_ge(f_logit, q + 1)
                dve.tensor_tensor(lg, TB[0][:, 0:T * NE].rearrange("p (t e) -> p t e", t=T),
                                  bg_s.unsqueeze(1).to_broadcast([P, T, NE]), ALU.add).then_inc(f_lg, 1)
                wait_apart(dve, f_lg, q + 1)
                for t in range(T):
                    last = dve.max(M8[:, t, :], LGX[:, t, :])
                last.then_inc(f_m8, 1)
                dve.wait_ge(f_m8, q + 1)
                dve.tensor_tensor(GAP[:, :], M8[:, :, 0], M8[:, :, 1], ALU.subtract).then_inc(f_gap, 1)
                dve.tensor_copy(VAL[:, :, 0:2], M8[:, :, 0:2]).then_inc(f_val, 1)
                dve.tensor_tensor(TOP[:], lg, M8[:, :, 0:1].to_broadcast([P, T, NE]), ALU.is_ge).then_inc(f_top, 1)
                wait_apart(dve, f_val, q + 1)
                for t in range(T):
                    last = dve.match_replace(out=MR[:, t, :], in_to_replace=VAL[:, t, :], in_values=LGX[:, t, :],
                                             imm_value=-SENTINEL)
                last.then_inc(f_mr, 1)
                dve.wait_ge(f_mr, q + 1)
                dve.tensor_tensor(CHO[:], MR[:, :, 0:NE], lg, ALU.not_equal).then_inc(f_cho, 1)
                dve.wait_ge(f_tanh, q + 1)
                dve.wait_ge(f_top, q + 1)
                dve.scalar_tensor_tensor(out=LEAN[:], in0=TOP[:], scalar=-0.5, in1=TH[:, :].unsqueeze(2).to_broadcast([P, T, NE]),
                                         op0=ALU.add, op1=ALU.mult).then_inc(f_lean, 1)
                dve.wait_ge(f_lean, q + 1)
                dve.wait_ge(f_cho, q + 1)
                if f or after_first(b):
                    dve.wait_ge(f_tmp, q * T * 2)
                dve.scalar_tensor_tensor(out=G[:], in0=LEAN[:], scalar=0.5, in1=CHO[:],
                                         op0=ALU.add, op1=ALU.mult).then_inc(f_gate, 1)
                dve.wait_ge(f_gate, q + 1)
                dve.tensor_copy(GH[:], G[:]).then_inc(f_gh, 1)
                dve.wait_ge(f_gh, q + 1)
                if f or after_first(b):
                    dve.wait_ge(f_g3t, q)
                gh = GH[:].bitcast(F32)
                dve.tensor_copy(G3[:, :, 0:NE], gh)
                dve.tensor_copy(G3[:, :, NE:2 * NE], gh)
                dve.tensor_tensor(G3[:, :, 2 * NE:], G[:], gh, ALU.subtract).then_inc(f_g3, 1)

            def experts(b, f, has1, ready, count):
                q = f * B + b
                low_part(b, LN_F[f])
                gates(b, f)
                if has1:
                    moments(b + 1, LN_F[f], ready, count)
                if f or after_first(b):
                    dve.wait_ge(f_x, q * T)
                for h in range(2):
                    dve.wait_ge(f_bias, q * 2 + h + 1)
                    dve.tensor_tensor(ACC[:, 2 * h:2 * h + 2, :], bank2(GB[4 + h]), two_tiles(b, h), ALU.add).then_inc(f_acc0, 1)
                dve.wait_ge(f_acc0, q * 2 + 2)
                for t in range(T):
                    n = q * T + t
                    for e in range(NE - 2):
                        if e % 2 == 0:
                            dve.wait_ge(f_mm, n * NP + e // 2 + 1)
                        if e:
                            dve.wait_ge(f_acc, n * 6 + e)
                        dve.scalar_tensor_tensor(out=ACC[:, t, :], in0=GB[e // 2][:, (e % 2) * D:(e % 2 + 1) * D],
                                                 scalar=G[:, t, e:e + 1], in1=ACC[:, t, :],
                                                 op0=ALU.mult, op1=ALU.add).then_inc(f_acc, 1)
                if has1:
                    normalise(b + 1, LN_F[f])

            moments(0, LN_F1, a_x1, 2)
            normalise(0, LN_F1)
            experts(0, 0, True, a_x1, 4)
            with dve.Fori(1, B - 1) as b:
                experts(b, 0, True, a_x1, b * 2 + 4)
            experts(B - 1, 0, False, None, 0)

            def k_parts(b, h):
                dve.wait_ge(b_ks, b * T + 2 * h + 2)
                if after_first(b):
                    dve.wait_ge(b_outer, b)
                for part_, tab in ((KC, cosN), (KSN, sinN)):
                    dve.tensor_tensor(part_[:, 2 * h:2 * h + 2, :], KS[:, 2 * h:2 * h + 2, :], tab[:, 2 * h:2 * h + 2, :],
                                      ALU.mult).then_inc(b_kc, 1)

            def masked_sums(b):
                dve.wait_ge(b_outer, b + 1)
                if after_first(b):
                    dve.wait_ge(b_o, b * 2)
                dve.tensor_tensor(KVM, GB[5].rearrange("p (g n) -> p g n", g=2 * KD),
                                  head_mask.unsqueeze(1).to_broadcast([P, 2 * KD, P]), ALU.mult).then_inc(b_kvm, 1)

            def out_moments(b):
                for t in range(T):
                    if t % 2 == 0:
                        dve.wait_ge(b_o, b * 2 + t // 2 + 1)
                    last = dve.bn_stats(ostats[:, t, :], GB[4 + t // 2][:, (t % 2) * D:(t % 2 + 1) * D])
                last.then_inc(b_ost, 1)
                wait_apart(dve, b_ost, b + 1)
                for t in range(T):
                    last = dve.bn_aggr(omv[:, t, :], ostats[:, t, :])
                last.then_inc(b_omv, 1)

            def out_normalise(b):
                dve.wait_ge(b_ors, b + 1)
                if after_first(b):
                    dve.wait_ge(b_ot, b * KD)
                for t in range(T):
                    last = dve.tensor_scalar(ON[:, t, :], GB[4 + t // 2][:, (t % 2) * D:(t % 2 + 1) * D], omv[:, t, 0:1],
                                             orstd[:, t:t + 1], ALU.subtract, ALU.mult)
                last.then_inc(b_on, 1)

            def gated(b):
                for c in range(KD):
                    dve.wait_ge(b_ona, b * KD + c + 1)
                    dve.wait_ge(b_ut, b * KD + c + 1)
                    if c == 0 and after_first(b):
                        dve.wait_ge(b_out, b * 2)
                    dve.tensor_tensor(ZT[:, c, :], UT[:, c, :], ONA[:, c, :], ALU.mult).then_inc(b_z, 1)

            def b_residual(b):
                dve.wait_ge(b_xb, b + 1)
                for h in range(2):
                    dve.wait_ge(b_out, b * 2 + h + 1)
                    dve.tensor_tensor(two_tiles(b, h), bank2(GB[4 + h]), XB[:, 2 * h:2 * h + 2, :], ALU.add).then_inc(b_x3, 1)

            def b_body(b, has1, has2, has3):
                masked_sums(b)
                if has1:
                    k_parts(b + 1, 0)
                out_moments(b)
                if has1:
                    k_parts(b + 1, 1)
                if has2:
                    normalise(b + 2, LN_B)
                out_normalise(b)
                gated(b)
                if has2:
                    low_part(b + 2, LN_B)
                if has3:
                    moments(b + 3, LN_B)
                b_residual(b)

            moments(0, LN_B, f_x, T)
            normalise(0, LN_B)
            moments(1, LN_B, f_x, 2 * T)
            low_part(0, LN_B)
            normalise(1, LN_B)
            dve.wait_ge(trig_n, 4)
            k_parts(0, 0)
            k_parts(0, 1)
            low_part(1, LN_B)
            moments(2, LN_B, f_x, B * T)
            b_body(0, True, True, True)
            with dve.Fori(1, B - 3) as b:
                b_body(b, True, True, True)
            b_body(B - 3, True, True, False)
            b_body(B - 2, True, False, False)
            b_body(B - 1, False, False, False)

            moments(0, LN_F2, b_x3, 2)
            normalise(0, LN_F2)
            with dve.Fori(0, B - 1) as b:
                experts(b, 1, True, b_x3, b * 2 + 4)
            experts(B - 1, 1, False, None, 0)


def kernel(**inputs):
    import concourse.bacc as bacc
    from concourse.bass_utils import run_bass_kernel_spmd

    a = {n.split("L0_")[1]: np.asarray(v) for n, v in inputs.items()}

    def cols(v):
        return v.reshape(-1, P).T

    def rows(v):
        return np.broadcast_to(v.reshape(1, -1), (P, v.size))

    def chunks(m):
        return m.reshape(-1, P, m.shape[1]).transpose(1, 0, 2).reshape(P, -1)

    bqkvu = a["attn_b_bqkvu"]
    params = {
        "bin": cols(a["attn_a_bin_"]), "dp": cols(a["attn_a_Dp"]), "bp": chunks(a["attn_a_Bp"]),
        "cp": chunks(a["attn_a_Cp"].T), "bq": cols(bqkvu[0:D]), "bu": cols(bqkvu[3 * D:]),
        "theta": cols(a["attn_b_theta"].reshape(-1)), "lnw": cols(a["attn_b_ln_w"]), "lnb": cols(a["attn_b_ln_b"]),
        "bg": rows(a["ffn_bg"]), "wg": chunks(a["ffn_Wg"]), "bout": rows(a["attn_a_bout"]), "bo": rows(a["attn_b_bout"]),
    }
    arrays = {
        "x": a["attn_a_x"],
        "consts": shape_constants(),
        "params": np.concatenate([params[n] for n in PAR], axis=1),
        "win": a["attn_a_Win"],
        "wout": a["attn_a_Wout"],
        "wqkvu": a["attn_b_Wqkvu"].T,
        "wo": a["attn_b_Wout"].T,
        "we": a["ffn_We"].transpose(2, 0, 1).reshape(D, NE * D),
        "be3": np.concatenate([a["ffn_be"]] * 3),
        "bkv2": np.stack([bqkvu[D:3 * D]] * 2),
    }
    arrays = {n: np.ascontiguousarray(v) for n, v in arrays.items()}
    nc = bacc.Bacc("TRN2", target_bir_lowering=False, num_devices=1)
    args = [nc.dram_tensor(n, v.shape, mybir.dt.from_np(v.dtype), kind="ExternalInput").ap() for n, v in arrays.items()]
    out = nc.dram_tensor("out", (B, L, D), F32, kind="ExternalOutput").ap()
    build(nc, *args, out)
    r = run_bass_kernel_spmd(nc, [arrays], core_ids=[0])
    return r.results[0]["out"]
```

```python
from contextlib import ExitStack

import numpy as np

import concourse.bass as bass
from concourse import mybir

ALU = mybir.AluOpType
ACT = mybir.ActivationFunctionType
AX = mybir.AxisListType
F32 = mybir.dt.float32
F32R = mybir.dt.float32r
BF16 = mybir.dt.bfloat16
U32 = mybir.dt.uint32
I32 = mybir.dt.int32

P = 128
B, L, D = 8, 512, 256
T = L // P
KD = D // P
DI = 512
MI = DI // P
DS = 16
DH = 16
NE = 8
ROOM = B * L // P + 1
TILES = 2 * B * T + NE
AT_ONCE = 8
PAIRS = AT_ONCE // 2
ROUNDS = TILES // AT_ONCE
ROW = 260
R_W2, R_DW, R_E1, R_TO = D, D + 1, D + 2, D + 3
NOWHERE = 1.0e6
LPAD = 16
DECAY = 0.9
EPS = 1e-5
SENTINEL = -3.0e38

TWO_PI_1, TWO_PI_2 = 6.28125, 0.0019350051879882812
TWO_PI_3 = float(2 * np.pi - TWO_PI_1 - TWO_PI_2)
INV_TWO_PI = float(1 / (2 * np.pi))
ROUND = 12582912.0
PI_BELOW = 3.1415925


def columns(*widths):
    at, out = 0, {}
    for name, w in widths:
        out[name] = (at, at + w)
        at += w
    return out, at


CON, CON_W = columns(("ident", P), ("mask", P), ("pos", L), ("before", P), ("expert", NE), ("first", NE), ("lane", 1),
                     ("place", B * T), ("tile", TILES), ("sel2", 2))
PAR, PAR_W = columns(("bin", MI), ("dp", MI), ("bp", MI * DS), ("cp", MI * DS), ("bq", KD), ("bu", KD), ("theta", KD),
                     ("lnw", KD), ("lnb", KD), ("bg", NE), ("wg", KD * NE))
ROWS, ROWS_W = columns(("bkv", 2 * D), ("bout", D), ("bo", D))


def shape_constants():
    c = np.zeros((P, CON_W), np.float32)
    c[:, slice(*CON["ident"])] = np.eye(P)
    c[:, slice(*CON["mask"])] = np.kron(np.eye(P // DH), np.ones((DH, DH)))
    c[:, slice(*CON["pos"])] = np.arange(L)[None, :]
    c[0:2, slice(*CON["sel2"])] = [[0, 1], [1, -1]]
    c[:, slice(*CON["before"])] = np.triu(np.ones((P, P)), 1)
    c[:, slice(*CON["expert"])] = np.arange(NE)[None, :]
    c[:, slice(*CON["first"])] = np.arange(NE)[None, :] * ROOM * P
    c[:, slice(*CON["lane"])] = np.arange(P)[:, None]
    c[:, slice(*CON["place"])] = 2 * (np.arange(B * T)[None, :] * P + np.arange(P)[:, None]) + 1
    c[:, slice(*CON["tile"])] = np.arange(TILES)[None, :]
    return c


def build(nc, x, consts, params, win, wout, wqkvu, wo, we, be2, rows2, slots, chosen, out):
    with ExitStack() as ctx:
        def sb(name, shape, dt=F32):
            return ctx.enter_context(nc.sbuf_tensor(name, shape, dt))

        def sem(name):
            return ctx.enter_context(nc.semaphore(name))

        X = sb("X", [P, B * T, D])
        con, par = sb("con", [P, CON_W]), sb("par", [P, PAR_W])
        ident, head_mask, pos, expert, first_slot, lane, place, tile = (
            con[:, slice(*CON[n])] for n in ("ident", "mask", "pos", "expert", "first", "lane", "place", "tile"))
        sel2 = CON["sel2"][0]
        bin_s, dp_s, bq_s, bu_s, theta_s, lnw_s, lnb_s, bg_s, wg_s = (
            par[:, slice(*PAR[n])] for n in ("bin", "dp", "bq", "bu", "theta", "lnw", "lnb", "bg", "wg"))
        win_h, win_l = sb("win_h", [P, KD, DI], F32R), sb("win_l", [P, KD, DI], F32R)
        wq_h, wq_l = sb("wq_h", [P, KD, 4 * D], F32R), sb("wq_l", [P, KD, 4 * D], F32R)
        we_h, we_l = sb("we_h", [P, KD, NE * D], F32R), sb("we_l", [P, KD, NE * D], F32R)
        be_rows, rows = sb("be_rows", [2, NE * D], F32R), sb("rows", [2, ROWS_W], F32R)
        ones_f, ones2 = sb("ones_f", [2, P]), sb("ones2", [2, P], F32R)
        wout_s, wo_s = sb("wout_s", [P, MI, D]), sb("wo_s", [P, KD, D])
        bc_s, g_s = sb("bc_s", [P, MI * DS]), sb("g_s", [P, MI])
        decay, minus_half = sb("decay", [P, L]), sb("minus_half", [P, T])
        cosT, sinT = sb("cosT", [P, KD, L]), sb("sinT", [P, KD, L])
        cosN, sinN = sb("cosN", [P, T, D]), sb("sinN", [P, T, D])

        stats, mv = sb("stats", [P, T, 6]), sb("mv", [P, T, 2])
        veps, rstd = sb("veps", [P, T]), sb("rstd", [P, T])
        XN = sb("XN", [P, T, D])
        XH, XL = sb("XH", [P, KD, L], F32R), sb("XL", [P, KD, L], F32R)

        work = sb("work", [P, 12 * 1024])

        def part(k, n, w):
            return work[:, k * 1024:k * 1024 + n * w].rearrange("p (n w) -> p n w", n=n)

        XI, XG, SG = part(0, MI, L), part(2, MI, L), part(4, MI, L)
        Y = [part(6, MI, L), part(8, MI, L)]
        SQ, QC, QS = part(0, KD, L), part(1, KD, L), part(2, KD, L)
        KS, KC, KSN, V = part(3, T, D), part(4, T, D), part(5, T, D), part(6, T, D)
        KVM = part(7, 2 * KD, P)
        ON, ONA, UT, ZT = part(8, T, D), part(9, KD, L), part(10, KD, L), part(11, KD, L)
        ostats, omv = sb("ostats", [P, T, 6]), sb("omv", [P, T, 2])
        oveps, orstd = sb("oveps", [P, T]), sb("orstd", [P, T])
        XR = work[:, 0:AT_ONCE * ROW].rearrange("p (s w) -> p s w", s=AT_ONCE)
        YO = part(3, AT_ONCE, D)
        EXH, EXL = ([whole_[:, i, :] for whole_ in parts for i in range(KD)] for parts in ((XH, win_h), (XL, win_l)))
        th, whole, turn = part(5, KD, L), part(6, 2 * KD, L), part(8, 2 * KD, L)
        we_raw = [part(10, KD, D), work[:, 10752:11264].rearrange("p (k d) -> p k d", k=KD)]
        win_raw = part(11, KD, DI)
        be_raw = work[0:2, 10 * 1024:12 * 1024]
        wq_raw = [cosN[:].rearrange("p t d -> p (t d)"), sinN[:].rearrange("p t d -> p (t d)")]
        rows_raw = cosT[0:2, :, :].rearrange("p k l -> p (k l)")

        rstats, rmv = sb("rstats", [P, T, 6]), sb("rmv", [P, T, 2])
        rveps, rrstd = sb("rveps", [P, T]), sb("rrstd", [P, T])
        XNR = [sb(f"XNR{i}", [P, T, ROW]) for i in range(2)]
        XT = sb("XT", [P, KD, L])
        LGX, M8, MIX = sb("LGX", [P, T, LPAD]), sb("M8", [P, T, 8]), sb("MIX", [P, T, 8], U32)
        EI, GAP = sb("EI", [P, T, 2]), sb("GAP", [P, T])
        MASK, BOTH = sb("MASK", [P, T, 2, NE], BF16), sb("BOTH", [P, T, NE], BF16)
        POS, PICK, SLOT = sb("POS", [P, T, NE]), sb("PICK", [P, T, 2, NE]), sb("SLOT", [P, T, 2])
        IDX = [sb(f"IDX{i}", [P, 2 * T], U32) for i in range(2)]
        before, ones_b = sb("before", [P, P], BF16), sb("ones_b", [P, P], BF16)
        NEXT = sb("NEXT", [P, NE])
        PAD = sb("PAD", [P, ROW])
        PADI = sb("PADI", [P, NE], U32)
        CNT, NT, CI, ones_e = sb("CNT", [P, NE]), sb("NT", [P, NE]), sb("CI", [P, NE]), sb("ones_e", [P, NE])
        CMP = work[:, 4096:4096 + TILES * NE].rearrange("p (t e) -> p t e", e=NE)
        ET, SKIP, RT = sb("ET", [P, TILES]), sb("SKIP", [P, TILES]), sb("RT", [P, TILES])
        EC = sb("EC", [P, TILES])
        RP_f, EP_f = sb("RP_f", [1, TILES // 2]), sb("EP_f", [1, ROUNDS])
        RP, EP = sb("RP", [1, TILES // 2], I32), sb("EP", [1, ROUNDS], I32)
        IND, GW, DEST = sb("IND", [P, AT_ONCE]), sb("GW", [P, AT_ONCE]), sb("DEST", [P, AT_ONCE], U32)

        ps = ctx.enter_context(nc.psum_tensor("ps", [P, 8, 512], F32))
        TB = [ps[:, 0, :], ps[:, 1, :]]
        GB = [ps[:, 2 + i, :] for i in range(6)]
        ET4 = [TB[0], TB[1], GB[4], GB[5]]

        ld_con, ld_par, ld_x0, ld_x, ld_win, ld_wout = (sem("ld_" + n) for n in ("con", "par", "x0", "x", "win", "wout"))
        ld_wq = [sem("ld_wq0"), sem("ld_wq1")]
        ld_wo, ld_be, ld_rows = (sem("ld_" + n) for n in ("wo", "be", "rows"))
        ld_we = [sem("ld_we0"), sem("ld_we1")]
        fills_p, fills_v = sem("fills_p"), sem("fills_v")
        win_hi, win_lo, wq_hi, wq_lo, we_hi, we_lo = (
            sem(n) for n in ("win_hi", "win_lo", "wq_hi", "wq_lo", "we_hi", "we_lo"))
        rows_hi, rows_a, rows_done, bc_done, g_done = (sem(n) for n in ("rows_hi", "rows_a", "rows_done", "bc_done", "g_done"))
        before_done = sem("before_done")
        arg_step, arg_done, trig_done, trig_t, trig_n = (sem(n) for n in ("arg_step", "arg_done", "trig_done", "trig_t", "trig_n"))
        st_done, mv_done, rs_add, rs_done = sem("st_done"), sem("mv_done"), sem("rs_add"), sem("rs_done")
        xn_done, t_done, hi_done, lo_done = sem("xn_done"), sem("t_done"), sem("hi_done"), sem("lo_done")
        a_win, a_silu, a_xg, a_scan, a_y, a_out, a_x1 = (
            sem("a_" + n) for n in ("win", "silu", "xg", "scan", "y", "out", "x1"))
        r_st, r_mv, r_add, r_rs, r_xn, r_t, r_xt, r_logit, r_lg, r_m8, r_mi, r_ei, r_gap = (
            sem("r_" + n) for n in ("st", "mv", "add", "rs", "xn", "t", "xt", "logit", "lg", "m8", "mi", "ei", "gap"))
        r_mask, r_both, r_cols, r_row, r_rank, r_pos, r_next, r_pick, r_slot, r_idx = (
            sem("r_" + n) for n in ("mask", "both", "cols", "row", "rank", "pos", "next", "pick", "slot", "idx"))
        r_scattered = [sem("r_scattered0"), sem("r_scattered1")]
        tab_step, tab_done, pad_idx, padded, spare = (sem(n) for n in ("tab_step", "tab_done", "pad_idx", "padded", "spare"))
        e_row = [sem(f"e_row{i}") for i in range(AT_ONCE)]
        e_sent = [sem(f"e_sent{i}") for i in range(AT_ONCE)]
        e_t, e_hi, e_lo, e_mm, e_ind, e_gate1, e_gate, e_y = (
            sem("e_" + n) for n in ("t", "hi", "lo", "mm", "ind", "gate1", "gate", "y"))
        added1, added2 = ([sem(f"added{k}_{i}") for i in range(2)] for k in (1, 2))
        final1 = [sem(f"final{i}") for i in range(B)]
        b_kv, b_ks, b_v, b_kc, b_q, b_sq, b_qc, b_qs, b_u, b_ut, b_outer, b_kvm = (
            sem("b_" + n) for n in ("kv", "ks", "v", "kc", "q", "sq", "qc", "qs", "u", "ut", "outer", "kvm"))
        b_o, b_ost, b_omv, b_oadd, b_ors, b_on, b_ot, b_ona, b_z, b_out, b_x3 = (
            sem("b_" + n) for n in ("o", "ost", "omv", "oadd", "ors", "on", "ot", "ona", "z", "out", "x3"))
        stored = sem("stored")

        LN_A, LN_B = 0, 1

        def after_first(b):
            return not isinstance(b, int) or b > 0

        wait_value = [nc.vector.alloc_register("wait_value"), nc.gpsimd.alloc_register("wait_value")]

        def wait_apart(engine, semaphore, value):
            if not isinstance(value, int):
                engine.reg_mov(wait_value[engine is nc.gpsimd], value)
                value = wait_value[engine is nc.gpsimd]
            engine.wait_ge(fills_p if engine is nc.gpsimd else fills_v, 2)
            engine.wait_ge(semaphore, value)

        def mm3(pe, acc, pairs, more=False):
            n = len(pairs)
            for i, (ah, al, bh, bl) in enumerate(pairs):
                pe.matmul(acc, ah, bh, start=(i == 0), stop=False)
                pe.matmul(acc, ah, bl, start=False, stop=False)
                last = pe.matmul(acc, al, bh, start=False, stop=(i == n - 1 and not more))
            return last

        def row(name):
            return rows[:, slice(*ROWS[name])]

        def two_tiles(b, h):
            return X[:, bass.ds(b * T + 2 * h, 2), :]

        def bank2(bank):
            return bank.rearrange("p (t d) -> p t d", t=2)

        block = ctx.enter_context(nc.Block())

        @block.sync
        def _(sp):
            xt = x.rearrange("b (t p) d -> p (b t) d", p=P)
            ot = out.rearrange("b (t p) d -> p (b t) d", p=P)
            sp.dma_start(X[:, 0:T, :], xt[:, 0:T, :]).then_inc(ld_x0, 16)
            sp.dma_start(con[:, :], consts).then_inc(ld_con, 16)
            sp.dma_start(par[:, :], params).then_inc(ld_par, 16)
            sp.dma_start(X[:, T:, :], xt[:, T:, :]).then_inc(ld_x, 16)
            sp.dma_start(wout_s[:], wout.rearrange("(m p) n -> p m n", p=P)).then_inc(ld_wout, 16)
            sp.dma_start(wo_s[:], wo.rearrange("(k p) n -> p k n", p=P)).then_inc(ld_wo, 16)
            for e in range(NE):
                if e >= 2:
                    sp.wait_ge(we_lo, e - 1)
                sp.dma_start(we_raw[e % 2], we.rearrange("(k p) n -> p k n", p=P)[:, :, e * D:(e + 1) * D]).then_inc(ld_we[e % 2], 16)
            sp.wait_ge(we_lo, NE)
            sp.dma_start(be_raw, be2).then_inc(ld_be, 16)

            pairs_read = sp.alloc_register("pairs_read")

            def round_rows(i, f):
                g = f * ROUNDS + i
                for j in range(PAIRS):
                    two = sp.value_load(RP[0:1, bass.ds(i * PAIRS + j, 1)], min_val=0, max_val=(1 << 18) - 1)
                    used = f or after_first(i)
                    if used:
                        sp.reg_mov(pairs_read, (g - 1) * PAIRS + j + 1)
                    for v in range(2):
                        first = sp.snap(nc.s_assert_within(((two >> 9) if v else two) & 511, 0, NE * ROOM + NE - 1,
                                                           skip_runtime_bounds_check_because="the table has no other tiles") * P)
                        if used:
                            sp.wait_ge(tab_done, f + 1)
                            sp.wait_ge(e_t, pairs_read)
                            sp.wait_ge(e_gate, pairs_read)
                        s = 2 * j + v
                        sp.dma_start(XR[:, s, :], slots[bass.ds(first, P), :]).then_inc(e_row[s], 16)

            for f in range(2):
                sp.wait_ge(tab_done, f + 1)
                for parity in range(2):
                    sp.wait_ge(r_scattered[parity], 16 * 2 * T * (B // 2) * (f + 1))
                sp.wait_ge(padded, 16 * NE * (f + 1))
                if f == 0:
                    sp.wait_ge(spare, 16)
                    sp.wait_ge(a_y, B * MI)
                    round_rows(0, 0)
                    with sp.Fori(1, ROUNDS) as i:
                        round_rows(i, 0)
                else:
                    sp.wait_ge(b_z, B * KD)
                    with sp.Fori(0, ROUNDS) as i:
                        round_rows(i, 1)
            for b in range(B):
                sp.wait_ge(final1[b], 32)
                sp.dma_start(ot[:, b * T:(b + 1) * T, :], X[:, b * T:(b + 1) * T, :]).then_inc(stored, 16)
            sp.wait_ge(stored, 16 * B)

        @block.tensor
        def _(pe):
            def transposes(b, p):
                q = p * B + b
                pe.wait_ge(xn_done, q + 1)
                if p or after_first(b):
                    pe.wait_ge(lo_done, q * KD)
                for c in range(KD):
                    for t in range(T):
                        last = pe.transpose(TB[c][:, t * P:(t + 1) * P], XN[:, t, c * P:(c + 1) * P], ident)
                    last.then_inc(t_done, 1)

            def win_products(b):
                pe.wait_ge(lo_done, b * KD + KD)
                for m in range(MI):
                    if after_first(b) or m >= 2:
                        pe.wait_ge(a_silu, b * MI + m - 1)
                    mm3(pe, GB[m % 2], [(win_h[:, k, m * P:(m + 1) * P], win_l[:, k, m * P:(m + 1) * P],
                                     XH[:, k, :], XL[:, k, :]) for k in range(KD)]).then_inc(a_win, 1)

            def wout_products(b, y, h):
                if h == 0:
                    pe.wait_ge(a_y, b * MI + MI)
                if after_first(b):
                    pe.wait_ge(a_x1, (b - 1) * 2 + h + 1)
                for t in (2 * h, 2 * h + 1):
                    acc = GB[4 + h][:, (t % 2) * D:(t % 2 + 1) * D]
                    for m in range(MI):
                        pe.matmul(acc, y[:, m, t * P:(t + 1) * P], wout_s[:, m, :], start=(m == 0), stop=False)
                    last = pe.matmul(acc, ones2[:, :], row("bout"), start=False, stop=True)
                last.then_inc(a_out, 1)

            def route_transposes(b, f, parity):
                r = f * B + b
                pe.wait_ge(r_xn, r + 1)
                if f or after_first(b):
                    pe.wait_ge(r_next, r)
                    pe.wait_ge(r_logit, r)
                for c in range(KD):
                    for t in range(T):
                        last = pe.transpose(GB[2 + c][:, t * P:(t + 1) * P], XNR[parity][:, t, c * P:(c + 1) * P], ident)
                    last.then_inc(r_t, 1)

            def route_logits(b, f):
                r = f * B + b
                pe.wait_ge(r_xt, r * KD + KD)
                for t in range(T):
                    for k in range(KD):
                        last = pe.matmul(GB[2][:, t * NE:(t + 1) * NE], XT[:, k, t * P:(t + 1) * P],
                                         wg_s[:, k * NE:(k + 1) * NE], start=(k == 0), stop=(k == KD - 1))
                last.then_inc(r_logit, 1)

            def route_ranks(b, f):
                r = f * B + b
                pe.wait_ge(r_both, r + 1)
                both = BOTH[:].rearrange("p t e -> p (t e)")
                pe.matmul(GB[3][:, 0:T * NE], before[:, :], both, start=True, stop=False)
                for u in range(1, T):
                    pe.matmul(GB[3][:, u * NE:T * NE], ones_b[:, :], both[:, 0:(T - u) * NE], start=False, stop=(u == T - 1))
                for u in range(T):
                    last = pe.matmul(GB[3][:, T * NE:(T + 1) * NE], ones_b[:, :], both[:, u * NE:(u + 1) * NE],
                                     start=(u == 0), stop=(u == T - 1))
                last.then_inc(r_rank, 1)

            def a_body(b, parity, has1, has2, routes, ranks):
                if has1:
                    win_products(b + 1)
                if ranks:
                    route_ranks(b - 2, 0)
                if has2:
                    transposes(b + 2, LN_A)
                wout_products(b, Y[parity], 0)
                if routes:
                    route_transposes(b - 1, 0, 1 - parity)
                wout_products(b, Y[parity], 1)
                if routes:
                    route_logits(b - 1, 0)

            pe.wait_ge(ld_con, 16)
            transposes(0, LN_A)
            pe.wait_ge(win_lo, 1)
            win_products(0)
            transposes(1, LN_A)
            pe.wait_ge(ld_wout, 16)
            pe.wait_ge(rows_done, 1)
            pe.wait_ge(rows_hi, 2)
            pe.wait_ge(before_done, 1)
            a_body(0, 0, True, True, False, False)
            a_body(1, 1, True, True, True, False)
            a_body(2, 0, True, True, True, True)
            with pe.Fori(1, (B - 4) // 2) as i:
                a_body(i * 2 + 1, 1, True, True, True, True)
                a_body(i * 2 + 2, 0, True, True, True, True)
            a_body(B - 3, 1, True, True, True, True)
            a_body(B - 2, 0, True, False, True, True)
            a_body(B - 1, 1, False, False, True, True)
            route_ranks(B - 2, 0)
            route_transposes(B - 1, 0, 1)
            route_logits(B - 1, 0)
            route_ranks(B - 1, 0)

            def slot_transposes(g, j):
                for v in range(2):
                    pe.wait_ge(e_row[2 * j + v], g * 16 + 16)
                if after_first(g):
                    pe.wait_ge(e_lo, (g - 1) * PAIRS + j + 1)
                for v in range(2):
                    for c in range(KD):
                        at = (v * KD + c) * P
                        last = pe.transpose(ET4[j][:, at:at + P], XR[:, 2 * j + v, c * P:(c + 1) * P], ident)
                last.then_inc(e_t, 1)

            def slot_products(g, j, choices):
                pe.wait_ge(e_lo, g * PAIRS + j + 1)
                if after_first(g):
                    pe.wait_ge(e_y, (g - 1) * AT_ONCE + 2 * j + 2)
                for v in range(2):
                    out_ = GB[j][:, v * D:(v + 1) * D]
                    first = pe.snap(((choices >> (3 * (2 * j + v))) & 7) * D, min_val=0, max_val=(NE - 1) * D)
                    for k in range(KD):
                        at = (v * KD + k) * P
                        high, low = EXH[j][:, at:at + P], EXL[j][:, at:at + P]
                        pe.matmul(out_, high, we_h[:, k, bass.ds(first, D)], start=(k == 0), stop=False)
                        pe.matmul(out_, high, we_l[:, k, bass.ds(first, D)], start=False, stop=False)
                        pe.matmul(out_, low, we_h[:, k, bass.ds(first, D)], start=False, stop=False)
                    last = pe.matmul(out_, ones2[:, :], be_rows[:, bass.ds(first, D)], start=False, stop=True)
                last.then_inc(e_mm, 1)

            def round_(i, f, more):
                g = f * ROUNDS + i
                choices = pe.value_load(EP[0:1, bass.ds(i, 1)], min_val=0, max_val=(1 << 3 * AT_ONCE) - 1)
                for j in range(PAIRS):
                    if j + 2 < PAIRS:
                        slot_transposes(g, j + 2)
                    elif more:
                        slot_transposes(g + 1, j + 2 - PAIRS)
                    slot_products(g, j, choices)

            def experts(f):
                pe.wait_ge(tab_done, f + 1)
                pe.wait_ge(r_next, (f + 1) * B)
                slot_transposes(f * ROUNDS, 0)
                slot_transposes(f * ROUNDS, 1)
                round_(0, f, True)
                with pe.Fori(1, ROUNDS - 1) as i:
                    round_(i, f, True)
                round_(ROUNDS - 1, f, False)

            pe.wait_ge(a_silu, B * MI)
            pe.wait_ge(lo_done, B * KD)
            pe.wait_ge(a_x1, B * 2)
            pe.wait_ge(we_lo, B)
            pe.wait_ge(rows_done, 2)
            experts(0)

            pe.wait_ge(trig_done, 2 * KD)
            pe.wait_ge(e_lo, TILES // 2)
            for i, tab in enumerate((cosT, sinT)):
                if i:
                    pe.wait_ge(trig_n, 2)
                for t in range(T):
                    for c in range(KD):
                        last = pe.transpose(TB[t // 2][:, (t % 2) * D + c * P:(t % 2) * D + (c + 1) * P],
                                            tab[:, c, t * P:(t + 1) * P], ident)
                    if t % 2:
                        last.then_inc(trig_t, 1)
            pe.wait_ge(trig_n, 4)

            def kv_products(b, tiles):
                for t in tiles:
                    n = b * T + t
                    if t >= 2:
                        pe.wait_ge(b_v, n - 1)
                    elif after_first(b):
                        pe.wait_ge(b_ut, (b - 1) * KD + t + 1)
                    mm3(pe, GB[t % 2], [(XH[:, k, t * P:(t + 1) * P], XL[:, k, t * P:(t + 1) * P],
                                         wq_h[:, k, D:3 * D], wq_l[:, k, D:3 * D]) for k in range(KD)], more=True)
                    pe.matmul(GB[t % 2], ones2[:, :], row("bkv"), start=False, stop=True).then_inc(b_kv, 1)

            def feature_products(b, first_col, done):
                for m in range(KD):
                    if first_col:
                        pe.wait_ge(b_sq, b * KD + m + 1)
                    else:
                        pe.wait_ge(b_v, b * T + m + 3)
                    col = first_col + m * P
                    mm3(pe, GB[m], [(wq_h[:, k, col:col + P], wq_l[:, k, col:col + P], XH[:, k, :], XL[:, k, :])
                                    for k in range(KD)]).then_inc(done, 1)

            def q_products(b):
                feature_products(b, 0, b_q)

            def u_products(b):
                feature_products(b, 3 * D, b_u)

            def outer_products(b):
                pe.wait_ge(b_v, b * T + T)
                pe.wait_ge(b_kc, b * 4 + 4)
                if after_first(b):
                    pe.wait_ge(b_x3, b * 2)
                for c in range(KD):
                    for s, kk in enumerate((KC, KSN)):
                        g = 2 * c + s
                        for t in range(T):
                            last = pe.matmul(GB[5][:, g * P:(g + 1) * P], kk[:, t, c * P:(c + 1) * P],
                                             V[:, t, c * P:(c + 1) * P], start=(t == 0), stop=(t == T - 1))
                last.then_inc(b_outer, 1)

            def attend(b):
                pe.wait_ge(b_kvm, b + 1)
                pe.wait_ge(b_qc, b * KD + KD)
                pe.wait_ge(b_qs, b * KD + KD)
                for h in range(2):
                    for t in (2 * h, 2 * h + 1):
                        for c in range(KD):
                            at = (t % 2) * D + c * P
                            for s, qq in enumerate((QC, QS)):
                                last = pe.matmul(GB[4 + h][:, at:at + P], qq[:, c, t * P:(t + 1) * P],
                                                 KVM[:, 2 * c + s, :], start=(s == 0), stop=(s == 1))
                    last.then_inc(b_o, 1)

            def out_transposes(b, has1):
                pe.wait_ge(b_on, b + 1)
                pe.wait_ge(lo_done, (LN_B * B + b + (2 if has1 else 1)) * KD)
                for c in range(KD):
                    for t in range(T):
                        last = pe.transpose(TB[c][:, t * P:(t + 1) * P], ON[:, t, c * P:(c + 1) * P], ident)
                    last.then_inc(b_ot, 1)

            def out_products(b):
                pe.wait_ge(b_z, b * KD + KD)
                for h in range(2):
                    for t in (2 * h, 2 * h + 1):
                        acc = GB[4 + h][:, (t % 2) * D:(t % 2 + 1) * D]
                        for c in range(KD):
                            pe.matmul(acc, ZT[:, c, t * P:(t + 1) * P], wo_s[:, c, :], start=(c == 0), stop=False)
                        last = pe.matmul(acc, ones2[:, :], row("bo"), start=False, stop=True)
                    last.then_inc(b_out, 1)

            def b_body(b, parity, has1, has2, routes, ranks):
                if has1:
                    pe.wait_ge(lo_done, (LN_B * B + b + 2) * KD)
                    kv_products(b + 1, (0,))
                if ranks:
                    route_ranks(b - 2, 1)
                outer_products(b)
                if has1:
                    kv_products(b + 1, (1,))
                attend(b)
                if has1:
                    kv_products(b + 1, (2, 3))
                    q_products(b + 1)
                out_transposes(b, has1)
                if has1:
                    u_products(b + 1)
                if routes:
                    route_transposes(b - 1, 1, 1 - parity)
                if has2:
                    pe.wait_ge(b_ona, b * KD + KD)
                    transposes(b + 2, LN_B)
                if routes:
                    route_logits(b - 1, 1)
                out_products(b)

            pe.wait_ge(e_y, TILES)
            pe.wait_ge(wq_lo, 2)
            pe.wait_ge(ld_wo, 16)
            transposes(0, LN_B)
            pe.wait_ge(lo_done, (LN_B * B + 1) * KD)
            kv_products(0, range(T))
            q_products(0)
            u_products(0)
            transposes(1, LN_B)
            b_body(0, 0, True, True, False, False)
            b_body(1, 1, True, True, True, False)
            b_body(2, 0, True, True, True, True)
            with pe.Fori(1, (B - 4) // 2) as i:
                b_body(i * 2 + 1, 1, True, True, True, True)
                b_body(i * 2 + 2, 0, True, True, True, True)
            b_body(B - 3, 1, True, True, True, True)
            b_body(B - 2, 0, True, False, True, True)
            b_body(B - 1, 1, False, False, True, True)
            route_ranks(B - 2, 1)
            pe.wait_ge(b_x3, B * 2)
            pe.wait_ge(b_ona, B * KD)
            pe.wait_ge(b_ut, B * KD)
            route_transposes(B - 1, 1, 1)
            route_logits(B - 1, 1)
            route_ranks(B - 1, 1)
            experts(1)

        @block.scalar
        def _(act):
            def high_part(b, p, free, count):
                q = p * B + b
                if free is not None:
                    act.wait_ge(free, count)
                for c in range(KD):
                    act.wait_ge(t_done, q * KD + c + 1)
                    act.activation(XH[:, c, :], TB[c], ACT.Copy).then_inc(hi_done, 1)

            act.dma_start(win_raw, win.rearrange("(k p) n -> p k n", p=P)).then_inc(ld_win, 16)
            for k in range(KD):
                act.dma_start(wq_raw[k], wqkvu[k * P:(k + 1) * P, :]).then_inc(ld_wq[k], 16)
            act.dma_start(rows_raw, rows2).then_inc(ld_rows, 16)

            def route_copies(b, f):
                for c in range(KD):
                    act.wait_ge(r_t, (f * B + b) * KD + c + 1)
                    act.activation(XT[:, c, :], GB[2 + c], ACT.Copy).then_inc(r_xt, 1)

            def route_columns(b, f, parity):
                act.wait_ge(r_gap, f * B + b + 1)
                act.activation(XNR[parity][:, :, R_DW], GAP[:, :], ACT.Tanh, scale=0.5)
                act.activation(XNR[parity][:, :, R_TO], place[:, bass.ds(b * T, T)], ACT.Copy).then_inc(r_cols, 1)

            def silu(b, m):
                act.wait_ge(a_win, b * MI + m + 1)
                if after_first(b):
                    act.wait_ge(a_y, (b - 1) * MI + m + 1)
                act.activation(XI[:, m, :], GB[m % 2], ACT.Silu, bias=bin_s[:, m:m + 1]).then_inc(a_silu, 1)

            def scaled(b, m):
                act.wait_ge(a_silu, b * MI + m + 1)
                act.mul(XG[:, m, :], XI[:, m, :], g_s[:, m:m + 1]).then_inc(a_xg, 1)

            def inner(b, between=None):
                silu(b, 0)
                for m in range(1, MI):
                    silu(b, m)
                    scaled(b, m - 1)
                    if m == 1 and between:
                        between()
                scaled(b, MI - 1)

            def we_high(e, ring, count):
                act.wait_ge(ld_we[ring], count * 16)
                act.activation(we_h[:, :, bass.ds(e * D, D)], we_raw[ring], ACT.Copy).then_inc(we_hi, 1)

            def a_body(b, parity, has1, has2, routes, ranks, turn_):
                if has1:
                    inner(b + 1, (lambda: route_columns(b - 2, 0, parity)) if ranks else None)
                elif ranks:
                    route_columns(b - 2, 0, parity)
                if has2:
                    high_part(b + 2, LN_A, a_win, (b + 2) * MI)
                if routes:
                    route_copies(b - 1, 0)
                we_high(b, parity, turn_)

            act.wait_ge(ld_win, 16)
            act.activation(win_h[:], win_raw, ACT.Copy).then_inc(win_hi, 1)
            high_part(0, LN_A, None, 0)
            act.wait_ge(ld_par, 16)
            act.wait_ge(g_done, 1)
            inner(0)
            act.wait_ge(ld_rows, 16)
            act.activation(rows[:, :], rows_raw, ACT.Copy).then_inc(rows_hi, 1)
            act.wait_ge(fills_p, 2)
            act.activation(ones2[:, :], ones_f[:, :], ACT.Copy).then_inc(rows_hi, 1)
            act.wait_ge(ld_con, 16)
            act.activation(before[:, :], con[:, slice(*CON["before"])], ACT.Copy).then_inc(before_done, 1)
            high_part(1, LN_A, a_win, MI)
            for k in range(KD):
                act.wait_ge(ld_wq[k], 16)
                act.activation(wq_h[:, k, :], wq_raw[k], ACT.Copy).then_inc(wq_hi, 1)
            a_body(0, 0, True, True, False, False, 1)
            a_body(1, 1, True, True, True, False, 1)
            a_body(2, 0, True, True, True, True, 2)
            with act.Fori(1, (B - 4) // 2) as i:
                a_body(i * 2 + 1, 1, True, True, True, True, i + 1)
                a_body(i * 2 + 2, 0, True, True, True, True, i + 2)
            a_body(B - 3, 1, True, True, True, True, (B - 2) // 2)
            a_body(B - 2, 0, True, False, True, True, B // 2)
            a_body(B - 1, 1, False, False, True, True, B // 2)
            route_columns(B - 2, 0, 0)
            route_copies(B - 1, 0)
            route_columns(B - 1, 0, 1)

            act.wait_ge(ld_be, 16)
            act.activation(be_rows[:, :], be_raw, ACT.Copy).then_inc(rows_hi, 1)
            act.wait_ge(arg_done, 1)
            for s, tab in enumerate((sinT, cosT)):
                for c in range(KD):
                    act.activation(tab[:, c, :], turn[:, s * KD + c, :], ACT.Sin).then_inc(trig_done, 1)

            def slot_high(g, j):
                act.wait_ge(e_t, g * PAIRS + j + 1)
                if after_first(g):
                    act.wait_ge(e_mm, (g - 1) * PAIRS + j + 1)
                act.activation(EXH[j], ET4[j], ACT.Copy).then_inc(e_hi, 1)

            def slot_outputs(g, j):
                act.wait_ge(e_mm, g * PAIRS + j + 1)
                act.wait_ge(e_gate, g * PAIRS + j + 1)
                for v in range(2):
                    s = 2 * j + v
                    if after_first(g):
                        act.wait_ge(e_sent[s], g * 16)
                    act.mul(YO[:, s, :], GB[j][:, v * D:(v + 1) * D], GW[:, s:s + 1]).then_inc(e_y, 1)

            def round_(i, f, more):
                g = f * ROUNDS + i
                for j in range(PAIRS):
                    if j + 2 < PAIRS:
                        slot_high(g, j + 2)
                    elif more:
                        slot_high(g + 1, j + 2 - PAIRS)
                    slot_outputs(g, j)

            def experts(f):
                slot_high(f * ROUNDS, 0)
                slot_high(f * ROUNDS, 1)
                round_(0, f, True)
                with act.Fori(1, ROUNDS - 1) as i:
                    round_(i, f, True)
                round_(ROUNDS - 1, f, False)

            experts(0)

            act.wait_ge(wq_lo, 2)
            for i, tab in enumerate((cosN, sinN)):
                for h in range(2):
                    act.wait_ge(trig_t, 2 * i + h + 1)
                    act.activation(tab[:, 2 * h:2 * h + 2, :], bank2(TB[h]), ACT.Copy).then_inc(trig_n, 1)

            def kv_parts(b, tiles):
                for t in tiles:
                    act.wait_ge(b_kv, b * T + t + 1)
                    if after_first(b):
                        act.wait_ge(b_kc, b * 4)
                        act.wait_ge(b_outer, b)
                    act.activation(KS[:, t, :], GB[t % 2][:, 0:D], ACT.Silu).then_inc(b_ks, 1)
                    act.activation(V[:, t, :], GB[t % 2][:, D:2 * D], ACT.Copy).then_inc(b_v, 1)

            def q_part(b):
                for m in range(KD):
                    act.wait_ge(b_q, b * KD + m + 1)
                    if after_first(b):
                        act.wait_ge(b_qc, b * KD)
                        act.wait_ge(b_qs, b * KD)
                    act.activation(SQ[:, m, :], GB[m], ACT.Silu, bias=bq_s[:, m:m + 1]).then_inc(b_sq, 1)

            def u_part(b):
                for m in range(KD):
                    act.wait_ge(b_u, b * KD + m + 1)
                    if after_first(b):
                        act.wait_ge(b_z, b * KD)
                    act.activation(UT[:, m, :], GB[m], ACT.Identity, bias=bu_s[:, m:m + 1]).then_inc(b_ut, 1)

            def affine(b):
                for c in range(KD):
                    act.wait_ge(b_ot, b * KD + c + 1)
                    if after_first(b):
                        act.wait_ge(b_z, b * KD)
                    act.activation(ONA[:, c, :], TB[c], ACT.Identity, scale=lnw_s[:, c:c + 1],
                                   bias=lnb_s[:, c:c + 1]).then_inc(b_ona, 1)

            def b_body(b, parity, has1, has2, routes, ranks):
                if ranks:
                    route_columns(b - 2, 1, parity)
                if has1:
                    kv_parts(b + 1, range(T))
                    q_part(b + 1)
                affine(b)
                if has1:
                    u_part(b + 1)
                if routes:
                    route_copies(b - 1, 1)
                if has2:
                    high_part(b + 2, LN_B, b_u, (b + 2) * KD)

            high_part(0, LN_B, None, 0)
            kv_parts(0, range(T))
            q_part(0)
            u_part(0)
            high_part(1, LN_B, b_u, KD)
            b_body(0, 0, True, True, False, False)
            b_body(1, 1, True, True, True, False)
            b_body(2, 0, True, True, True, True)
            with act.Fori(1, (B - 4) // 2) as i:
                b_body(i * 2 + 1, 1, True, True, True, True)
                b_body(i * 2 + 2, 0, True, True, True, True)
            b_body(B - 3, 1, True, True, True, True)
            b_body(B - 2, 0, True, False, True, True)
            b_body(B - 1, 1, False, False, True, True)
            route_columns(B - 2, 1, 0)
            route_copies(B - 1, 1)
            route_columns(B - 1, 1, 1)
            experts(1)

        @block.gpsimd
        def _(pool):
            def inv_std(b, p):
                q = p * B + b
                wait_apart(pool, mv_done, q + 1)
                pool.tensor_scalar(veps[:, :], mv[:, :, 1], EPS, None, ALU.add).then_inc(rs_add, 1)
                pool.wait_ge(rs_add, q + 1)
                pool.tensor_tensor(rstd[:, :], veps[:, :], minus_half[:, :], ALU.pow).then_inc(rs_done, 1)

            def route_inv_std(b, f):
                r = f * B + b
                wait_apart(pool, r_mv, r + 1)
                pool.tensor_scalar(rveps[:, :], rmv[:, :, 1], EPS, None, ALU.add).then_inc(r_add, 1)
                pool.wait_ge(r_add, r + 1)
                pool.tensor_tensor(rrstd[:, :], rveps[:, :], minus_half[:, :], ALU.pow).then_inc(r_rs, 1)

            def scatter(b, f, parity):
                count = f * B + b + 1
                if not isinstance(count, int):
                    count = pool.snap(count)
                pool.wait_ge(r_idx, count)
                pool.wait_ge(r_cols, count)
                for t in range(T):
                    for k in range(2):
                        j = 2 * t + k
                        pool.indirect_dma_start(out=slots, out_offset=bass.IndirectOffsetOnAxis(ap=IDX[parity][:, j:j + 1], axis=0),
                                                in_=XNR[parity][:, t, :], in_offset=None).then_inc(r_scattered[parity], 16)

            def we_low(e, ring):
                pool.wait_ge(we_hi, e + 1)
                cols = bass.ds(e * D, D)
                pool.tensor_tensor(we_l[:, :, cols], we_raw[ring], we_h[:, :, cols].bitcast(F32), ALU.subtract).then_inc(we_lo, 1)

            def pad_slots(f):
                pool.wait_ge(pad_idx, f + 1)
                for e in range(NE):
                    pool.indirect_dma_start(out=slots, out_offset=bass.IndirectOffsetOnAxis(ap=PADI[:, e:e + 1], axis=0),
                                            in_=PAD[:, :], in_offset=None).then_inc(padded, 16)

            def a_body(b, parity, routes, routed, has3):
                if routes:
                    route_inv_std(b - 1, 0)
                if routed:
                    scatter(b - 2, 0, parity)
                we_low(b, parity)
                if has3:
                    inv_std(b + 3, LN_A)

            def finish_routing(f):
                route_inv_std(B - 1, f)
                scatter(B - 2, f, 0)
                scatter(B - 1, f, 1)
                pad_slots(f)

            pool.memset(minus_half[:, :], -0.5).then_inc(fills_p, 1)
            pool.memset(ones_f[:, :], 1.0).then_inc(fills_p, 1)
            pool.memset(ones_b[:, :], 1.0).then_inc(fills_p, 1)
            pool.memset(ones_e[:, :], 1.0).then_inc(fills_p, 1)
            pool.memset(PAD[:, :], 0.0).then_inc(fills_p, 1)
            pool.wait_ge(fills_p, 5)
            pool.memset(PAD[:, R_E1:R_E1 + 1], -1.0).then_inc(fills_p, 1)
            pool.memset(PAD[:, R_TO:R_TO + 1], NOWHERE).then_inc(fills_p, 1)
            pool.wait_ge(fills_p, 7)
            pool.dma_start(slots[NE * ROOM * P:, :].rearrange("(n p) w -> p n w", p=P),
                           PAD[:, :].unsqueeze(1).to_broadcast([P, NE, ROW])).then_inc(spare, 16)
            inv_std(0, LN_A)
            inv_std(1, LN_A)
            inv_std(2, LN_A)
            a_body(0, 0, False, False, True)
            a_body(1, 1, True, False, True)
            a_body(2, 0, True, True, True)
            with pool.Fori(1, (B - 4) // 2) as i:
                a_body(i * 2 + 1, 1, True, True, True)
                a_body(i * 2 + 2, 0, True, True, True)
            a_body(B - 3, 1, True, True, False)
            a_body(B - 2, 0, True, True, False)
            a_body(B - 1, 1, True, True, False)
            finish_routing(0)

            def send(g, s):
                wait_apart(pool, e_y, g * AT_ONCE + s + 1)
                pool.indirect_dma_start(out=chosen, out_offset=bass.IndirectOffsetOnAxis(ap=DEST[:, s:s + 1], axis=0),
                                        in_=YO[:, s, :], in_offset=None, bounds_check=2 * B * L - 1,
                                        oob_is_err=False).then_inc(e_sent[s], 16)

            def experts(f):
                with pool.Fori(0, ROUNDS) as i:
                    for s in range(AT_ONCE):
                        send(i + f * ROUNDS, s)
                for s in range(AT_ONCE):
                    pool.wait_ge(e_sent[s], 16 * ROUNDS * (f + 1))

            experts(0)

            by_choice = chosen.rearrange("(t p k) d -> k p t d", p=P, k=2)

            def add_first(b):
                pool.dma_start(X[:, bass.ds(b * T, T), :], by_choice[1][:, bass.ds(b * T, T), :], accum_op=ALU.add).then_inc(added1[b % 2], 16)

            def add_second(b):
                pool.wait_ge(added1[b % 2], (b // 2 + 1) * 16)
                if b >= 2:
                    pool.wait_ge(added2[b % 2], (b // 2) * 16)
                pool.dma_start(X[:, bass.ds(b * T, T), :], by_choice[0][:, bass.ds(b * T, T), :], accum_op=ALU.add).then_inc(added2[b % 2], 16)

            def q_parts(b):
                for c in range(KD):
                    pool.wait_ge(b_sq, b * KD + c + 1)
                    if after_first(b):
                        pool.wait_ge(b_o, b * 2)
                    pool.tensor_tensor(QS[:, c, :], SQ[:, c, :], sinT[:, c, :], ALU.mult).then_inc(b_qs, 1)

            def out_inv_std(b):
                wait_apart(pool, b_omv, b + 1)
                pool.tensor_scalar(oveps[:, :], omv[:, :, 1], EPS, None, ALU.add).then_inc(b_oadd, 1)
                pool.wait_ge(b_oadd, b + 1)
                pool.tensor_tensor(orstd[:, :], oveps[:, :], minus_half[:, :], ALU.pow).then_inc(b_ors, 1)

            def b_body(b, parity, has1, has3, has4, routes, routed):
                if routed:
                    scatter(b - 2, 1, parity)
                if routes:
                    route_inv_std(b - 1, 1)
                out_inv_std(b)
                if has4:
                    add_first(b + 4)
                if has1:
                    q_parts(b + 1)
                if has4:
                    add_second(b + 4)
                if has3:
                    inv_std(b + 3, LN_B)

            for b in range(4):
                add_first(b)
                if b:
                    add_second(b - 1)
            add_second(3)
            inv_std(0, LN_B)
            inv_std(1, LN_B)
            q_parts(0)
            inv_std(2, LN_B)
            b_body(0, 0, True, True, True, False, False)
            b_body(1, 1, True, True, True, True, False)
            b_body(2, 0, True, True, True, True, True)
            b_body(3, 1, True, True, True, True, True)
            b_body(4, 0, True, True, False, True, True)
            b_body(B - 3, 1, True, False, False, True, True)
            b_body(B - 2, 0, True, False, False, True, True)
            b_body(B - 1, 1, False, False, False, True, True)
            finish_routing(1)

            experts(1)
            for b in range(B):
                pool.dma_start(X[:, b * T:(b + 1) * T, :], by_choice[1][:, b * T:(b + 1) * T, :], accum_op=ALU.add).then_inc(final1[b], 16)
            for b in range(B):
                pool.wait_ge(final1[b], 16)
                pool.dma_start(X[:, b * T:(b + 1) * T, :], by_choice[0][:, b * T:(b + 1) * T, :], accum_op=ALU.add).then_inc(final1[b], 16)

        @block.vector
        def _(dve):
            def moments(b, p, ready=None, count=0):
                q = p * B + b
                if ready is not None:
                    wait_apart(dve, ready, count)
                for t in range(T):
                    last = dve.bn_stats(stats[:, t, :], X[:, bass.ds(b * T + t, 1), :].squeeze(1))
                last.then_inc(st_done, 1)
                wait_apart(dve, st_done, q + 1)
                for t in range(T):
                    last = dve.bn_aggr(mv[:, t, :], stats[:, t, :])
                last.then_inc(mv_done, 1)

            def normalise(b, p):
                q = p * B + b
                dve.wait_ge(rs_done, q + 1)
                if p or after_first(b):
                    dve.wait_ge(t_done, q * KD)
                for t in range(T):
                    last = dve.tensor_scalar(XN[:, t, :], X[:, bass.ds(b * T + t, 1), :].squeeze(1), mv[:, t, 0:1],
                                             rstd[:, t:t + 1], ALU.subtract, ALU.mult)
                last.then_inc(xn_done, 1)

            def low_part(b, p):
                q = p * B + b
                for c in range(KD):
                    dve.wait_ge(hi_done, q * KD + c + 1)
                    dve.tensor_tensor(XL[:, c, :], TB[c], XH[:, c, :].bitcast(F32), ALU.subtract).then_inc(lo_done, 1)

            def scan(b, m):
                dve.wait_ge(a_xg, b * MI + m + 1)
                dve.tensor_tensor_scan(SG[:, m, :], decay[:, :], XG[:, m, :], 0.0, ALU.mult, ALU.add).then_inc(a_scan, 1)

            def channel_out(b, y, m):
                if m == 0 and (not isinstance(b, int) or b >= 2):
                    dve.wait_ge(a_out, (b - 1) * 2)
                dve.wait_ge(a_scan, b * MI + m + 1)
                dve.scalar_tensor_tensor(out=y[:, m, :], in0=XI[:, m, :], scalar=dp_s[:, m:m + 1], in1=SG[:, m, :],
                                         op0=ALU.mult, op1=ALU.add).then_inc(a_y, 1)

            def channels(b, y, between=None):
                scan(b, 0)
                for m in range(1, MI):
                    scan(b, m)
                    channel_out(b, y, m - 1)
                    if m == 2 and between:
                        between()
                channel_out(b, y, MI - 1)

            def a_residual(b):
                for h in range(2):
                    dve.wait_ge(a_out, b * 2 + h + 1)
                    dve.tensor_tensor(two_tiles(b, h), bank2(GB[4 + h]), two_tiles(b, h), ALU.add).then_inc(a_x1, 1)

            def route_moments(b, f):
                r = f * B + b
                wait_apart(dve, (a_x1, b_x3)[f], b * 2 + 2)
                for t in range(T):
                    last = dve.bn_stats(rstats[:, t, :], X[:, bass.ds(b * T + t, 1), :].squeeze(1))
                last.then_inc(r_st, 1)
                wait_apart(dve, r_st, r + 1)
                for t in range(T):
                    last = dve.bn_aggr(rmv[:, t, :], rstats[:, t, :])
                last.then_inc(r_mv, 1)

            def route_normalise(b, f, parity):
                r = f * B + b
                dve.wait_ge(r_rs, r + 1)
                if f or not isinstance(b, int) or b >= 2:
                    dve.wait_ge(r_scattered[parity], (r >> 1) * 2 * T * 16)
                for t in range(T):
                    last = dve.tensor_scalar(XNR[parity][:, t, 0:D], X[:, bass.ds(b * T + t, 1), :].squeeze(1), rmv[:, t, 0:1],
                                             rrstd[:, t:t + 1], ALU.subtract, ALU.mult)
                last.then_inc(r_xn, 1)

            def route_choice(b, f):
                r = f * B + b
                dve.wait_ge(r_logit, r + 1)
                dve.tensor_tensor(LGX[:, :, 0:NE], GB[2][:, 0:T * NE].rearrange("p (t e) -> p t e", t=T),
                                  bg_s.unsqueeze(1).to_broadcast([P, T, NE]), ALU.add).then_inc(r_lg, 1)
                wait_apart(dve, r_lg, r + 1)
                for t in range(T):
                    last = dve.max(M8[:, t, :], LGX[:, t, :])
                last.then_inc(r_m8, 1)
                wait_apart(dve, r_m8, r + 1)
                for t in range(T):
                    last = dve.max_index(MIX[:, t, :], M8[:, t, :], LGX[:, t, :])
                last.then_inc(r_mi, 1)
                if f or after_first(b):
                    dve.wait_ge(r_cols, r)
                dve.tensor_tensor(GAP[:, :], M8[:, :, 0], M8[:, :, 1], ALU.subtract).then_inc(r_gap, 1)
                dve.wait_ge(r_mi, r + 1)
                dve.tensor_copy(EI[:], MIX[:, :, 0:2]).then_inc(r_ei, 1)
                dve.wait_ge(r_ei, r + 1)
                dve.tensor_tensor(MASK[:], expert.unsqueeze(1).unsqueeze(1).to_broadcast([P, T, 2, NE]),
                                  EI[:].unsqueeze(3).to_broadcast([P, T, 2, NE]), ALU.is_equal).then_inc(r_mask, 1)
                dve.wait_ge(r_mask, r + 1)
                dve.tensor_tensor(BOTH[:], MASK[:, :, 0, :], MASK[:, :, 1, :], ALU.add).then_inc(r_both, 1)

            def route_slots(b, f, parity):
                r = f * B + b
                dve.wait_ge(r_rank, r + 1)
                if after_first(b):
                    dve.wait_ge(r_next, r)
                elif f:
                    dve.wait_ge(tab_done, 1)
                dve.tensor_tensor(POS[:], GB[3][:, 0:T * NE].rearrange("p (t e) -> p t e", t=T),
                                  NEXT[:, :].unsqueeze(1).to_broadcast([P, T, NE]), ALU.add).then_inc(r_pos, 1)
                dve.wait_ge(r_pos, r + 1)
                dve.tensor_tensor(NEXT[:, :], NEXT[:, :], GB[3][:, T * NE:(T + 1) * NE], ALU.add).then_inc(r_next, 1)
                dve.tensor_tensor(PICK[:], MASK[:], POS[:].unsqueeze(2).to_broadcast([P, T, 2, NE]), ALU.mult).then_inc(r_pick, 1)
                dve.wait_ge(r_pick, r + 1)
                dve.tensor_reduce(SLOT[:], PICK[:], AX.X, ALU.add).then_inc(r_slot, 1)
                dve.wait_ge(r_cols, r + 1)
                dve.tensor_scalar(XNR[parity][:, :, R_W2], XNR[parity][:, :, R_DW], -0.5, 0.5, ALU.mult, ALU.add)
                dve.tensor_copy(XNR[parity][:, :, R_E1], EI[:, :, 0])
                dve.wait_ge(r_slot, r + 1)
                dve.tensor_copy(IDX[parity][:, :], SLOT[:].rearrange("p t k -> p (t k)")).then_inc(r_idx, 1)

            TABLE_STEPS = 12 + AT_ONCE

            def tile_table(f):
                steps = [f * TABLE_STEPS]

                def step(ins):
                    steps[0] += 1
                    ins.then_inc(tab_step, 1)
                    dve.wait_ge(tab_step, steps[0])

                dve.wait_ge(r_next, (f + 1) * B)
                dve.tensor_scalar(PADI[:, :], NEXT[:, :], lane, None, ALU.add).then_inc(pad_idx, 1)
                step(dve.tensor_tensor(CNT[:, :], NEXT[:, :], first_slot, ALU.subtract))
                step(dve.tensor_scalar(CNT[:, :], CNT[:, :], float(P - 1), 1.0 / P, ALU.add, ALU.mult))
                step(dve.tensor_scalar(CNT[:, :], CNT[:, :], 0.5 / P - 0.5, ROUND, ALU.add, ALU.add))
                step(dve.tensor_scalar(NT[:, :], CNT[:, :], -ROUND, None, ALU.add))
                step(dve.tensor_tensor_scan(CI[:, :], ones_e[:, :], NT[:, :], 0.0, ALU.mult, ALU.add))
                step(dve.tensor_tensor(CMP, tile.unsqueeze(2).to_broadcast([P, TILES, NE]),
                                       CI[:, :].unsqueeze(1).to_broadcast([P, TILES, NE]), ALU.is_ge))
                step(dve.tensor_reduce(ET[:, :], CMP, AX.X, ALU.add))
                step(dve.tensor_tensor(CMP, CMP, NT[:, :].unsqueeze(1).to_broadcast([P, TILES, NE]), ALU.mult))
                step(dve.tensor_reduce(SKIP[:, :], CMP, AX.X, ALU.add))
                step(dve.tensor_tensor(RT[:, :], tile, SKIP[:, :], ALU.subtract))
                step(dve.scalar_tensor_tensor(out=RT[:, :], in0=ET[:, :], scalar=float(ROOM), in1=RT[:, :],
                                              op0=ALU.mult, op1=ALU.add))
                step(dve.tensor_scalar(EC[:, :], ET[:, :], float(NE - 1), None, ALU.min))
                two = RT[0:1, :].rearrange("p (n v) -> p n v", v=2)
                step(dve.scalar_tensor_tensor(out=RP_f[:, :], in0=two[:, :, 1], scalar=512.0, in1=two[:, :, 0],
                                              op0=ALU.mult, op1=ALU.add))
                each = EC[0:1, :].rearrange("p (n v) -> p n v", v=AT_ONCE)
                step(dve.scalar_tensor_tensor(out=EP_f[:, :], in0=each[:, :, AT_ONCE - 1], scalar=8.0, in1=each[:, :, AT_ONCE - 2],
                                              op0=ALU.mult, op1=ALU.add))
                for v in range(AT_ONCE - 3, -1, -1):
                    step(dve.scalar_tensor_tensor(out=EP_f[:, :], in0=EP_f[:, :], scalar=8.0, in1=each[:, :, v],
                                                  op0=ALU.mult, op1=ALU.add))
                assert steps[0] == (f + 1) * TABLE_STEPS
                dve.tensor_copy(NEXT[:, :], first_slot)
                dve.tensor_copy(RP[:, :], RP_f[:, :])
                dve.tensor_copy(EP[:, :], EP_f[:, :]).then_inc(tab_done, 1)

            def a_body(b, parity, has1, has2, has3, routes, ranks):
                if routes:
                    route_moments(b - 1, 0)
                if has2:
                    normalise(b + 2, LN_A)
                if ranks:
                    route_slots(b - 2, 0, parity)
                if has1:
                    channels(b + 1, Y[1 - parity], (lambda: route_normalise(b - 1, 0, 1 - parity)) if routes else None)
                elif routes:
                    route_normalise(b - 1, 0, 1 - parity)
                if has2:
                    low_part(b + 2, LN_A)
                if has3:
                    moments(b + 3, LN_A)
                a_residual(b)
                if routes:
                    route_choice(b - 1, 0)

            def finish_routing(f):
                route_moments(B - 1, f)
                route_slots(B - 2, f, 0)
                route_normalise(B - 1, f, 1)
                route_choice(B - 1, f)
                route_slots(B - 1, f, 1)
                tile_table(f)

            dve.memset(decay[:, :], DECAY).then_inc(fills_v, 1)
            dve.memset(LGX[:], SENTINEL).then_inc(fills_v, 1)
            dve.wait_ge(fills_v, 2)
            dve.wait_ge(ld_x0, 16)
            moments(0, LN_A)
            dve.wait_ge(ld_par, 16)
            dve.tensor_tensor(bc_s[:, :], par[:, slice(*PAR["bp"])], par[:, slice(*PAR["cp"])], ALU.mult).then_inc(bc_done, 1)
            normalise(0, LN_A)
            dve.wait_ge(win_hi, 1)
            dve.tensor_tensor(win_l[:], win_raw, win_h[:].bitcast(F32), ALU.subtract).then_inc(win_lo, 1)
            low_part(0, LN_A)
            dve.wait_ge(bc_done, 1)
            dve.tensor_reduce(g_s[:, :], bc_s[:, :].rearrange("p (m s) -> p m s", m=MI), AX.X, ALU.add).then_inc(g_done, 1)
            dve.wait_ge(ld_x, 16)
            moments(1, LN_A)
            normalise(1, LN_A)
            channels(0, Y[0])

            def split_rows(n, whole_rows, raw):
                dve.wait_ge(rows_hi, (1, 3)[n])
                dve.tensor_scalar(raw, raw, con[0:2, sel2:sel2 + 1], None, ALU.mult).then_inc(rows_a, 1)
                dve.wait_ge(rows_a, n + 1)
                dve.scalar_tensor_tensor(out=whole_rows[:, :], in0=whole_rows[:, :].bitcast(F32), scalar=con[0:2, sel2 + 1:sel2 + 2],
                                         in1=raw, op0=ALU.mult, op1=ALU.add).then_inc(rows_done, 1)

            dve.wait_ge(ld_con, 16)
            split_rows(0, rows, rows_raw)
            dve.tensor_copy(NEXT[:, :], first_slot).then_inc(fills_v, 1)
            low_part(1, LN_A)
            for k in range(KD):
                dve.wait_ge(wq_hi, k + 1)
                dve.tensor_tensor(wq_l[:, k, :], wq_raw[k], wq_h[:, k, :].bitcast(F32), ALU.subtract).then_inc(wq_lo, 1)
            moments(2, LN_A)
            dve.wait_ge(fills_v, 3)
            a_body(0, 0, True, True, True, False, False)
            a_body(1, 1, True, True, True, True, False)
            a_body(2, 0, True, True, True, True, True)
            with dve.Fori(1, (B - 4) // 2) as i:
                a_body(i * 2 + 1, 1, True, True, True, True, True)
                a_body(i * 2 + 2, 0, True, True, True, True, True)
            a_body(B - 3, 1, True, True, False, True, True)
            a_body(B - 2, 0, True, False, False, True, True)
            a_body(B - 1, 1, False, False, False, True, True)
            finish_routing(0)
            split_rows(1, be_rows, be_raw)

            def trig_arguments():
                steps = [0]

                def step(ins):
                    steps[0] += 1
                    ins.then_inc(arg_step, 1)

                def settle():
                    dve.wait_ge(arg_step, steps[0])

                for c in range(KD):
                    step(dve.tensor_scalar(th[:, c, :], pos, theta_s[:, c:c + 1], None, ALU.mult))
                settle()
                step(dve.tensor_scalar(whole[:, 0:KD, :], th, INV_TWO_PI, ROUND, ALU.mult, ALU.add))
                step(dve.tensor_scalar(turn[:, KD:, :], th, INV_TWO_PI, 0.25, ALU.mult, ALU.add))
                settle()
                step(dve.tensor_scalar(whole[:, KD:, :], turn[:, KD:, :], ROUND, None, ALU.add))
                settle()
                step(dve.tensor_scalar(whole, whole, -ROUND, None, ALU.add))
                settle()
                for s in range(2):
                    mine = slice(s * KD, (s + 1) * KD)
                    for i, of_2pi in enumerate((TWO_PI_1, TWO_PI_2, TWO_PI_3)):
                        step(dve.scalar_tensor_tensor(out=turn[:, mine, :], in0=whole[:, mine, :], scalar=-of_2pi,
                                                      in1=th if i == 0 else turn[:, mine, :], op0=ALU.mult, op1=ALU.add))
                        settle()
                step(dve.tensor_scalar(turn[:, KD:, :], turn[:, KD:, :], float(np.pi / 2), None, ALU.add))
                settle()
                dve.tensor_scalar(turn, turn, PI_BELOW, -PI_BELOW, ALU.min, ALU.max).then_inc(arg_done, 1)

            trig_arguments()

            def slot_gates(g, i, j):
                two = slice(2 * j, 2 * j + 2)
                q = g * PAIRS + j
                for v in range(2):
                    dve.wait_ge(e_row[2 * j + v], g * 16 + 16)
                if after_first(g):
                    dve.wait_ge(e_y, (g - 1) * AT_ONCE + 2 * j + 2)
                    for v in range(2):
                        dve.wait_ge(e_sent[2 * j + v], g * 16)
                dve.tensor_tensor(IND[:, two], XR[:, two, R_E1], EC[:, bass.ds(i * AT_ONCE + 2 * j, 2)], ALU.is_equal).then_inc(e_ind, 1)
                dve.wait_ge(e_ind, q + 1)
                dve.tensor_tensor(DEST[:, two], XR[:, two, R_TO], IND[:, two], ALU.subtract)
                dve.tensor_tensor(GW[:, two], XR[:, two, R_DW], IND[:, two], ALU.mult).then_inc(e_gate1, 1)
                dve.wait_ge(e_gate1, q + 1)
                dve.tensor_tensor(GW[:, two], GW[:, two], XR[:, two, R_W2], ALU.add).then_inc(e_gate, 1)

            def slot_low(g, j):
                dve.wait_ge(e_hi, g * PAIRS + j + 1)
                dve.tensor_tensor(EXL[j], ET4[j], EXH[j].bitcast(F32), ALU.subtract).then_inc(e_lo, 1)

            def slots_ahead(g, i, j):
                slot_low(g, j)
                slot_gates(g, i, j)

            def round_(i, f, more):
                g = f * ROUNDS + i
                for j in range(PAIRS):
                    if j + 2 < PAIRS:
                        slots_ahead(g, i, j + 2)
                    elif more:
                        slots_ahead(g + 1, i + 1, j + 2 - PAIRS)

            def experts(f):
                slots_ahead(f * ROUNDS, 0, 0)
                slots_ahead(f * ROUNDS, 0, 1)
                round_(0, f, True)
                with dve.Fori(1, ROUNDS - 1) as i:
                    round_(i, f, True)
                round_(ROUNDS - 1, f, False)

            experts(0)

            def k_parts(b, h):
                dve.wait_ge(b_ks, b * T + 2 * h + 2)
                if after_first(b):
                    dve.wait_ge(b_outer, b)
                for part_, tab in ((KC, cosN), (KSN, sinN)):
                    dve.tensor_tensor(part_[:, 2 * h:2 * h + 2, :], KS[:, 2 * h:2 * h + 2, :], tab[:, 2 * h:2 * h + 2, :],
                                      ALU.mult).then_inc(b_kc, 1)

            def q_parts(b):
                for c in range(KD):
                    dve.wait_ge(b_sq, b * KD + c + 1)
                    if after_first(b):
                        dve.wait_ge(b_o, b * 2)
                    dve.tensor_tensor(QC[:, c, :], SQ[:, c, :], cosT[:, c, :], ALU.mult).then_inc(b_qc, 1)

            def masked_sums(b):
                dve.wait_ge(b_outer, b + 1)
                if after_first(b):
                    dve.wait_ge(b_o, b * 2)
                dve.tensor_tensor(KVM, GB[5].rearrange("p (g n) -> p g n", g=2 * KD),
                                  head_mask.unsqueeze(1).to_broadcast([P, 2 * KD, P]), ALU.mult).then_inc(b_kvm, 1)

            def out_moments(b):
                for t in range(T):
                    if t % 2 == 0:
                        dve.wait_ge(b_o, b * 2 + t // 2 + 1)
                    last = dve.bn_stats(ostats[:, t, :], GB[4 + t // 2][:, (t % 2) * D:(t % 2 + 1) * D])
                last.then_inc(b_ost, 1)
                wait_apart(dve, b_ost, b + 1)
                for t in range(T):
                    last = dve.bn_aggr(omv[:, t, :], ostats[:, t, :])
                last.then_inc(b_omv, 1)

            def out_normalise(b):
                dve.wait_ge(b_ors, b + 1)
                if after_first(b):
                    dve.wait_ge(b_ot, b * KD)
                for t in range(T):
                    last = dve.tensor_scalar(ON[:, t, :], GB[4 + t // 2][:, (t % 2) * D:(t % 2 + 1) * D], omv[:, t, 0:1],
                                             orstd[:, t:t + 1], ALU.subtract, ALU.mult)
                last.then_inc(b_on, 1)

            def gated(b):
                for c in range(KD):
                    dve.wait_ge(b_ona, b * KD + c + 1)
                    dve.wait_ge(b_ut, b * KD + c + 1)
                    if c == 0 and after_first(b):
                        dve.wait_ge(b_out, b * 2)
                    dve.tensor_tensor(ZT[:, c, :], UT[:, c, :], ONA[:, c, :], ALU.mult).then_inc(b_z, 1)

            def b_residual(b):
                for h in range(2):
                    dve.wait_ge(b_out, b * 2 + h + 1)
                    dve.tensor_tensor(two_tiles(b, h), bank2(GB[4 + h]), two_tiles(b, h), ALU.add).then_inc(b_x3, 1)

            def b_body(b, parity, has1, has2, has3, routes, ranks):
                if ranks:
                    route_slots(b - 2, 1, parity)
                if has2:
                    normalise(b + 2, LN_B)
                if routes:
                    route_moments(b - 1, 1)
                masked_sums(b)
                if has1:
                    k_parts(b + 1, 0)
                out_moments(b)
                if routes:
                    route_normalise(b - 1, 1, 1 - parity)
                out_normalise(b)
                if has1:
                    k_parts(b + 1, 1)
                    q_parts(b + 1)
                gated(b)
                if has3:
                    moments(b + 3, LN_B, added2[1 - parity], (((b + 3) >> 1) + 1) * 16)
                if has2:
                    low_part(b + 2, LN_B)
                if routes:
                    route_choice(b - 1, 1)
                b_residual(b)

            moments(0, LN_B, added2[0], 16)
            normalise(0, LN_B)
            moments(1, LN_B, added2[1], 16)
            low_part(0, LN_B)
            normalise(1, LN_B)
            dve.wait_ge(trig_n, 4)
            k_parts(0, 0)
            k_parts(0, 1)
            q_parts(0)
            low_part(1, LN_B)
            moments(2, LN_B, added2[0], 32)
            b_body(0, 0, True, True, True, False, False)
            b_body(1, 1, True, True, True, True, False)
            b_body(2, 0, True, True, True, True, True)
            with dve.Fori(1, (B - 4) // 2) as i:
                b_body(i * 2 + 1, 1, True, True, True, True, True)
                b_body(i * 2 + 2, 0, True, True, True, True, True)
            b_body(B - 3, 1, True, True, False, True, True)
            b_body(B - 2, 0, True, False, False, True, True)
            b_body(B - 1, 1, False, False, False, True, True)
            finish_routing(1)
            experts(1)


def kernel(**inputs):
    import concourse.bacc as bacc
    from concourse.bass_utils import run_bass_kernel_spmd

    a = {n.split("L0_")[1]: np.asarray(v) for n, v in inputs.items()}

    def cols(v):
        return v.reshape(-1, P).T

    def rows(v):
        return np.broadcast_to(v.reshape(1, -1), (P, v.size))

    def chunks(m):
        return m.reshape(-1, P, m.shape[1]).transpose(1, 0, 2).reshape(P, -1)

    bqkvu = a["attn_b_bqkvu"]
    params = {
        "bin": cols(a["attn_a_bin_"]), "dp": cols(a["attn_a_Dp"]), "bp": chunks(a["attn_a_Bp"]),
        "cp": chunks(a["attn_a_Cp"].T), "bq": cols(bqkvu[0:D]), "bu": cols(bqkvu[3 * D:]),
        "theta": cols(a["attn_b_theta"].reshape(-1)), "lnw": cols(a["attn_b_ln_w"]), "lnb": cols(a["attn_b_ln_b"]),
        "bg": rows(a["ffn_bg"]), "wg": chunks(a["ffn_Wg"]),
    }
    arrays = {
        "x": a["attn_a_x"],
        "consts": shape_constants(),
        "params": np.concatenate([params[n] for n in PAR], axis=1),
        "win": a["attn_a_Win"],
        "wout": a["attn_a_Wout"],
        "wqkvu": a["attn_b_Wqkvu"].T,
        "wo": a["attn_b_Wout"].T,
        "we": a["ffn_We"].transpose(2, 0, 1).reshape(D, NE * D),
        "be2": np.stack([a["ffn_be"].reshape(-1)] * 2),
        "rows2": np.stack([np.concatenate([bqkvu[D:3 * D], a["attn_a_bout"], a["attn_b_bout"]])] * 2),
    }
    arrays = {n: np.ascontiguousarray(v) for n, v in arrays.items()}
    nc = bacc.Bacc("TRN2", target_bir_lowering=False, num_devices=1)
    args = [nc.dram_tensor(n, v.shape, mybir.dt.from_np(v.dtype), kind="ExternalInput").ap() for n, v in arrays.items()]
    out = nc.dram_tensor("out", (B, L, D), F32, kind="ExternalOutput").ap()
    slots = nc.dram_tensor("slots", ((NE * ROOM + NE) * P, ROW), F32, kind="Internal").ap()
    chosen = nc.dram_tensor("chosen", (2 * B * L, D), F32, kind="Internal").ap()
    build(nc, *args, slots, chosen, out)
    r = run_bass_kernel_spmd(nc, [arrays], core_ids=[0])
    return r.results[0]["out"]
```

```python
from contextlib import ExitStack

import numpy as np

import concourse.bass as bass
from concourse import mybir

ALU = mybir.AluOpType
ACT = mybir.ActivationFunctionType
AX = mybir.AxisListType
F32 = mybir.dt.float32
F32R = mybir.dt.float32r
BF16 = mybir.dt.bfloat16
U32 = mybir.dt.uint32
I32 = mybir.dt.int32

P = 128
B, L, D = 8, 512, 256
T = L // P
KD = D // P
DI = 512
MI = DI // P
DS = 16
DH = 16
NE = 8
HALF = B // 2
ROOM = HALF * T + 1
TILES = 2 * HALF * T + NE
AT_ONCE = 8
PAIRS = AT_ONCE // 2
ROUNDS = TILES // AT_ONCE
ROW = 260
R_W2, R_DW, R_E1, R_TO = D, D + 1, D + 2, D + 3
NOWHERE = 1.0e6
LPAD = 16
DECAY = 0.9
EPS = 1e-5
SENTINEL = -3.0e38

TWO_PI_1, TWO_PI_2 = 6.28125, 0.0019350051879882812
TWO_PI_3 = float(2 * np.pi - TWO_PI_1 - TWO_PI_2)
INV_TWO_PI = float(1 / (2 * np.pi))
ROUND = 12582912.0
PI_BELOW = 3.1415925


def columns(*widths):
    at, out = 0, {}
    for name, w in widths:
        out[name] = (at, at + w)
        at += w
    return out, at


CON, CON_W = columns(("ident", P), ("mask", P), ("pos", L), ("before", P), ("expert", NE), ("first", NE),
                     ("place", B * T), ("tile", TILES), ("sel2", 2))
PAR, PAR_W = columns(("bin", MI), ("dp", MI), ("bp", MI * DS), ("cp", MI * DS), ("bq", KD), ("bu", KD), ("theta", KD),
                     ("lnw", KD), ("lnb", KD), ("bg", NE), ("wg", KD * NE))
ROWS, ROWS_W = columns(("bkv", 2 * D), ("bout", D), ("bo", D))


def shape_constants():
    c = np.zeros((P, CON_W), np.float32)
    c[:, slice(*CON["ident"])] = np.eye(P)
    c[:, slice(*CON["mask"])] = np.kron(np.eye(P // DH), np.ones((DH, DH)))
    c[:, slice(*CON["pos"])] = np.arange(L)[None, :]
    c[0:2, slice(*CON["sel2"])] = [[0, 1], [1, -1]]
    c[:, slice(*CON["before"])] = np.triu(np.ones((P, P)), 1)
    c[:, slice(*CON["expert"])] = np.arange(NE)[None, :]
    c[:, slice(*CON["first"])] = np.arange(NE)[None, :] * ROOM * P
    c[:, slice(*CON["place"])] = 2 * ((np.arange(B * T)[None, :] % (HALF * T)) * P + np.arange(P)[:, None]) + 1
    c[:, slice(*CON["tile"])] = np.arange(TILES)[None, :]
    return c


def build(nc, x, consts, params, win, wout, wqkvu, wo, we, be2, rows2, slots, chosen, out):
    with ExitStack() as ctx:
        def sb(name, shape, dt=F32):
            return ctx.enter_context(nc.sbuf_tensor(name, shape, dt))

        def sem(name):
            return ctx.enter_context(nc.semaphore(name))

        X = sb("X", [P, B * T, D])
        con, par = sb("con", [P, CON_W]), sb("par", [P, PAR_W])
        ident, head_mask, pos, expert, first_slot, place, tile = (
            con[:, slice(*CON[n])] for n in ("ident", "mask", "pos", "expert", "first", "place", "tile"))
        sel2 = CON["sel2"][0]
        bin_s, dp_s, bq_s, bu_s, theta_s, lnw_s, lnb_s, bg_s, wg_s = (
            par[:, slice(*PAR[n])] for n in ("bin", "dp", "bq", "bu", "theta", "lnw", "lnb", "bg", "wg"))
        win_h, win_l = sb("win_h", [P, KD, DI], F32R), sb("win_l", [P, KD, DI], F32R)
        wq_h, wq_l = sb("wq_h", [P, KD, 4 * D], F32R), sb("wq_l", [P, KD, 4 * D], F32R)
        we_h, we_l = sb("we_h", [P, KD, NE * D], F32R), sb("we_l", [P, KD, NE * D], F32R)
        be_rows, rows = sb("be_rows", [2, NE * D], F32R), sb("rows", [2, ROWS_W], F32R)
        unused = sb("unused", [2, 1])
        ones_f, ones2 = sb("ones_f", [2, P]), sb("ones2", [2, P], F32R)
        wout_s, wo_s = sb("wout_s", [P, MI, D]), sb("wo_s", [P, KD, D])
        bc_s, g_s = sb("bc_s", [P, MI * DS]), sb("g_s", [P, MI])
        decay, minus_half = sb("decay", [P, L]), sb("minus_half", [P, T])
        cosT, sinT = sb("cosT", [P, KD, L]), sb("sinT", [P, KD, L])
        cosN, sinN = sb("cosN", [P, T, D]), sb("sinN", [P, T, D])

        stats, mv = sb("stats", [P, T, 6]), sb("mv", [P, T, 2])
        veps, rstd = sb("veps", [P, T]), sb("rstd", [P, T])
        XN = sb("XN", [P, T, D])
        XH, XL = sb("XH", [P, KD, L], F32R), sb("XL", [P, KD, L], F32R)

        work = sb("work", [P, 12 * 1024])

        def part(k, n, w):
            return work[:, k * 1024:k * 1024 + n * w].rearrange("p (n w) -> p n w", n=n)

        XI, XG, SG = part(0, MI, L), part(2, MI, L), part(4, MI, L)
        Y = [part(6, MI, L), part(8, MI, L)]
        SQ, QC, QS = part(0, KD, L), part(1, KD, L), part(2, KD, L)
        KS, KC, KSN, V = part(3, T, D), part(4, T, D), part(5, T, D), part(6, T, D)
        KVM = part(7, 2 * KD, P)
        ON, ONA, UT, ZT = part(8, T, D), part(9, KD, L), part(10, KD, L), part(11, KD, L)
        ostats, omv = sb("ostats", [P, T, 6]), sb("omv", [P, T, 2])
        oveps, orstd = sb("oveps", [P, T]), sb("orstd", [P, T])
        XR = work[:, 0:AT_ONCE * ROW].rearrange("p (s w) -> p s w", s=AT_ONCE)
        YO = part(3, AT_ONCE, D)
        EXH, EXL = ([whole_[:, i, :] for whole_ in parts for i in range(KD)] for parts in ((XH, win_h), (XL, win_l)))
        BACK = part(10, T, 2 * D)
        LAST = [part(2 * k, T, 2 * D) for k in range(HALF)]
        by_token = [rows_.rearrange("(t p k) d -> p t (k d)", p=P, k=2) for rows_ in chosen]
        th, whole, turn = part(5, KD, L), part(6, 2 * KD, L), part(8, 2 * KD, L)
        we_raw = [part(10, KD, D), work[:, 10752:11264].rearrange("p (k d) -> p k d", k=KD)]
        win_raw = part(11, KD, DI)
        be_raw = [tab[0:2, :, :].rearrange("p k l -> p (k l)") for tab in (cosT, sinT)]
        wq_raw = [cosN[:].rearrange("p t d -> p (t d)"), sinN[:].rearrange("p t d -> p (t d)")]

        rstats, rmv = sb("rstats", [P, T, 6]), sb("rmv", [P, T, 2])
        rveps, rrstd = sb("rveps", [P, T]), sb("rrstd", [P, T])
        XNR = [sb(f"XNR{i}", [P, T, ROW]) for i in range(2)]
        rows_raw = XNR[0][0:2, :, :].rearrange("p t w -> p (t w)")[:, 0:ROWS_W]
        XT = sb("XT", [P, KD, L])
        LGX, M8, MIX = sb("LGX", [P, T, LPAD]), sb("M8", [P, T, 8]), sb("MIX", [P, T, 8], U32)
        EI, GAP = sb("EI", [P, T, 2]), sb("GAP", [P, T])
        MASK, BOTH = sb("MASK", [P, T, 2, NE], BF16), sb("BOTH", [P, T, NE], BF16)
        POS, PICK, SLOT = sb("POS", [P, T, NE]), sb("PICK", [P, T, 2, NE]), sb("SLOT", [P, T, 2])
        IDX = [sb(f"IDX{i}", [P, 2 * T], U32) for i in range(2)]
        before, ones_b = sb("before", [P, P], BF16), sb("ones_b", [P, P], BF16)
        NEXT = sb("NEXT", [P, NE])
        PAD = sb("PAD", [P, ROW])
        USED_f, USED = sb("USED_f", [1, NE // 2]), sb("USED", [1, 4 * NE // 2], I32)
        CNT, NT, CI, ones_e = sb("CNT", [P, NE]), sb("NT", [P, NE]), sb("CI", [P, NE]), sb("ones_e", [P, NE])
        CMP = [free.rearrange("p (t e) -> p t e", e=NE) for free in (work[:, 11264:11264 + TILES * NE], decay[:, 0:TILES * NE])]
        ET, SKIP, RT = sb("ET", [P, TILES]), sb("SKIP", [P, TILES]), sb("RT", [P, TILES])
        RP_f, EP_f = sb("RP_f", [1, TILES // 2]), sb("EP_f", [1, ROUNDS])
        EC, RP, EP = sb("EC", [P, 2 * TILES]), sb("RP", [1, TILES], I32), sb("EP", [1, 2 * ROUNDS], I32)
        BESIDE = sb("BESIDE", [P, AT_ONCE, ROW - D])
        B_W2, B_DW, B_E1, B_TO = (c - D for c in (R_W2, R_DW, R_E1, R_TO))
        IND, GW, DEST = sb("IND", [P, AT_ONCE]), sb("GW", [P, AT_ONCE]), sb("DEST", [P, AT_ONCE], U32)

        ps = ctx.enter_context(nc.psum_tensor("ps", [P, 8, 512], F32))
        TB = [ps[:, 0, :], ps[:, 1, :]]
        GB = [ps[:, 2 + i, :] for i in range(6)]
        ET4 = [TB[0], TB[1], GB[4], GB[5]]

        ld_con, ld_par, ld_x0, ld_x1, ld_x, ld_win, ld_wout = (sem("ld_" + n) for n in ("con", "par", "x0", "x1", "x", "win", "wout"))
        ld_wq = [sem("ld_wq0"), sem("ld_wq1")]
        ld_wo, ld_be, ld_rows = (sem("ld_" + n) for n in ("wo", "be", "rows"))
        ld_we = [sem("ld_we0"), sem("ld_we1")]
        fills_p, fills_v = sem("fills_p"), sem("fills_v")
        win_hi, win_lo, wq_hi, wq_lo, we_hi, we_lo = (
            sem(n) for n in ("win_hi", "win_lo", "wq_hi", "wq_lo", "we_hi", "we_lo"))
        rows_hi, rows_a, rows_done, bc_done, g_done = (sem(n) for n in ("rows_hi", "rows_a", "rows_done", "bc_done", "g_done"))
        before_done = sem("before_done")
        arg_step, arg_done, trig_done, trig_t, trig_n = (sem(n) for n in ("arg_step", "arg_done", "trig_done", "trig_t", "trig_n"))
        st_done, mv_done, rs_add, rs_done = sem("st_done"), sem("mv_done"), sem("rs_add"), sem("rs_done")
        xn_done, t_done, hi_done, lo_done = sem("xn_done"), sem("t_done"), sem("hi_done"), sem("lo_done")
        a_win, a_silu, a_xg, a_scan, a_y, a_out, a_x1 = (
            sem("a_" + n) for n in ("win", "silu", "xg", "scan", "y", "out", "x1"))
        r_st, r_mv, r_add, r_rs, r_xn, r_t, r_xt, r_logit, r_lg, r_m8, r_mi, r_ei, r_gap = (
            sem("r_" + n) for n in ("st", "mv", "add", "rs", "xn", "t", "xt", "logit", "lg", "m8", "mi", "ei", "gap"))
        r_mask, r_both, r_cols, r_rank, r_pos, r_next, r_pick, r_slot, r_idx = (
            sem("r_" + n) for n in ("mask", "both", "cols", "rank", "pos", "next", "pick", "slot", "idx"))
        r_scattered = [sem("r_scattered0"), sem("r_scattered1")]
        count_step, tab_step, tab_done, pad_idx, padded, spare = (sem(n) for n in ("count_step", "tab_step", "tab_done", "pad_idx", "padded", "spare"))
        e_row = [sem(f"e_row{i}") for i in range(AT_ONCE)]
        e_sent = [sem(f"e_sent{i}") for i in range(AT_ONCE)]
        e_t, e_hi, e_lo, e_mm, e_beside, e_ind, e_gate1, e_gate, e_y = (
            sem("e_" + n) for n in ("t", "hi", "lo", "mm", "beside", "ind", "gate1", "gate", "y"))
        back_in, back_one, back_done = sem("back_in"), sem("back_one"), sem("back_done")
        added1, added2 = ([sem(f"added{k}_{i}") for i in range(2)] for k in (1, 2))
        last_in = [sem(f"last_in{i}") for i in range(HALF)]
        last_one, last_done = sem("last_one"), sem("last_done")
        b_kv, b_ks, b_v, b_kc, b_q, b_sq, b_qc, b_qs, b_u, b_ut, b_outer, b_kvm = (
            sem("b_" + n) for n in ("kv", "ks", "v", "kc", "q", "sq", "qc", "qs", "u", "ut", "outer", "kvm"))
        b_o, b_ost, b_omv, b_oadd, b_ors, b_on, b_ot, b_ona, b_z, b_out, b_x3 = (
            sem("b_" + n) for n in ("o", "ost", "omv", "oadd", "ors", "on", "ot", "ona", "z", "out", "x3"))
        stored = sem("stored")

        LN_A, LN_B = 0, 1

        def after_first(b):
            return not isinstance(b, int) or b > 0

        wait_value = [nc.vector.alloc_register("wait_value"), nc.gpsimd.alloc_register("wait_value")]

        def wait_apart(engine, semaphore, value):
            if not isinstance(value, int):
                engine.reg_mov(wait_value[engine is nc.gpsimd], value)
                value = wait_value[engine is nc.gpsimd]
            engine.wait_ge(fills_p if engine is nc.gpsimd else fills_v, 2)
            engine.wait_ge(semaphore, value)

        def mm3(pe, acc, pairs, more=False):
            n = len(pairs)
            for i, (ah, al, bh, bl) in enumerate(pairs):
                pe.matmul(acc, ah, bh, start=(i == 0), stop=False)
                pe.matmul(acc, ah, bl, start=False, stop=False)
                last = pe.matmul(acc, al, bh, start=False, stop=(i == n - 1 and not more))
            return last

        def row(name):
            return rows[:, slice(*ROWS[name])]

        def two_tiles(b, h):
            return X[:, bass.ds(b * T + 2 * h, 2), :]

        def bank2(bank):
            return bank.rearrange("p (t d) -> p t d", t=2)

        block = ctx.enter_context(nc.Block())

        @block.sync
        def _(sp):
            xt = x.rearrange("b (t p) d -> p (b t) d", p=P)
            ot = out.rearrange("b (t p) d -> p (b t) d", p=P)
            sp.dma_start(X[:, 0:T, :], xt[:, 0:T, :]).then_inc(ld_x0, 16)
            sp.dma_start(con[:, :], consts).then_inc(ld_con, 16)
            sp.dma_start(par[:, :], params).then_inc(ld_par, 16)
            sp.dma_start(X[:, T:2 * T, :], xt[:, T:2 * T, :]).then_inc(ld_x1, 16)
            sp.dma_start(wout_s[:], wout.rearrange("(m p) n -> p m n", p=P)).then_inc(ld_wout, 16)
            sp.dma_start(X[:, 2 * T:, :], xt[:, 2 * T:, :]).then_inc(ld_x, 16)
            sp.dma_start(wo_s[:], wo.rearrange("(k p) n -> p k n", p=P)).then_inc(ld_wo, 16)
            for e in range(NE):
                if e >= 2:
                    sp.wait_ge(we_lo, e - 1)
                sp.dma_start(we_raw[e % 2], we.rearrange("(k p) n -> p k n", p=P)[:, :, e * D:(e + 1) * D]).then_inc(ld_we[e % 2], 16)

            pairs_read = sp.alloc_register("pairs_read")

            def pad_slots(n, pair_of_experts):
                at = n * NE // 2 + pair_of_experts
                two = sp.value_load(USED[0:1, at:at + 1], min_val=0, max_val=(1 << 24) - 1)
                for v in range(2):
                    used = nc.s_assert_within(((two >> 12) if v else two) & 4095, 0, HALF * L,
                                              skip_runtime_bounds_check_because="no expert has more tokens")
                    behind = sp.snap(used + (2 * pair_of_experts + v) * ROOM * P)
                    sp.dma_start(slots[n % 2][bass.ds(behind, P), :], PAD[:, :]).then_inc(padded, 16)

            def round_rows(i, n, pads=False):
                g = n * ROUNDS + i
                if pads:
                    sp.wait_ge(pad_idx, n + 2)
                for j in range(PAIRS):
                    two = sp.value_load(RP[0:1, bass.ds((n % 2) * (TILES // 2) + i * PAIRS + j, 1)], min_val=0, max_val=(1 << 18) - 1)
                    used = n or after_first(i)
                    if used:
                        sp.reg_mov(pairs_read, (g - 1) * PAIRS + j + 1)
                    for v in range(2):
                        first = sp.snap(nc.s_assert_within(((two >> 9) if v else two) & 511, 0, NE * ROOM + NE - 1,
                                                           skip_runtime_bounds_check_because="the table has no other tiles") * P)
                        if used and v == 0:
                            sp.wait_ge(tab_done, n + 1)
                            sp.wait_ge(e_t, pairs_read)
                            sp.wait_ge(e_beside, pairs_read)
                        s = 2 * j + v
                        sp.dma_start(XR[:, s, :], slots[n % 2][bass.ds(first, P), :]).then_inc(e_row[s], 16)
                    if pads:
                        pad_slots(n + 1, j)

            sp.wait_ge(fills_p, 7)
            for n in range(4):
                if n % 2 == 0:
                    sp.wait_ge(pad_idx, n + 1)
                    for pair_of_experts in range(NE // 2):
                        pad_slots(n, pair_of_experts)
                sp.wait_ge(tab_done, n + 1)
                for parity in range(2):
                    sp.wait_ge(r_scattered[parity], 16 * 2 * T * (HALF // 2) * (n + 1))
                sp.wait_ge(padded, 16 * NE * (n + 1))
                if n % 2 == 0:
                    if n == 0:
                        sp.wait_ge(spare, 32)
                        sp.wait_ge(a_y, B * MI)
                    else:
                        sp.wait_ge(b_o, B * 2)
                    round_rows(0, n)
                    with sp.Fori(1, ROUNDS - 1) as i:
                        round_rows(i, n)
                    round_rows(ROUNDS - 1, n, True)
                else:
                    with sp.Fori(0, ROUNDS) as i:
                        round_rows(i, n)
            for b in range(HALF):
                sp.wait_ge(back_done, HALF + b + 1)
                sp.dma_start(ot[:, b * T:(b + 1) * T, :], X[:, b * T:(b + 1) * T, :]).then_inc(stored, 16)
            for s in range(AT_ONCE):
                sp.wait_ge(e_sent[s], 4 * ROUNDS * 16)
            for k in range(HALF):
                sp.dma_start(LAST[k], by_token[1][:, k * T:(k + 1) * T, :]).then_inc(last_in[k], 16)
            for b in range(HALF, B):
                sp.wait_ge(last_done, b - HALF + 1)
                sp.dma_start(ot[:, b * T:(b + 1) * T, :], X[:, b * T:(b + 1) * T, :]).then_inc(stored, 16)
            sp.wait_ge(stored, 16 * B)

        @block.tensor
        def _(pe):
            def transposes(b, p):
                q = p * B + b
                pe.wait_ge(xn_done, q + 1)
                if p or after_first(b):
                    pe.wait_ge(lo_done, q * KD)
                for c in range(KD):
                    for t in range(T):
                        last = pe.transpose(TB[c][:, t * P:(t + 1) * P], XN[:, t, c * P:(c + 1) * P], ident)
                    last.then_inc(t_done, 1)

            def win_products(b):
                pe.wait_ge(lo_done, b * KD + KD)
                for m in range(MI):
                    if after_first(b) or m >= 2:
                        pe.wait_ge(a_silu, b * MI + m - 1)
                    mm3(pe, GB[m % 2], [(win_h[:, k, m * P:(m + 1) * P], win_l[:, k, m * P:(m + 1) * P],
                                     XH[:, k, :], XL[:, k, :]) for k in range(KD)]).then_inc(a_win, 1)

            def wout_products(b, y, h):
                if h == 0:
                    pe.wait_ge(a_y, b * MI + MI)
                if after_first(b):
                    pe.wait_ge(a_x1, (b - 1) * 2 + h + 1)
                for t in (2 * h, 2 * h + 1):
                    acc = GB[4 + h][:, (t % 2) * D:(t % 2 + 1) * D]
                    for m in range(MI):
                        pe.matmul(acc, y[:, m, t * P:(t + 1) * P], wout_s[:, m, :], start=(m == 0), stop=False)
                    last = pe.matmul(acc, ones2[:, :], row("bout"), start=False, stop=True)
                last.then_inc(a_out, 1)

            def route_transposes(b, f, parity):
                r = f * B + b
                pe.wait_ge(r_xn, r + 1)
                if f or after_first(b):
                    pe.wait_ge(r_next, r)
                    pe.wait_ge(r_logit, r)
                for c in range(KD):
                    for t in range(T):
                        last = pe.transpose(GB[2 + c][:, t * P:(t + 1) * P], XNR[parity][:, t, c * P:(c + 1) * P], ident)
                    last.then_inc(r_t, 1)

            def route_logits(b, f):
                r = f * B + b
                pe.wait_ge(r_xt, r * KD + KD)
                for t in range(T):
                    for k in range(KD):
                        last = pe.matmul(GB[2][:, t * NE:(t + 1) * NE], XT[:, k, t * P:(t + 1) * P],
                                         wg_s[:, k * NE:(k + 1) * NE], start=(k == 0), stop=(k == KD - 1))
                last.then_inc(r_logit, 1)

            def route_ranks(b, f):
                r = f * B + b
                pe.wait_ge(r_both, r + 1)
                both = BOTH[:].rearrange("p t e -> p (t e)")
                pe.matmul(GB[3][:, 0:T * NE], before[:, :], both, start=True, stop=False)
                for u in range(1, T):
                    pe.matmul(GB[3][:, u * NE:T * NE], ones_b[:, :], both[:, 0:(T - u) * NE], start=False, stop=(u == T - 1))
                for u in range(T):
                    last = pe.matmul(GB[3][:, T * NE:(T + 1) * NE], ones_b[:, :], both[:, u * NE:(u + 1) * NE],
                                     start=(u == 0), stop=(u == T - 1))
                last.then_inc(r_rank, 1)

            def a_body(b, parity, has1, has2, routes, ranks):
                if has1:
                    win_products(b + 1)
                if ranks:
                    route_ranks(b - 2, 0)
                if has2:
                    transposes(b + 2, LN_A)
                wout_products(b, Y[parity], 0)
                if not has2:
                    wout_products(b, Y[parity], 1)
                if routes:
                    route_transposes(b - 1, 0, 1 - parity)
                if has2:
                    wout_products(b, Y[parity], 1)
                if routes:
                    route_logits(b - 1, 0)

            pe.wait_ge(ld_con, 16)
            transposes(0, LN_A)
            pe.wait_ge(win_lo, 1)
            win_products(0)
            transposes(1, LN_A)
            win_products(1)
            pe.wait_ge(ld_wout, 16)
            pe.wait_ge(rows_done, 1)
            pe.wait_ge(rows_hi, 2)
            pe.wait_ge(before_done, 1)
            a_body(0, 0, False, True, False, False)
            a_body(1, 1, True, True, True, False)
            a_body(2, 0, True, True, True, True)
            with pe.Fori(1, (B - 4) // 2) as i:
                a_body(i * 2 + 1, 1, True, True, True, True)
                a_body(i * 2 + 2, 0, True, True, True, True)
            a_body(B - 3, 1, True, True, True, True)
            a_body(B - 2, 0, True, False, True, True)
            a_body(B - 1, 1, False, False, True, True)

            def slot_transposes(g, j):
                for v in range(2):
                    pe.wait_ge(e_row[2 * j + v], g * 16 + 16)
                if after_first(g):
                    pe.wait_ge(e_lo, (g - 1) * PAIRS + j + 1)
                for v in range(2):
                    for c in range(KD):
                        at = (v * KD + c) * P
                        last = pe.transpose(ET4[j][:, at:at + P], XR[:, 2 * j + v, c * P:(c + 1) * P], ident)
                last.then_inc(e_t, 1)

            def slot_products(g, j, choices):
                pe.wait_ge(e_lo, g * PAIRS + j + 1)
                if after_first(g) or j >= 2:
                    pe.wait_ge(e_y, g * AT_ONCE + 2 * j - 2)
                for v in range(2):
                    out_ = GB[j % 2][:, v * D:(v + 1) * D]
                    first = pe.snap(((choices >> (3 * (2 * j + v))) & 7) * D, min_val=0, max_val=(NE - 1) * D)
                    for k in range(KD):
                        at = (v * KD + k) * P
                        high, low = EXH[j][:, at:at + P], EXL[j][:, at:at + P]
                        pe.matmul(out_, high, we_h[:, k, bass.ds(first, D)], start=(k == 0), stop=False)
                        pe.matmul(out_, high, we_l[:, k, bass.ds(first, D)], start=False, stop=False)
                        pe.matmul(out_, low, we_h[:, k, bass.ds(first, D)], start=False, stop=False)
                    last = pe.matmul(out_, ones2[:, :], be_rows[:, bass.ds(first, D)], start=False, stop=True)
                last.then_inc(e_mm, 1)

            def pair_(g, j, more, choices):
                if j + 2 < PAIRS:
                    slot_transposes(g, j + 2)
                elif more:
                    slot_transposes(g + 1, j + 2 - PAIRS)
                slot_products(g, j, choices)

            def round_(i, n, more, others=False):
                choices = pe.value_load(EP[0:1, bass.ds((n % 2) * ROUNDS + i, 1)], min_val=0, max_val=(1 << 3 * AT_ONCE) - 1)
                for j in range(PAIRS):
                    pair_(n * ROUNDS + i, j, more, choices)
                    if others and n % 2 == 0:
                        last_routing(n // 2, i * PAIRS + j)
                    elif others and j % 2 == 0:
                        trig_transposes(j // 2)

            def trig_transposes(i):
                pe.wait_ge(trig_done, 2 * KD)
                if i:
                    pe.wait_ge(trig_n, 2)
                tab = (cosT, sinT)[i]
                for t in range(T):
                    for c in range(KD):
                        last = pe.transpose(GB[2 + t // 2][:, (t % 2) * D + c * P:(t % 2) * D + (c + 1) * P],
                                            tab[:, c, t * P:(t + 1) * P], ident)
                    if t % 2:
                        last.then_inc(trig_t, 1)

            def last_routing(f, after):
                if after == 2:
                    route_transposes(B - 1, f, 1)
                elif after == 6:
                    route_logits(B - 1, f)
                elif after == 9:
                    route_ranks(B - 1, f)

            def experts(n):
                if n % 2 == 0:
                    route_ranks(B - 2, n // 2)
                pe.wait_ge(tab_done, n + 1)
                slot_transposes(n * ROUNDS, 0)
                slot_transposes(n * ROUNDS, 1)
                if n % 2 == 0:
                    for i in range(ROUNDS):
                        round_(i, n, i < ROUNDS - 1, True)
                else:
                    round_(0, n, True)
                    with pe.Fori(1, ROUNDS - 1) as i:
                        round_(i, n, True)
                    round_(ROUNDS - 1, n, False, n == 1)

            pe.wait_ge(a_silu, B * MI)
            pe.wait_ge(lo_done, B * KD)
            pe.wait_ge(a_x1, B * 2)
            pe.wait_ge(we_lo, B)
            pe.wait_ge(rows_done, 3)
            experts(0)
            experts(1)

            def kv_products(b, tiles):
                for t in tiles:
                    n = b * T + t
                    if t >= 2:
                        pe.wait_ge(b_v, n - 1)
                    elif after_first(b):
                        pe.wait_ge(b_ut, (b - 1) * KD + t + 1)
                    mm3(pe, GB[t % 2], [(XH[:, k, t * P:(t + 1) * P], XL[:, k, t * P:(t + 1) * P],
                                         wq_h[:, k, D:3 * D], wq_l[:, k, D:3 * D]) for k in range(KD)], more=True)
                    pe.matmul(GB[t % 2], ones2[:, :], row("bkv"), start=False, stop=True).then_inc(b_kv, 1)

            def feature_products(b, first_col, done):
                for m in range(KD):
                    if first_col:
                        pe.wait_ge(b_sq, b * KD + m + 1)
                    else:
                        pe.wait_ge(b_v, b * T + m + 3)
                    col = first_col + m * P
                    mm3(pe, GB[m], [(wq_h[:, k, col:col + P], wq_l[:, k, col:col + P], XH[:, k, :], XL[:, k, :])
                                    for k in range(KD)]).then_inc(done, 1)

            def q_products(b):
                feature_products(b, 0, b_q)

            def u_products(b):
                feature_products(b, 3 * D, b_u)

            def outer_products(b):
                pe.wait_ge(b_v, b * T + T)
                pe.wait_ge(b_kc, b * 4 + 4)
                if after_first(b):
                    pe.wait_ge(b_x3, b * 2)
                for c in range(KD):
                    for s, kk in enumerate((KC, KSN)):
                        g = 2 * c + s
                        for t in range(T):
                            last = pe.matmul(GB[5][:, g * P:(g + 1) * P], kk[:, t, c * P:(c + 1) * P],
                                             V[:, t, c * P:(c + 1) * P], start=(t == 0), stop=(t == T - 1))
                last.then_inc(b_outer, 1)

            def attend(b):
                pe.wait_ge(b_kvm, b + 1)
                pe.wait_ge(b_qc, b * KD + KD)
                pe.wait_ge(b_qs, b * KD + KD)
                for h in range(2):
                    for t in (2 * h, 2 * h + 1):
                        for c in range(KD):
                            at = (t % 2) * D + c * P
                            for s, qq in enumerate((QC, QS)):
                                last = pe.matmul(GB[4 + h][:, at:at + P], qq[:, c, t * P:(t + 1) * P],
                                                 KVM[:, 2 * c + s, :], start=(s == 0), stop=(s == 1))
                    last.then_inc(b_o, 1)

            def out_transposes(b, has1):
                pe.wait_ge(b_on, b + 1)
                pe.wait_ge(lo_done, (LN_B * B + b + (2 if has1 else 1)) * KD)
                for c in range(KD):
                    for t in range(T):
                        last = pe.transpose(TB[c][:, t * P:(t + 1) * P], ON[:, t, c * P:(c + 1) * P], ident)
                    last.then_inc(b_ot, 1)

            def out_products(b):
                pe.wait_ge(b_z, b * KD + KD)
                for h in range(2):
                    for t in (2 * h, 2 * h + 1):
                        acc = GB[4 + h][:, (t % 2) * D:(t % 2 + 1) * D]
                        for c in range(KD):
                            pe.matmul(acc, ZT[:, c, t * P:(t + 1) * P], wo_s[:, c, :], start=(c == 0), stop=False)
                        last = pe.matmul(acc, ones2[:, :], row("bo"), start=False, stop=True)
                    last.then_inc(b_out, 1)

            def b_body(b, parity, has1, has2, routes, ranks):
                if has1:
                    pe.wait_ge(lo_done, (LN_B * B + b + 2) * KD)
                    kv_products(b + 1, (0,))
                if ranks:
                    route_ranks(b - 2, 1)
                outer_products(b)
                if has1:
                    kv_products(b + 1, (1,))
                attend(b)
                if has1:
                    kv_products(b + 1, (2, 3))
                    q_products(b + 1)
                out_transposes(b, has1)
                if has1:
                    u_products(b + 1)
                if routes:
                    route_transposes(b - 1, 1, 1 - parity)
                if has2:
                    pe.wait_ge(b_ona, b * KD + KD)
                    transposes(b + 2, LN_B)
                if routes:
                    route_logits(b - 1, 1)
                out_products(b)

            pe.wait_ge(e_y, 2 * TILES)
            pe.wait_ge(wq_lo, 2)
            pe.wait_ge(trig_n, 4)
            pe.wait_ge(ld_wo, 16)
            transposes(0, LN_B)
            pe.wait_ge(lo_done, (LN_B * B + 1) * KD)
            kv_products(0, range(T))
            q_products(0)
            u_products(0)
            transposes(1, LN_B)
            b_body(0, 0, True, True, False, False)
            b_body(1, 1, True, True, True, False)
            b_body(2, 0, True, True, True, True)
            with pe.Fori(1, (B - 4) // 2) as i:
                b_body(i * 2 + 1, 1, True, True, True, True)
                b_body(i * 2 + 2, 0, True, True, True, True)
            b_body(B - 3, 1, True, True, True, True)
            b_body(B - 2, 0, True, False, True, True)
            b_body(B - 1, 1, False, False, True, True)
            pe.wait_ge(b_x3, B * 2)
            pe.wait_ge(b_ona, B * KD)
            pe.wait_ge(b_ut, B * KD)
            experts(2)
            experts(3)

        @block.scalar
        def _(act):
            def high_part(b, p, free, count):
                q = p * B + b
                if free is not None:
                    act.wait_ge(free, count)
                for c in range(KD):
                    act.wait_ge(t_done, q * KD + c + 1)
                    act.activation(XH[:, c, :], TB[c], ACT.Copy).then_inc(hi_done, 1)

            act.dma_start(win_raw, win.rearrange("(k p) n -> p k n", p=P)).then_inc(ld_win, 16)
            for k in range(KD):
                act.dma_start(wq_raw[k], wqkvu[k * P:(k + 1) * P, :]).then_inc(ld_wq[k], 16)
            act.dma_start(rows_raw, rows2).then_inc(ld_rows, 16)
            for h in range(2):
                act.dma_start(be_raw[h], be2[:, h * NE * D // 2:(h + 1) * NE * D // 2]).then_inc(ld_be, 16)

            def route_copies(b, f):
                for c in range(KD):
                    act.wait_ge(r_t, (f * B + b) * KD + c + 1)
                    act.activation(XT[:, c, :], GB[2 + c], ACT.Copy).then_inc(r_xt, 1)

            def route_columns(b, f, parity):
                act.wait_ge(r_gap, f * B + b + 1)
                act.activation(XNR[parity][:, :, R_DW], GAP[:, :], ACT.Tanh, scale=0.5)
                act.activation(XNR[parity][:, :, R_TO], place[:, bass.ds(b * T, T)], ACT.Copy).then_inc(r_cols, 1)

            def silu(b, m):
                act.wait_ge(a_win, b * MI + m + 1)
                if after_first(b):
                    act.wait_ge(a_y, (b - 1) * MI + m + 1)
                act.activation(XI[:, m, :], GB[m % 2], ACT.Silu, bias=bin_s[:, m:m + 1]).then_inc(a_silu, 1)

            def scaled(b, m):
                act.wait_ge(a_silu, b * MI + m + 1)
                act.mul(XG[:, m, :], XI[:, m, :], g_s[:, m:m + 1]).then_inc(a_xg, 1)

            def inner(b, between=None):
                silu(b, 0)
                for m in range(1, MI):
                    silu(b, m)
                    scaled(b, m - 1)
                    if m == 1 and between:
                        between()
                scaled(b, MI - 1)

            def we_high(e, ring, count):
                act.wait_ge(ld_we[ring], count * 16)
                act.activation(we_h[:, :, bass.ds(e * D, D)], we_raw[ring], ACT.Copy).then_inc(we_hi, 1)

            def a_body(b, parity, has1, has2, routes, ranks, turn_):
                if has1:
                    inner(b + 1, (lambda: route_columns(b - 2, 0, parity)) if ranks else None)
                elif ranks:
                    route_columns(b - 2, 0, parity)
                if has2:
                    high_part(b + 2, LN_A, a_win, (b + 2) * MI)
                if routes:
                    route_copies(b - 1, 0)
                we_high(b, parity, turn_)

            act.wait_ge(fills_p, 2)
            act.activation(unused[:, :], ones_f[:, 0:1], ACT.Silu)
            act.wait_ge(ld_win, 16)
            act.activation(win_h[:], win_raw, ACT.Copy).then_inc(win_hi, 1)
            high_part(0, LN_A, None, 0)
            act.wait_ge(ld_par, 16)
            act.wait_ge(g_done, 1)
            inner(0)
            high_part(1, LN_A, a_win, MI)
            act.wait_ge(ld_rows, 16)
            act.activation(rows[:, :], rows_raw, ACT.Copy).then_inc(rows_hi, 1)
            act.wait_ge(fills_p, 2)
            act.activation(ones2[:, :], ones_f[:, :], ACT.Copy).then_inc(rows_hi, 1)
            act.wait_ge(ld_con, 16)
            act.activation(before[:, :], con[:, slice(*CON["before"])], ACT.Copy).then_inc(before_done, 1)
            a_body(0, 0, True, True, False, False, 1)
            a_body(1, 1, True, True, True, False, 1)
            a_body(2, 0, True, True, True, True, 2)
            with act.Fori(1, (B - 4) // 2) as i:
                a_body(i * 2 + 1, 1, True, True, True, True, i + 1)
                a_body(i * 2 + 2, 0, True, True, True, True, i + 2)
            a_body(B - 3, 1, True, True, True, True, (B - 2) // 2)
            a_body(B - 2, 0, True, False, True, True, B // 2)
            act.wait_ge(ld_be, 32)
            for h in range(2):
                act.activation(be_rows[:, h * NE * D // 2:(h + 1) * NE * D // 2], be_raw[h], ACT.Copy).then_inc(rows_hi, 1)
            a_body(B - 1, 1, False, False, True, True, B // 2)
            route_columns(B - 2, 0, 0)

            def slot_high(g, j):
                act.wait_ge(e_t, g * PAIRS + j + 1)
                if after_first(g):
                    act.wait_ge(e_mm, (g - 1) * PAIRS + j + 1)
                act.activation(EXH[j], ET4[j], ACT.Copy).then_inc(e_hi, 1)

            def slot_outputs(g, j):
                act.wait_ge(e_mm, g * PAIRS + j + 1)
                act.wait_ge(e_gate, g * PAIRS + j + 1)
                for v in range(2):
                    s = 2 * j + v
                    if after_first(g):
                        act.wait_ge(e_sent[s], g * 16)
                    act.mul(YO[:, s, :], GB[j % 2][:, v * D:(v + 1) * D], GW[:, s:s + 1]).then_inc(e_y, 1)

            def round_(i, n, more, others=False):
                g = n * ROUNDS + i
                for j in range(PAIRS):
                    if j + 2 < PAIRS:
                        slot_high(g, j + 2)
                    elif more:
                        slot_high(g + 1, j + 2 - PAIRS)
                    slot_outputs(g, j)
                    if n % 2 and more and j == PAIRS - 1:
                        load_back(i, n)
                    if others and n % 2 == 0:
                        last_routing(n // 2, i * PAIRS + j)
                    elif others and j % 2:
                        trig_tables_by_token(j // 2)

            def last_routing(f, after):
                if after == 4:
                    route_copies(B - 1, f)
                elif after == 8:
                    route_columns(B - 1, f, 1)

            def load_back(i, n):
                if isinstance(i, int) and i == 0:
                    for s in range(AT_ONCE):
                        act.wait_ge(e_sent[s], n * ROUNDS * 16)
                else:
                    act.wait_ge(back_done, n // 2 * HALF + i)
                act.dma_start(BACK, by_token[0][:, bass.ds(i * T, T), :]).then_inc(back_in, 16)

            def trig_tables():
                act.wait_ge(arg_done, 1)
                for s, tab in enumerate((sinT, cosT)):
                    for c in range(KD):
                        act.activation(tab[:, c, :], turn[:, s * KD + c, :], ACT.Sin).then_inc(trig_done, 1)

            def trig_tables_by_token(i):
                act.wait_ge(wq_lo, 2)
                for h in range(2):
                    act.wait_ge(trig_t, 2 * i + h + 1)
                    act.activation((cosN, sinN)[i][:, 2 * h:2 * h + 2, :], bank2(GB[2 + h]), ACT.Copy).then_inc(trig_n, 1)

            def experts(n):
                slot_high(n * ROUNDS, 0)
                slot_high(n * ROUNDS, 1)
                if n % 2 == 0:
                    for i in range(ROUNDS):
                        round_(i, n, i < ROUNDS - 1, True)
                else:
                    round_(0, n, True)
                    with act.Fori(1, ROUNDS - 1) as i:
                        round_(i, n, True)
                    if n == 1:
                        trig_tables()
                    round_(ROUNDS - 1, n, False, n == 1)

            experts(0)
            for k in range(KD):
                act.wait_ge(ld_wq[k], 16)
                act.activation(wq_h[:, k, :], wq_raw[k], ACT.Copy).then_inc(wq_hi, 1)
            experts(1)

            def kv_parts(b, tiles):
                for t in tiles:
                    act.wait_ge(b_kv, b * T + t + 1)
                    if after_first(b):
                        act.wait_ge(b_kc, b * 4)
                        act.wait_ge(b_outer, b)
                    act.activation(KS[:, t, :], GB[t % 2][:, 0:D], ACT.Silu).then_inc(b_ks, 1)
                    act.activation(V[:, t, :], GB[t % 2][:, D:2 * D], ACT.Copy).then_inc(b_v, 1)

            def q_part(b):
                for m in range(KD):
                    act.wait_ge(b_q, b * KD + m + 1)
                    if after_first(b):
                        act.wait_ge(b_qc, b * KD)
                        act.wait_ge(b_qs, b * KD)
                    act.activation(SQ[:, m, :], GB[m], ACT.Silu, bias=bq_s[:, m:m + 1]).then_inc(b_sq, 1)

            def u_part(b):
                for m in range(KD):
                    act.wait_ge(b_u, b * KD + m + 1)
                    if after_first(b):
                        act.wait_ge(b_z, b * KD)
                    act.activation(UT[:, m, :], GB[m], ACT.Identity, bias=bu_s[:, m:m + 1]).then_inc(b_ut, 1)

            def affine(b):
                for c in range(KD):
                    act.wait_ge(b_ot, b * KD + c + 1)
                    if after_first(b):
                        act.wait_ge(b_z, b * KD)
                    act.activation(ONA[:, c, :], TB[c], ACT.Identity, scale=lnw_s[:, c:c + 1],
                                   bias=lnb_s[:, c:c + 1]).then_inc(b_ona, 1)

            def b_body(b, parity, has1, has2, routes, ranks):
                if ranks:
                    route_columns(b - 2, 1, parity)
                if has1:
                    kv_parts(b + 1, range(T))
                    q_part(b + 1)
                affine(b)
                if has1:
                    u_part(b + 1)
                if routes:
                    route_copies(b - 1, 1)
                if has2:
                    high_part(b + 2, LN_B, b_u, (b + 2) * KD)

            high_part(0, LN_B, None, 0)
            for s in range(AT_ONCE):
                act.wait_ge(e_sent[s], 2 * ROUNDS * 16)
            kv_parts(0, range(T))
            q_part(0)
            u_part(0)
            high_part(1, LN_B, b_u, KD)
            b_body(0, 0, True, True, False, False)
            b_body(1, 1, True, True, True, False)
            b_body(2, 0, True, True, True, True)
            with act.Fori(1, (B - 4) // 2) as i:
                b_body(i * 2 + 1, 1, True, True, True, True)
                b_body(i * 2 + 2, 0, True, True, True, True)
            b_body(B - 3, 1, True, True, True, True)
            b_body(B - 2, 0, True, False, True, True)
            b_body(B - 1, 1, False, False, True, True)
            route_columns(B - 2, 1, 0)
            experts(2)
            experts(3)

        @block.gpsimd
        def _(pool):
            def inv_std(b, p):
                q = p * B + b
                wait_apart(pool, mv_done, q + 1)
                pool.tensor_scalar(veps[:, :], mv[:, :, 1], EPS, None, ALU.add).then_inc(rs_add, 1)
                pool.wait_ge(rs_add, q + 1)
                pool.tensor_tensor(rstd[:, :], veps[:, :], minus_half[:, :], ALU.pow).then_inc(rs_done, 1)

            def route_inv_std(b, f):
                r = f * B + b
                wait_apart(pool, r_mv, r + 1)
                pool.tensor_scalar(rveps[:, :], rmv[:, :, 1], EPS, None, ALU.add).then_inc(r_add, 1)
                pool.wait_ge(r_add, r + 1)
                pool.tensor_tensor(rrstd[:, :], rveps[:, :], minus_half[:, :], ALU.pow).then_inc(r_rs, 1)

            def scatter(b, f, parity):
                count = f * B + b + 1
                if not isinstance(count, int):
                    count = pool.snap(count)
                pool.wait_ge(r_idx, count)
                pool.wait_ge(r_cols, count)
                for t in range(T):
                    scatter_tile(b, parity, t)

            def scatter_tile(b, parity, t):
                half = b // HALF if isinstance(b, int) else 0
                for k in range(2):
                    j = 2 * t + k
                    pool.indirect_dma_start(out=slots[half], out_offset=bass.IndirectOffsetOnAxis(ap=IDX[parity][:, j:j + 1], axis=0),
                                            in_=XNR[parity][:, t, :], in_offset=None).then_inc(r_scattered[parity], 16)

            def we_low(e, ring):
                pool.wait_ge(we_hi, e + 1)
                cols = bass.ds(e * D, D)
                pool.tensor_tensor(we_l[:, :, cols], we_raw[ring], we_h[:, :, cols].bitcast(F32), ALU.subtract).then_inc(we_lo, 1)

            def a_body(b, parity, routes, routed, has3):
                if routes:
                    route_inv_std(b - 1, 0)
                if routed:
                    scatter(b - 2, 0, parity)
                we_low(b, parity)
                if has3:
                    inv_std(b + 3, LN_A)

            pool.memset(minus_half[:, :], -0.5).then_inc(fills_p, 1)
            pool.memset(ones_f[:, :], 1.0).then_inc(fills_p, 1)
            pool.memset(ones_b[:, :], 1.0).then_inc(fills_p, 1)
            pool.memset(ones_e[:, :], 1.0).then_inc(fills_p, 1)
            pool.memset(PAD[:, :], 0.0).then_inc(fills_p, 1)
            pool.wait_ge(fills_p, 5)
            pool.memset(PAD[:, R_E1:R_E1 + 1], -1.0).then_inc(fills_p, 1)
            pool.memset(PAD[:, R_TO:R_TO + 1], NOWHERE).then_inc(fills_p, 1)
            pool.wait_ge(fills_p, 7)
            inv_std(0, LN_A)
            inv_std(1, LN_A)
            inv_std(2, LN_A)
            for h in range(2):
                pool.dma_start(slots[h][NE * ROOM * P:, :].rearrange("(n p) w -> p n w", p=P),
                               PAD[:, :].unsqueeze(1).to_broadcast([P, NE, ROW])).then_inc(spare, 16)
            a_body(0, 0, False, False, True)
            a_body(1, 1, True, False, True)
            a_body(2, 0, True, True, True)
            with pool.Fori(1, (B - 4) // 2) as i:
                a_body(i * 2 + 1, 1, True, True, True)
                a_body(i * 2 + 2, 0, True, True, True)
            a_body(B - 3, 1, True, True, False)
            a_body(B - 2, 0, True, True, False)
            a_body(B - 1, 1, True, True, False)

            def send(g, s, half):
                wait_apart(pool, e_y, g * AT_ONCE + s + 1)
                pool.indirect_dma_start(out=chosen[half], out_offset=bass.IndirectOffsetOnAxis(ap=DEST[:, s:s + 1], axis=0),
                                        in_=YO[:, s, :], in_offset=None, bounds_check=2 * HALF * L - 1,
                                        oob_is_err=False).then_inc(e_sent[s], 16)

            by_choice = chosen[1].rearrange("(t p k) d -> k p t d", p=P, k=2)

            def add_first(b):
                at = (b - HALF) * T
                pool.dma_start(X[:, b * T:(b + 1) * T, :], by_choice[1][:, at:at + T, :],
                               accum_op=ALU.add).then_inc(added1[b % 2], 16)

            def add_second(b):
                at = (b - HALF) * T
                pool.wait_ge(added1[b % 2], (b // 2 - 1) * 16)
                if b >= HALF + 2:
                    pool.wait_ge(added2[b % 2], 16)
                pool.dma_start(X[:, b * T:(b + 1) * T, :], by_choice[0][:, at:at + T, :],
                               accum_op=ALU.add).then_inc(added2[b % 2], 16)

            def all_sent(n):
                for s in range(AT_ONCE):
                    pool.wait_ge(e_sent[s], 16 * ROUNDS * (n + 1))

            def first_half(f):
                route_inv_std(B - 1, f)
                scatter(B - 2, f, 0)
                for i in range(ROUNDS):
                    for j in range(PAIRS):
                        for v in range(2):
                            send(2 * f * ROUNDS + i, 2 * j + v, 0)
                        after = i * PAIRS + j - 10
                        if after == 0:
                            pool.wait_ge(r_idx, (f + 1) * B)
                            pool.wait_ge(r_cols, (f + 1) * B)
                        if 0 <= after < T:
                            scatter_tile(B - 1, 1, after)

            def second_half(f):
                n = 2 * f + 1
                with pool.Fori(0, ROUNDS - 1) as i:
                    for s in range(AT_ONCE):
                        send(i + n * ROUNDS, s, 1)
                if f == 0:
                    inv_std(0, LN_B)
                for s in range(AT_ONCE):
                    send(n * ROUNDS + ROUNDS - 1, s, 1)

            first_half(0)
            second_half(0)

            def q_parts(b):
                for c in range(KD):
                    pool.wait_ge(b_sq, b * KD + c + 1)
                    if after_first(b):
                        pool.wait_ge(b_o, b * 2)
                    pool.tensor_tensor(QS[:, c, :], SQ[:, c, :], sinT[:, c, :], ALU.mult).then_inc(b_qs, 1)

            def out_inv_std(b):
                wait_apart(pool, b_omv, b + 1)
                pool.tensor_scalar(oveps[:, :], omv[:, :, 1], EPS, None, ALU.add).then_inc(b_oadd, 1)
                pool.wait_ge(b_oadd, b + 1)
                pool.tensor_tensor(orstd[:, :], oveps[:, :], minus_half[:, :], ALU.pow).then_inc(b_ors, 1)

            def b_body(b, parity, has1, has3, has4, routes, routed):
                if routed:
                    scatter(b - 2, 1, parity)
                if routes and has1:
                    route_inv_std(b - 1, 1)
                out_inv_std(b)
                if not has1:
                    route_inv_std(b - 1, 1)
                if has4:
                    add_first(b + 4)
                if has1:
                    q_parts(b + 1)
                if has4:
                    add_second(b + 4)
                if has3:
                    inv_std(b + 3, LN_B)

            inv_std(1, LN_B)
            q_parts(0)
            inv_std(2, LN_B)
            all_sent(1)
            b_body(0, 0, True, True, True, False, False)
            b_body(1, 1, True, True, True, True, False)
            b_body(2, 0, True, True, True, True, True)
            b_body(3, 1, True, True, True, True, True)
            b_body(4, 0, True, True, False, True, True)
            b_body(B - 3, 1, True, False, False, True, True)
            b_body(B - 2, 0, True, False, False, True, True)
            b_body(B - 1, 1, False, False, False, True, True)
            first_half(1)
            second_half(1)
            all_sent(3)

        @block.vector
        def _(dve):
            def moments(b, p, ready=None, count=0):
                q = p * B + b
                if ready is not None:
                    wait_apart(dve, ready, count)
                for t in range(T):
                    last = dve.bn_stats(stats[:, t, :], X[:, bass.ds(b * T + t, 1), :].squeeze(1))
                last.then_inc(st_done, 1)
                wait_apart(dve, st_done, q + 1)
                for t in range(T):
                    last = dve.bn_aggr(mv[:, t, :], stats[:, t, :])
                last.then_inc(mv_done, 1)

            def normalise(b, p):
                q = p * B + b
                dve.wait_ge(rs_done, q + 1)
                if p or after_first(b):
                    dve.wait_ge(t_done, q * KD)
                for t in range(T):
                    last = dve.tensor_scalar(XN[:, t, :], X[:, bass.ds(b * T + t, 1), :].squeeze(1), mv[:, t, 0:1],
                                             rstd[:, t:t + 1], ALU.subtract, ALU.mult)
                last.then_inc(xn_done, 1)

            def low_part(b, p):
                q = p * B + b
                for c in range(KD):
                    dve.wait_ge(hi_done, q * KD + c + 1)
                    dve.tensor_tensor(XL[:, c, :], TB[c], XH[:, c, :].bitcast(F32), ALU.subtract).then_inc(lo_done, 1)

            def scan(b, m):
                dve.wait_ge(a_xg, b * MI + m + 1)
                dve.tensor_tensor_scan(SG[:, m, :], decay[:, :], XG[:, m, :], 0.0, ALU.mult, ALU.add).then_inc(a_scan, 1)

            def channel_out(b, y, m):
                if m == 0 and (not isinstance(b, int) or b >= 2):
                    dve.wait_ge(a_out, (b - 1) * 2)
                dve.wait_ge(a_scan, b * MI + m + 1)
                dve.scalar_tensor_tensor(out=y[:, m, :], in0=XI[:, m, :], scalar=dp_s[:, m:m + 1], in1=SG[:, m, :],
                                         op0=ALU.mult, op1=ALU.add).then_inc(a_y, 1)

            def channels(b, y, between=None):
                scan(b, 0)
                for m in range(1, MI):
                    scan(b, m)
                    channel_out(b, y, m - 1)
                    if m == 2 and between:
                        between()
                channel_out(b, y, MI - 1)

            def a_residual(b):
                for h in range(2):
                    dve.wait_ge(a_out, b * 2 + h + 1)
                    dve.tensor_tensor(two_tiles(b, h), bank2(GB[4 + h]), two_tiles(b, h), ALU.add).then_inc(a_x1, 1)

            def route_moments(b, f):
                r = f * B + b
                wait_apart(dve, (a_x1, b_x3)[f], b * 2 + 2)
                for t in range(T):
                    last = dve.bn_stats(rstats[:, t, :], X[:, bass.ds(b * T + t, 1), :].squeeze(1))
                last.then_inc(r_st, 1)
                wait_apart(dve, r_st, r + 1)
                for t in range(T):
                    last = dve.bn_aggr(rmv[:, t, :], rstats[:, t, :])
                last.then_inc(r_mv, 1)

            def route_normalise(b, f, parity):
                r = f * B + b
                dve.wait_ge(r_rs, r + 1)
                if f or not isinstance(b, int) or b >= 2:
                    dve.wait_ge(r_scattered[parity], (r >> 1) * 2 * T * 16)
                for t in range(T):
                    last = dve.tensor_scalar(XNR[parity][:, t, 0:D], X[:, bass.ds(b * T + t, 1), :].squeeze(1), rmv[:, t, 0:1],
                                             rrstd[:, t:t + 1], ALU.subtract, ALU.mult)
                last.then_inc(r_xn, 1)

            def route_choice(b, f):
                r = f * B + b
                dve.wait_ge(r_logit, r + 1)
                dve.tensor_tensor(LGX[:, :, 0:NE], GB[2][:, 0:T * NE].rearrange("p (t e) -> p t e", t=T),
                                  bg_s.unsqueeze(1).to_broadcast([P, T, NE]), ALU.add).then_inc(r_lg, 1)
                wait_apart(dve, r_lg, r + 1)
                for t in range(T):
                    last = dve.max(M8[:, t, :], LGX[:, t, :])
                last.then_inc(r_m8, 1)
                wait_apart(dve, r_m8, r + 1)
                for t in range(T):
                    last = dve.max_index(MIX[:, t, :], M8[:, t, :], LGX[:, t, :])
                last.then_inc(r_mi, 1)
                if f or after_first(b):
                    dve.wait_ge(r_cols, r)
                dve.tensor_tensor(GAP[:, :], M8[:, :, 0], M8[:, :, 1], ALU.subtract).then_inc(r_gap, 1)
                dve.wait_ge(r_mi, r + 1)
                dve.tensor_copy(EI[:], MIX[:, :, 0:2]).then_inc(r_ei, 1)
                dve.wait_ge(r_ei, r + 1)
                dve.tensor_tensor(MASK[:], expert.unsqueeze(1).unsqueeze(1).to_broadcast([P, T, 2, NE]),
                                  EI[:].unsqueeze(3).to_broadcast([P, T, 2, NE]), ALU.is_equal).then_inc(r_mask, 1)
                dve.wait_ge(r_mask, r + 1)
                dve.tensor_tensor(BOTH[:], MASK[:, :, 0, :], MASK[:, :, 1, :], ALU.add).then_inc(r_both, 1)

            def route_slots(b, f, parity):
                r = f * B + b
                dve.wait_ge(r_rank, r + 1)
                if not isinstance(b, int) or b % HALF:
                    dve.wait_ge(r_next, r)
                elif r:
                    dve.wait_ge(pad_idx, r // HALF)
                dve.tensor_tensor(POS[:], GB[3][:, 0:T * NE].rearrange("p (t e) -> p t e", t=T),
                                  NEXT[:, :].unsqueeze(1).to_broadcast([P, T, NE]), ALU.add).then_inc(r_pos, 1)
                dve.wait_ge(r_pos, r + 1)
                dve.tensor_tensor(NEXT[:, :], NEXT[:, :], GB[3][:, T * NE:(T + 1) * NE], ALU.add).then_inc(r_next, 1)
                dve.tensor_tensor(PICK[:], MASK[:], POS[:].unsqueeze(2).to_broadcast([P, T, 2, NE]), ALU.mult).then_inc(r_pick, 1)
                dve.wait_ge(r_pick, r + 1)
                dve.tensor_reduce(SLOT[:], PICK[:], AX.X, ALU.add).then_inc(r_slot, 1)
                dve.wait_ge(r_cols, r + 1)
                dve.tensor_scalar(XNR[parity][:, :, R_W2], XNR[parity][:, :, R_DW], -0.5, 0.5, ALU.mult, ALU.add)
                dve.tensor_copy(XNR[parity][:, :, R_E1], EI[:, :, 0])
                dve.wait_ge(r_slot, r + 1)
                dve.tensor_copy(IDX[parity][:, :], SLOT[:].rearrange("p t k -> p (t k)")).then_inc(r_idx, 1)

            TABLE_STEPS = 11 + AT_ONCE

            def count_slots(n):
                dve.wait_ge(r_next, (n + 1) * HALF)
                dve.tensor_tensor(CNT[:, :], NEXT[:, :], first_slot, ALU.subtract).then_inc(count_step, 1)
                dve.wait_ge(count_step, 2 * n + 1)
                two = CNT[0:1, :].rearrange("p (n v) -> p n v", v=2)
                dve.scalar_tensor_tensor(out=USED_f[:, :], in0=two[:, :, 1], scalar=4096.0, in1=two[:, :, 0],
                                         op0=ALU.mult, op1=ALU.add).then_inc(count_step, 1)
                dve.wait_ge(count_step, 2 * n + 2)
                dve.tensor_copy(NEXT[:, :], first_slot)
                dve.tensor_copy(USED[:, n * NE // 2:(n + 1) * NE // 2], USED_f[:, :]).then_inc(pad_idx, 1)

            def tile_table(n, parts=range(4)):
                steps = [n * TABLE_STEPS]
                first_expert, cmp_, h = (n % 2) * TILES, CMP[n > 0], n % 2
                ec = EC[:, first_expert:first_expert + TILES]
                each = ec[0:1, :].rearrange("p (n v) -> p n v", v=AT_ONCE)

                def step(ins):
                    steps[0] += 1
                    ins.then_inc(tab_step, 1)
                    dve.wait_ge(tab_step, steps[0])

                if 0 in parts:
                    step(dve.tensor_scalar(CNT[:, :], CNT[:, :], float(P - 1), 1.0 / P, ALU.add, ALU.mult))
                    step(dve.tensor_scalar(CNT[:, :], CNT[:, :], 0.5 / P - 0.5, ROUND, ALU.add, ALU.add))
                    step(dve.tensor_scalar(NT[:, :], CNT[:, :], -ROUND, None, ALU.add))
                    step(dve.tensor_tensor_scan(CI[:, :], ones_e[:, :], NT[:, :], 0.0, ALU.mult, ALU.add))
                    step(dve.tensor_tensor(cmp_, tile.unsqueeze(2).to_broadcast([P, TILES, NE]),
                                           CI[:, :].unsqueeze(1).to_broadcast([P, TILES, NE]), ALU.is_ge))
                steps[0] = n * TABLE_STEPS + 5
                if 1 in parts:
                    step(dve.tensor_reduce(ET[:, :], cmp_, AX.X, ALU.add))
                    step(dve.tensor_tensor(cmp_, cmp_, NT[:, :].unsqueeze(1).to_broadcast([P, TILES, NE]), ALU.mult))
                    step(dve.tensor_reduce(SKIP[:, :], cmp_, AX.X, ALU.add))
                steps[0] = n * TABLE_STEPS + 8
                if 2 in parts:
                    step(dve.tensor_tensor(RT[:, :], tile, SKIP[:, :], ALU.subtract))
                    step(dve.scalar_tensor_tensor(out=RT[:, :], in0=ET[:, :], scalar=float(ROOM), in1=RT[:, :],
                                                  op0=ALU.mult, op1=ALU.add))
                    step(dve.tensor_scalar(ec, ET[:, :], float(NE - 1), None, ALU.min))
                    two = RT[0:1, :].rearrange("p (n v) -> p n v", v=2)
                    step(dve.scalar_tensor_tensor(out=RP_f[:, :], in0=two[:, :, 1], scalar=512.0, in1=two[:, :, 0],
                                                  op0=ALU.mult, op1=ALU.add))
                    dve.tensor_copy(RP[:, h * TILES // 2:(h + 1) * TILES // 2], RP_f[:, :])
                    step(dve.scalar_tensor_tensor(out=EP_f[:, :], in0=each[:, :, AT_ONCE - 1], scalar=8.0, in1=each[:, :, AT_ONCE - 2],
                                                  op0=ALU.mult, op1=ALU.add))
                steps[0] = n * TABLE_STEPS + 13
                if 3 in parts:
                    for v in range(AT_ONCE - 3, -1, -1):
                        step(dve.scalar_tensor_tensor(out=EP_f[:, :], in0=EP_f[:, :], scalar=8.0, in1=each[:, :, v],
                                                      op0=ALU.mult, op1=ALU.add))
                    assert steps[0] == (n + 1) * TABLE_STEPS
                    dve.tensor_copy(EP[:, h * ROUNDS:(h + 1) * ROUNDS], EP_f[:, :]).then_inc(tab_done, 1)

            def a_body(b, parity, has1, has2, has3, routes, ranks):
                if routes:
                    route_moments(b - 1, 0)
                if has2:
                    normalise(b + 2, LN_A)
                if ranks:
                    route_slots(b - 2, 0, parity)
                if has1:
                    channels(b + 1, Y[1 - parity], (lambda: route_normalise(b - 1, 0, 1 - parity)) if routes else None)
                if has2:
                    low_part(b + 2, LN_A)
                if has3:
                    moments(b + 3, LN_A)
                if not has1:
                    tile_table(0, (0, 1))
                a_residual(b)
                if not has1:
                    route_normalise(b - 1, 0, 1 - parity)
                    tile_table(0, (2, 3))
                if routes:
                    route_choice(b - 1, 0)

            dve.memset(decay[:, :], DECAY).then_inc(fills_v, 1)
            dve.memset(LGX[:], SENTINEL).then_inc(fills_v, 1)
            dve.wait_ge(fills_v, 2)
            dve.wait_ge(ld_x0, 16)
            moments(0, LN_A)
            normalise(0, LN_A)
            dve.wait_ge(ld_par, 16)
            dve.tensor_tensor(bc_s[:, :], par[:, slice(*PAR["bp"])], par[:, slice(*PAR["cp"])], ALU.mult).then_inc(bc_done, 1)
            dve.wait_ge(win_hi, 1)
            dve.tensor_tensor(win_l[:], win_raw, win_h[:].bitcast(F32), ALU.subtract).then_inc(win_lo, 1)
            low_part(0, LN_A)
            dve.wait_ge(bc_done, 1)
            dve.tensor_reduce(g_s[:, :], bc_s[:, :].rearrange("p (m s) -> p m s", m=MI), AX.X, ALU.add).then_inc(g_done, 1)
            dve.wait_ge(ld_x1, 16)
            moments(1, LN_A)
            normalise(1, LN_A)
            channels(0, Y[0], lambda: low_part(1, LN_A))

            def split_rows(n, high_count, whole_rows, raw):
                dve.wait_ge(rows_hi, high_count)
                dve.tensor_scalar(raw, raw, con[0:2, sel2:sel2 + 1], None, ALU.mult).then_inc(rows_a, 1)
                dve.wait_ge(rows_a, n + 1)
                dve.scalar_tensor_tensor(out=whole_rows, in0=whole_rows.bitcast(F32), scalar=con[0:2, sel2 + 1:sel2 + 2],
                                         in1=raw, op0=ALU.mult, op1=ALU.add).then_inc(rows_done, 1)

            dve.wait_ge(ld_con, 16)
            split_rows(0, 1, rows[:, :], rows_raw)
            dve.tensor_copy(NEXT[:, :], first_slot).then_inc(fills_v, 1)
            dve.wait_ge(ld_x, 16)
            moments(2, LN_A)
            dve.wait_ge(fills_v, 3)
            a_body(0, 0, True, True, True, False, False)
            a_body(1, 1, True, True, True, True, False)
            a_body(2, 0, True, True, True, True, True)
            with dve.Fori(1, (B - 4) // 2) as i:
                a_body(i * 2 + 1, 1, True, True, True, True, True)
                a_body(i * 2 + 2, 0, True, True, True, True, True)
            a_body(B - 3, 1, True, True, False, True, True)
            count_slots(0)
            a_body(B - 2, 0, True, False, False, True, True)
            for h in range(2):
                split_rows(1 + h, 3 + h, be_rows[:, h * NE * D // 2:(h + 1) * NE * D // 2], be_raw[h])
            a_body(B - 1, 1, False, False, False, True, True)
            route_moments(B - 1, 0)
            route_slots(B - 2, 0, 0)

            def trig_argument(k):
                if k:
                    dve.wait_ge(arg_step, k)
                if k < KD:
                    step = dve.tensor_scalar(th[:, k, :], pos, theta_s[:, k:k + 1], None, ALU.mult)
                elif k == 2:
                    step = dve.tensor_scalar(whole[:, 0:KD, :], th, INV_TWO_PI, ROUND, ALU.mult, ALU.add)
                elif k == 3:
                    step = dve.tensor_scalar(turn[:, KD:, :], th, INV_TWO_PI, 0.25, ALU.mult, ALU.add)
                elif k == 4:
                    step = dve.tensor_scalar(whole[:, KD:, :], turn[:, KD:, :], ROUND, None, ALU.add)
                elif k == 5:
                    step = dve.tensor_scalar(whole, whole, -ROUND, None, ALU.add)
                elif k < 12:
                    s, i = divmod(k - 6, 3)
                    mine = slice(s * KD, (s + 1) * KD)
                    step = dve.scalar_tensor_tensor(out=turn[:, mine, :], in0=whole[:, mine, :],
                                                    scalar=-(TWO_PI_1, TWO_PI_2, TWO_PI_3)[i],
                                                    in1=turn[:, mine, :] if i else th, op0=ALU.mult, op1=ALU.add)
                elif k == 12:
                    step = dve.tensor_scalar(turn[:, KD:, :], turn[:, KD:, :], float(np.pi / 2), None, ALU.add)
                else:
                    step = dve.tensor_scalar(turn, turn, PI_BELOW, -PI_BELOW, ALU.min, ALU.max)
                step.then_inc(arg_done if k == 13 else arg_step, 1)

            def slot_gates(g, i, j, first_tile):
                two = slice(2 * j, 2 * j + 2)
                q = g * PAIRS + j
                dve.wait_ge(e_beside, q + 1)
                if after_first(g):
                    dve.wait_ge(e_y, (g - 1) * AT_ONCE + 2 * j + 2)
                    for v in range(2):
                        dve.wait_ge(e_sent[2 * j + v], g * 16)
                dve.tensor_tensor(IND[:, two], BESIDE[:, two, B_E1], EC[:, bass.ds(first_tile + i * AT_ONCE + 2 * j, 2)], ALU.is_equal).then_inc(e_ind, 1)
                dve.wait_ge(e_ind, q + 1)
                dve.tensor_tensor(DEST[:, two], BESIDE[:, two, B_TO], IND[:, two], ALU.subtract)
                dve.tensor_tensor(GW[:, two], BESIDE[:, two, B_DW], IND[:, two], ALU.mult).then_inc(e_gate1, 1)
                dve.wait_ge(e_gate1, q + 1)
                dve.tensor_tensor(GW[:, two], GW[:, two], BESIDE[:, two, B_W2], ALU.add).then_inc(e_gate, 1)

            def slot_low(g, j):
                for v in range(2):
                    dve.wait_ge(e_row[2 * j + v], g * 16 + 16)
                dve.tensor_copy(BESIDE[:, 2 * j:2 * j + 2, :], XR[:, 2 * j:2 * j + 2, D:]).then_inc(e_beside, 1)
                dve.wait_ge(e_hi, g * PAIRS + j + 1)
                dve.tensor_tensor(EXL[j], ET4[j], EXH[j].bitcast(F32), ALU.subtract).then_inc(e_lo, 1)

            def add_back(rows_, b, choice, one, done, before):
                if choice:
                    dve.wait_ge(one, before + 1)
                here = X[:, bass.ds(b * T, T), :]
                dve.tensor_tensor(here, here, rows_[:, :, (1 - choice) * D:(2 - choice) * D],
                                  ALU.add).then_inc(done if choice else one, 1)

            def round_(i, n, more, others=None, back=False):
                g, first_tile = n * ROUNDS + i, (n % 2) * TILES
                for j in range(PAIRS):
                    if j + 2 < PAIRS:
                        slot_low(g, j + 2)
                    elif more:
                        slot_low(g + 1, j + 2 - PAIRS)
                    if j + 1 < PAIRS:
                        slot_gates(g, i, j + 1, first_tile)
                    elif more:
                        slot_gates(g + 1, i + 1, 0, first_tile)
                    if back and j in (1, 2):
                        added = n // 2 * HALF + i - 1
                        if j == 1:
                            dve.wait_ge(back_in, added * 16 + 16)
                        add_back(BACK, i - 1, j - 1, back_one, back_done, added)
                    if others:
                        others(n // 2, i * PAIRS + j)

            def last_routing(f, after):
                if after == 0:
                    route_normalise(B - 1, f, 1)
                elif after == 8:
                    route_choice(B - 1, f)
                elif after == 10:
                    route_slots(B - 1, f, 1)
                    count_slots(2 * f + 1)
                elif 11 <= after < 15:
                    tile_table(2 * f + 1, (after - 11,))
                elif f == 0 and (after < 7 or after >= 15):
                    trig_argument(after - 1 if after < 7 else after - 9)

            def preparations(f, after):
                if after < 3:
                    trig_argument(11 + after)
                elif after in (10, 12):
                    k = (after - 10) // 2
                    dve.wait_ge(wq_hi, k + 1)
                    dve.tensor_tensor(wq_l[:, k, :], wq_raw[k], wq_h[:, k, :].bitcast(F32), ALU.subtract).then_inc(wq_lo, 1)
                elif after == 13:
                    moments(0, LN_B, back_done, 1)

            def experts(n):
                slot_low(n * ROUNDS, 0)
                slot_gates(n * ROUNDS, 0, 0, (n % 2) * TILES)
                slot_low(n * ROUNDS, 1)
                if n < 3:
                    for i in range(ROUNDS):
                        round_(i, n, i < ROUNDS - 1, preparations if n == 1 else last_routing, n == 1 and i > 0)
                else:
                    round_(0, n, True)
                    with dve.Fori(1, ROUNDS - 1) as i:
                        round_(i, n, True, None, True)
                    round_(ROUNDS - 1, n, False, None, True)

            experts(0)
            experts(1)

            def k_parts(b, h):
                dve.wait_ge(b_ks, b * T + 2 * h + 2)
                if after_first(b):
                    dve.wait_ge(b_outer, b)
                for part_, tab in ((KC, cosN), (KSN, sinN)):
                    dve.tensor_tensor(part_[:, 2 * h:2 * h + 2, :], KS[:, 2 * h:2 * h + 2, :], tab[:, 2 * h:2 * h + 2, :],
                                      ALU.mult).then_inc(b_kc, 1)

            def q_parts(b):
                for c in range(KD):
                    dve.wait_ge(b_sq, b * KD + c + 1)
                    if after_first(b):
                        dve.wait_ge(b_o, b * 2)
                    dve.tensor_tensor(QC[:, c, :], SQ[:, c, :], cosT[:, c, :], ALU.mult).then_inc(b_qc, 1)

            def masked_sums(b):
                dve.wait_ge(b_outer, b + 1)
                if after_first(b):
                    dve.wait_ge(b_o, b * 2)
                dve.tensor_tensor(KVM, GB[5].rearrange("p (g n) -> p g n", g=2 * KD),
                                  head_mask.unsqueeze(1).to_broadcast([P, 2 * KD, P]), ALU.mult).then_inc(b_kvm, 1)

            def out_moments(b):
                for t in range(T):
                    if t % 2 == 0:
                        dve.wait_ge(b_o, b * 2 + t // 2 + 1)
                    last = dve.bn_stats(ostats[:, t, :], GB[4 + t // 2][:, (t % 2) * D:(t % 2 + 1) * D])
                last.then_inc(b_ost, 1)
                wait_apart(dve, b_ost, b + 1)
                for t in range(T):
                    last = dve.bn_aggr(omv[:, t, :], ostats[:, t, :])
                last.then_inc(b_omv, 1)

            def out_normalise(b):
                dve.wait_ge(b_ors, b + 1)
                if after_first(b):
                    dve.wait_ge(b_ot, b * KD)
                for t in range(T):
                    last = dve.tensor_scalar(ON[:, t, :], GB[4 + t // 2][:, (t % 2) * D:(t % 2 + 1) * D], omv[:, t, 0:1],
                                             orstd[:, t:t + 1], ALU.subtract, ALU.mult)
                last.then_inc(b_on, 1)

            def gated(b):
                for c in range(KD):
                    dve.wait_ge(b_ona, b * KD + c + 1)
                    dve.wait_ge(b_ut, b * KD + c + 1)
                    if c == 0 and after_first(b):
                        dve.wait_ge(b_out, b * 2)
                    dve.tensor_tensor(ZT[:, c, :], UT[:, c, :], ONA[:, c, :], ALU.mult).then_inc(b_z, 1)

            def b_residual(b):
                for h in range(2):
                    dve.wait_ge(b_out, b * 2 + h + 1)
                    dve.tensor_tensor(two_tiles(b, h), bank2(GB[4 + h]), two_tiles(b, h), ALU.add).then_inc(b_x3, 1)

            def b_body(b, parity, has1, has2, has3, routes, ranks):
                if ranks:
                    route_slots(b - 2, 1, parity)
                if has2:
                    normalise(b + 2, LN_B)
                if routes:
                    route_moments(b - 1, 1)
                if not has1:
                    tile_table(2, (0,))
                masked_sums(b)
                if has1:
                    k_parts(b + 1, 0)
                else:
                    tile_table(2, (1,))
                out_moments(b)
                if not has1:
                    tile_table(2, (2,))
                if routes and has1:
                    route_normalise(b - 1, 1, 1 - parity)
                out_normalise(b)
                if not has1:
                    route_normalise(b - 1, 1, 1 - parity)
                if has1:
                    k_parts(b + 1, 1)
                    q_parts(b + 1)
                gated(b)
                if not has1:
                    tile_table(2, (3,))
                if has3:
                    if isinstance(b, int) and b + 3 < HALF:
                        moments(b + 3, LN_B, back_done, b + 4)
                    else:
                        moments(b + 3, LN_B, added2[1 - parity], (((b + 3) >> 1) - 1) * 16)
                if has2:
                    low_part(b + 2, LN_B)
                if routes:
                    route_choice(b - 1, 1)
                b_residual(b)

            normalise(0, LN_B)
            moments(1, LN_B, back_done, 2)
            low_part(0, LN_B)
            normalise(1, LN_B)
            dve.wait_ge(trig_n, 4)
            k_parts(0, 0)
            k_parts(0, 1)
            q_parts(0)
            low_part(1, LN_B)
            moments(2, LN_B, back_done, 3)
            b_body(0, 0, True, True, True, False, False)
            b_body(1, 1, True, True, True, True, False)
            b_body(2, 0, True, True, True, True, True)
            with dve.Fori(1, (B - 4) // 2) as i:
                b_body(i * 2 + 1, 1, True, True, True, True, True)
                b_body(i * 2 + 2, 0, True, True, True, True, True)
            b_body(B - 3, 1, True, True, False, True, True)
            count_slots(2)
            b_body(B - 2, 0, True, False, False, True, True)
            b_body(B - 1, 1, False, False, False, True, True)
            route_moments(B - 1, 1)
            route_slots(B - 2, 1, 0)
            experts(2)
            experts(3)
            for k in range(HALF):
                dve.wait_ge(last_in[k], 16)
                for choice in range(2):
                    add_back(LAST[k], HALF + k, choice, last_one, last_done, k)


def kernel(**inputs):
    import concourse.bacc as bacc
    from concourse.bass_utils import run_bass_kernel_spmd

    a = {n.split("L0_")[1]: np.asarray(v) for n, v in inputs.items()}

    def cols(v):
        return v.reshape(-1, P).T

    def rows(v):
        return np.broadcast_to(v.reshape(1, -1), (P, v.size))

    def chunks(m):
        return m.reshape(-1, P, m.shape[1]).transpose(1, 0, 2).reshape(P, -1)

    bqkvu = a["attn_b_bqkvu"]
    params = {
        "bin": cols(a["attn_a_bin_"]), "dp": cols(a["attn_a_Dp"]), "bp": chunks(a["attn_a_Bp"]),
        "cp": chunks(a["attn_a_Cp"].T), "bq": cols(bqkvu[0:D]), "bu": cols(bqkvu[3 * D:]),
        "theta": cols(a["attn_b_theta"].reshape(-1)), "lnw": cols(a["attn_b_ln_w"]), "lnb": cols(a["attn_b_ln_b"]),
        "bg": rows(a["ffn_bg"]), "wg": chunks(a["ffn_Wg"]),
    }
    arrays = {
        "x": a["attn_a_x"],
        "consts": shape_constants(),
        "params": np.concatenate([params[n] for n in PAR], axis=1),
        "win": a["attn_a_Win"],
        "wout": a["attn_a_Wout"],
        "wqkvu": a["attn_b_Wqkvu"].T,
        "wo": a["attn_b_Wout"].T,
        "we": a["ffn_We"].transpose(2, 0, 1).reshape(D, NE * D),
        "be2": np.stack([a["ffn_be"].reshape(-1)] * 2),
        "rows2": np.stack([np.concatenate([bqkvu[D:3 * D], a["attn_a_bout"], a["attn_b_bout"]])] * 2),
    }
    arrays = {n: np.ascontiguousarray(v) for n, v in arrays.items()}
    nc = bacc.Bacc("TRN2", target_bir_lowering=False, num_devices=1)
    args = [nc.dram_tensor(n, v.shape, mybir.dt.from_np(v.dtype), kind="ExternalInput").ap() for n, v in arrays.items()]
    out = nc.dram_tensor("out", (B, L, D), F32, kind="ExternalOutput").ap()
    slots = [nc.dram_tensor(f"slots{h}", ((NE * ROOM + NE) * P, ROW), F32, kind="Internal").ap() for h in range(2)]
    chosen = [nc.dram_tensor(f"chosen{h}", (2 * HALF * L, D), F32, kind="Internal").ap() for h in range(2)]
    build(nc, *args, slots, chosen, out)
    r = run_bass_kernel_spmd(nc, [arrays], core_ids=[0])
    return r.results[0]["out"]
```
